# Optimizing a Trainium2 kernel written in Bass

```python
import numpy as np
import jax
import jax.numpy as jnp

def _softmax(x, axis=-1):
    return jax.nn.softmax(x, axis=axis)

def _gelu(x):
    return jax.nn.gelu(x, approximate=True)

def _silu(x):
    return jax.nn.silu(x)

def _sigmoid(x):
    return jax.nn.sigmoid(x)

def _layernorm(x, axis=-1, eps=1e-05):
    m = jnp.mean(x, axis=axis, keepdims=True)
    v = jnp.var(x, axis=axis, keepdims=True)
    return (x - m) / jnp.sqrt(v + eps)

def _scatter_add(tgt, idx, src, axis=0):
    return tgt.at[idx].add(src)

def _segment_sum(src, seg, n):
    return jax.ops.segment_sum(src, seg, n)
kernel_name = 'mk_vit_tower_cls_d1_tok_img512_r4_8c1fb7'

def setup_inputs(seed: int=0):
    np.random.seed(seed)
    _w = jnp.asarray

    def _rec_inputs():
        import jax
        import jax.numpy as jnp
        _rk = jax.random.key(seed)
        x = -0.000392918 + 0.999932 * jax.random.normal(jax.random.fold_in(_rk, 1), (32, 1, 128, 128), jnp.float32)
        cls_tok = 0.02 * jax.random.normal(jax.random.fold_in(_rk, 5), (1, 1, 128), jnp.float32)
        return (x, cls_tok)
    x, cls_tok = _rec_inputs()

    def _L0_tok_setup():
        import math
        import jax, jax.numpy as jnp
        import numpy as np
        PW = PH = 16
        EMB = 128
        HID = 128
        B, H, W = (64, 128, 128)
        L = H // PW * (W // PH)
        SIGMA_ZERO = 0.1

        def _f_noise(x):
            return jnp.sign(x) * jnp.sqrt(jnp.abs(x))

        def _noisy_linear(x, w, b, sw, sb, eps_in, eps_out):
            ei = _f_noise(eps_in)
            eo = _f_noise(eps_out)
            w_n = w + sw * (eo[:, None] * ei[None, :])
            b_n = b + sb * eo
            return x @ w_n.T + b_n

        def _unfold_patches(x):
            b = x.shape[0]
            p = x.reshape(b, H // PW, PW, W // PH, PH)
            p = p.transpose(0, 1, 3, 2, 4)
            return p.reshape(b, L, PW * PH)

        def _pos_encoding(x):
            pos = jnp.arange(L, dtype=jnp.float32)[:, None]
            div = jnp.exp(jnp.arange(0, EMB, 2, dtype=jnp.float32) * (-math.log(10000.0) / EMB))
            ang = pos * div
            pe = jnp.stack([jnp.sin(ang), jnp.cos(ang)], axis=-1).reshape(L, EMB)
            return x + pe[None, :, :]
        key = jax.random.key(seed)
        ks = jax.random.split(key, 12)
        in_f = PW * PH
        sig = SIGMA_ZERO / math.sqrt(in_f)
        bnd1 = 1.0 / math.sqrt(in_f)
        bnd3 = 1.0 / math.sqrt(HID)
        u = lambda k, shape, bnd: jax.random.uniform(k, shape, jnp.float32, -bnd, bnd)
        return {'inputs': jax.random.normal(ks[0], (B, 1, H, W), jnp.float32), 'W1_w': u(ks[1], (HID, in_f), bnd1), 'W1_b': u(ks[2], (HID,), bnd1), 'W1_sw': jnp.full((HID, in_f), sig, jnp.float32), 'W1_sb': jnp.full((HID,), sig, jnp.float32), 'W2_w': u(ks[3], (HID, in_f), bnd1), 'W2_b': u(ks[4], (HID,), bnd1), 'W2_sw': jnp.full((HID, in_f), sig, jnp.float32), 'W2_sb': jnp.full((HID,), sig, jnp.float32), 'W3_w': u(ks[5], (EMB, HID), bnd3), 'W3_b': u(ks[6], (EMB,), bnd3), 'eps_in1': jax.random.normal(ks[7], (in_f,), jnp.float32), 'eps_out1': jax.random.normal(ks[8], (HID,), jnp.float32), 'eps_in2': jax.random.normal(ks[9], (in_f,), jnp.float32), 'eps_out2': jax.random.normal(ks[10], (HID,), jnp.float32)}
    _L0_tok_all = _L0_tok_setup()
    _L0_tok_in = {k: v for k, v in _L0_tok_all.items() if k in ('W1_w', 'W1_b', 'W1_sw', 'W1_sb', 'W2_w', 'W2_b', 'W2_sw', 'W2_sb', 'W3_w', 'W3_b', 'eps_in1', 'eps_out1', 'eps_in2', 'eps_out2')}
    del _L0_tok_all

    def _L0_attn_setup():
        import jax, jax.numpy as jnp
        import numpy as np
        import math
        B, T, C = (8, 256, 128)
        H = 8
        HD = C // H
        MAX_REL = 64 + 4

        def _rel_index(t):
            r = jnp.arange(t)
            dist = jnp.clip(r[None, :] - r[:, None], -MAX_REL, MAX_REL)
            return dist + MAX_REL
        key = jax.random.key(seed)
        ks = jax.random.split(key, 12)
        xavier = lambda k, shape: jax.random.uniform(k, shape, jnp.float32, -1.0, 1.0) * math.sqrt(6.0 / (shape[0] + shape[1]))
        return {'x': jax.random.normal(ks[0], (B, T, C), jnp.float32), 'Wq': xavier(ks[1], (C, C)), 'bq': jnp.zeros((C,), jnp.float32), 'Wk': xavier(ks[2], (C, C)), 'bk': jnp.zeros((C,), jnp.float32), 'Wv': xavier(ks[3], (C, C)), 'bv': jnp.zeros((C,), jnp.float32), 'Wo': xavier(ks[4], (C, C)), 'bo': jnp.zeros((C,), jnp.float32), 'rel_k': xavier(ks[5], (2 * MAX_REL + 1, HD)), 'rel_v': xavier(ks[6], (2 * MAX_REL + 1, HD))}
    _L0_attn_all = _L0_attn_setup()
    _L0_attn_in = {k: v for k, v in _L0_attn_all.items() if k in ('Wq', 'bq', 'Wk', 'bk', 'Wv', 'bv', 'Wo', 'bo', 'rel_k', 'rel_v')}
    del _L0_attn_all

    def _L0_ffn_setup():
        import jax, jax.numpy as jnp
        import numpy as np
        B, S, D, H, E = (4, 512, 128, 256, 8)
        key = jax.random.key(seed)
        ks = jax.random.split(key, 4)
        x = jax.random.normal(ks[0], (B, S, D), jnp.float32)
        Wr = jax.random.normal(ks[1], (E, D), jnp.float32) * 0.02
        br = jnp.zeros((E,), jnp.float32)
        W1 = jax.random.normal(ks[2], (E, D, H), jnp.float32) * 0.02
        b1 = jnp.zeros((E, H), jnp.float32)
        W2 = jax.random.normal(ks[3], (E, H, D), jnp.float32) * 0.02
        b2 = jnp.zeros((E, D), jnp.float32)
        return {'x': x, 'Wr': Wr, 'br': br, 'W1': W1, 'b1': b1, 'W2': W2, 'b2': b2}
    _L0_ffn_all = _L0_ffn_setup()
    _L0_ffn_in = {k: v for k, v in _L0_ffn_all.items() if k in ('Wr', 'br', 'W1', 'b1', 'W2', 'b2')}
    del _L0_ffn_all
    return {'x': x, 'cls_tok': cls_tok, 'L0_tok_W1_w': _L0_tok_in['W1_w'], 'L0_tok_W1_b': _L0_tok_in['W1_b'], 'L0_tok_W1_sw': _L0_tok_in['W1_sw'], 'L0_tok_W1_sb': _L0_tok_in['W1_sb'], 'L0_tok_W2_w': _L0_tok_in['W2_w'], 'L0_tok_W2_b': _L0_tok_in['W2_b'], 'L0_tok_W2_sw': _L0_tok_in['W2_sw'], 'L0_tok_W2_sb': _L0_tok_in['W2_sb'], 'L0_tok_W3_w': _L0_tok_in['W3_w'], 'L0_tok_W3_b': _L0_tok_in['W3_b'], 'L0_tok_eps_in1': _L0_tok_in['eps_in1'], 'L0_tok_eps_out1': _L0_tok_in['eps_out1'], 'L0_tok_eps_in2': _L0_tok_in['eps_in2'], 'L0_tok_eps_out2': _L0_tok_in['eps_out2'], 'L0_attn_Wq': _L0_attn_in['Wq'], 'L0_attn_bq': _L0_attn_in['bq'], 'L0_attn_Wk': _L0_attn_in['Wk'], 'L0_attn_bk': _L0_attn_in['bk'], 'L0_attn_Wv': _L0_attn_in['Wv'], 'L0_attn_bv': _L0_attn_in['bv'], 'L0_attn_Wo': _L0_attn_in['Wo'], 'L0_attn_bo': _L0_attn_in['bo'], 'L0_attn_rel_k': _L0_attn_in['rel_k'], 'L0_attn_rel_v': _L0_attn_in['rel_v'], 'L0_ffn_Wr': _L0_ffn_in['Wr'], 'L0_ffn_br': _L0_ffn_in['br'], 'L0_ffn_W1': _L0_ffn_in['W1'], 'L0_ffn_b1': _L0_ffn_in['b1'], 'L0_ffn_W2': _L0_ffn_in['W2'], 'L0_ffn_b2': _L0_ffn_in['b2']}

def reference(x, cls_tok, L0_tok_W1_w, L0_tok_W1_b, L0_tok_W1_sw, L0_tok_W1_sb, L0_tok_W2_w, L0_tok_W2_b, L0_tok_W2_sw, L0_tok_W2_sb, L0_tok_W3_w, L0_tok_W3_b, L0_tok_eps_in1, L0_tok_eps_out1, L0_tok_eps_in2, L0_tok_eps_out2, L0_attn_Wq, L0_attn_bq, L0_attn_Wk, L0_attn_bk, L0_attn_Wv, L0_attn_bv, L0_attn_Wo, L0_attn_bo, L0_attn_rel_k, L0_attn_rel_v, L0_ffn_Wr, L0_ffn_br, L0_ffn_W1, L0_ffn_b1, L0_ffn_W2, L0_ffn_b2):
    import jax
    import jax.numpy as jnp

    def _L0_tok_ref(inputs, W1_w, W1_b, W1_sw, W1_sb, W2_w, W2_b, W2_sw, W2_sb, W3_w, W3_b, eps_in1, eps_out1, eps_in2, eps_out2):
        import math
        import jax, jax.numpy as jnp
        import numpy as np
        PW = PH = 16
        EMB = 128
        HID = 128
        B, H, W = (64, 128, 128)
        L = H // PW * (W // PH)
        SIGMA_ZERO = 0.1

        def _f_noise(x):
            return jnp.sign(x) * jnp.sqrt(jnp.abs(x))

        def _noisy_linear(x, w, b, sw, sb, eps_in, eps_out):
            ei = _f_noise(eps_in)
            eo = _f_noise(eps_out)
            w_n = w + sw * (eo[:, None] * ei[None, :])
            b_n = b + sb * eo
            return x @ w_n.T + b_n

        def _unfold_patches(x):
            b = x.shape[0]
            p = x.reshape(b, H // PW, PW, W // PH, PH)
            p = p.transpose(0, 1, 3, 2, 4)
            return p.reshape(b, L, PW * PH)

        def _pos_encoding(x):
            pos = jnp.arange(L, dtype=jnp.float32)[:, None]
            div = jnp.exp(jnp.arange(0, EMB, 2, dtype=jnp.float32) * (-math.log(10000.0) / EMB))
            ang = pos * div
            pe = jnp.stack([jnp.sin(ang), jnp.cos(ang)], axis=-1).reshape(L, EMB)
            return x + pe[None, :, :]
        x = _unfold_patches(inputs)
        g = _noisy_linear(x, W1_w, W1_b, W1_sw, W1_sb, eps_in1, eps_out1)
        x_gate = g * jnp.tanh(jax.nn.softplus(g))
        x_inner = _noisy_linear(x, W2_w, W2_b, W2_sw, W2_sb, eps_in2, eps_out2)
        x = x_gate * x_inner
        x = x @ W3_w.T + W3_b
        return _pos_encoding(x)

    def _L0_attn_ref(x, Wq, bq, Wk, bk, Wv, bv, Wo, bo, rel_k, rel_v):
        import jax, jax.numpy as jnp
        import numpy as np
        import math
        B, T, C = (8, 256, 128)
        H = 8
        HD = C // H
        MAX_REL = 64 + 4

        def _rel_index(t):
            r = jnp.arange(t)
            dist = jnp.clip(r[None, :] - r[:, None], -MAX_REL, MAX_REL)
            return dist + MAX_REL
        b, t, c = x.shape
        h, hd = (H, HD)
        q = x @ Wq + bq
        k = x @ Wk + bk
        v = x @ Wv + bv
        rq = q.reshape(b, t, h, hd).transpose(0, 2, 1, 3)
        rk = k.reshape(b, t, h, hd).transpose(0, 2, 1, 3)
        rv = v.reshape(b, t, h, hd).transpose(0, 2, 1, 3)
        idx = _rel_index(t)
        rk2 = rel_k[idx]
        rv2 = rel_v[idx]
        attn1 = jnp.einsum('bhqd,bhkd->bhqk', rq, rk)
        attn2 = jnp.einsum('bhqd,qkd->bhqk', rq, rk2)
        attn = jax.nn.softmax((attn1 + attn2) * (1.0 / math.sqrt(c)), axis=-1)
        w1 = jnp.einsum('bhqk,bhkd->bhqd', attn, rv)
        w2 = jnp.einsum('bhqk,qkd->bhqd', attn, rv2)
        out = (w1 + w2).transpose(0, 2, 1, 3).reshape(b, t, c)
        return out @ Wo + bo

    def _L0_ffn_ref(x, Wr, br, W1, b1, W2, b2):
        import jax, jax.numpy as jnp
        import numpy as np
        B, S, D, H, E = (4, 512, 128, 256, 8)
        b, s, d = x.shape
        n = b * s
        e = Wr.shape[0]
        xf = x.reshape(n, d)
        logits = xf @ Wr.T + br
        probs = jax.nn.softmax(logits, axis=-1)
        top2_prob, top2_idx = jax.lax.top_k(probs, 2)
        comb = jnp.zeros((n, e), x.dtype).at[jnp.arange(n)[:, None], top2_idx].add(top2_prob)
        h = jax.nn.gelu(jnp.einsum('nd,edh->enh', xf, W1) + b1[:, None, :], approximate=False)
        o = jnp.einsum('enh,ehd->end', h, W2) + b2[:, None, :]
        y = jnp.einsum('ne,end->nd', comb, o)
        return y.reshape(b, s, d)
    h = _L0_tok_ref(x, L0_tok_W1_w, L0_tok_W1_b, L0_tok_W1_sw, L0_tok_W1_sb, L0_tok_W2_w, L0_tok_W2_b, L0_tok_W2_sw, L0_tok_W2_sb, L0_tok_W3_w, L0_tok_W3_b, L0_tok_eps_in1, L0_tok_eps_out1, L0_tok_eps_in2, L0_tok_eps_out2)
    h = jnp.concatenate([jnp.broadcast_to(cls_tok, (h.shape[0], 1, h.shape[2])), h], axis=1)
    h = h + _L0_attn_ref(_layernorm(h, axis=-1), L0_attn_Wq, L0_attn_bq, L0_attn_Wk, L0_attn_bk, L0_attn_Wv, L0_attn_bv, L0_attn_Wo, L0_attn_bo, L0_attn_rel_k, L0_attn_rel_v)
    h = h + _L0_ffn_ref(_layernorm(h, axis=-1), L0_ffn_Wr, L0_ffn_br, L0_ffn_W1, L0_ffn_b1, L0_ffn_W2, L0_ffn_b2)
    return h

_drawn_inputs = setup_inputs


def setup_inputs(seed=0):
    import zlib

    import numpy as np

    out = dict(_drawn_inputs(seed))
    spreads = {'L0_tok_W1_sw': (0.0062500000931322575, 0.6),
     'L0_tok_W1_sb': (0.0062500000931322575, 0.6),
     'L0_tok_W2_sw': (0.0062500000931322575, 0.6),
     'L0_tok_W2_sb': (0.0062500000931322575, 0.6),
     'L0_attn_bq': (0.0, 0.8),
     'L0_attn_bk': (0.0, 0.8),
     'L0_attn_bv': (0.0, 0.1),
     'L0_attn_bo': (0.0, 0.1),
     'L0_ffn_br': (0.0, 0.389),
     'L0_ffn_b1': (0.0, 0.8),
     'L0_ffn_b2': (0.0, 0.321)}
    factors = {'L0_tok_W1_b': 6.873,
     'L0_tok_W2_b': 6.422,
     'L0_tok_eps_in1': 2.981,
     'L0_tok_eps_out1': 2.844,
     'L0_tok_eps_in2': 2.784,
     'L0_attn_rel_k': 8.0,
     'L0_attn_rel_v': 3.676,
     'L0_ffn_W1': 5.746,
     'L0_ffn_W2': 5.37}
    for name, (base, spread) in spreads.items():
        noise = np.random.default_rng([zlib.crc32(name.encode()), seed]).standard_normal(out[name].shape)
        drawn = base * np.exp(spread * noise) if base else spread * noise
        out[name] = jnp.asarray(drawn.astype(out[name].dtype))
    for name, factor in factors.items():
        out[name] = (out[name] * factor).astype(out[name].dtype)
    return out
```

```python
from contextlib import ExitStack

import numpy as np

import concourse.bass as bass
from concourse import mybir

ALU = mybir.AluOpType
ACT = mybir.ActivationFunctionType
AX_X = mybir.AxisListType.X
F32 = mybir.dt.float32

P = 128
IMG = 32
NPATCH = 64
PAIRS = IMG // 2
TOK = IMG * NPATCH
C = 128
PIX = 256
H, HD = 8, 16
PJ = H // 2
QC = NPATCH + 1
E = 8
FH = 256
BLK = 512
NBLK = TOK // BLK
TPB = BLK // P
MAX_REL = 68
SCALE = 1.0 / float(np.sqrt(C))
EPS = 1e-5
ALL = TOK + IMG
NT = PAIRS + 1
FB = ALL // 5

K_ID, K_PE, K_E8, K_VM, K_E8T = 0, 128, 256, 384, 512
K_PM, K_HP, K_KP, K_PR, K_PRIO = 640, 644, 646, 648, 664
K_ALL = 672

V_B1, V_SB1, V_EO1, V_B2, V_SB2, V_EO2, V_BQ, V_BK, V_BV, V_FB1 = 0, 1, 2, 3, 4, 5, 6, 7, 8, 9
NVEC = V_FB1 + E * FH // P

M_W3, M_WR, M_RK, M_RV, M_XC = 0, 128, 136, 265, 330
M_ALL = 331


def constants():
    p = np.arange(P)[:, None]
    c = np.arange(P)[None, :]
    k = np.zeros((P, K_ALL), np.float32)
    k[:, K_ID:K_ID + P] = p == c
    pos = np.arange(NPATCH, dtype=np.float32)[:, None]
    div = np.exp(np.arange(0, C, 2, dtype=np.float32) * np.float32(-np.log(10000.0) / C))
    ang = pos * div
    pe = np.stack([np.sin(ang), np.cos(ang)], axis=-1).reshape(NPATCH, C)
    k[:, K_PE:K_PE + C] = np.concatenate([pe, pe], axis=0)
    k[:, K_E8:K_E8 + P] = p // HD == c % H
    k[:, K_VM:K_VM + P] = p % 2 == (c // HD) % 2
    k[:, K_E8T:K_E8T + P] = p % H == c // HD
    k[:, K_PM:K_PM + PJ] = p // 32 == np.arange(PJ)
    k[:, K_HP:K_HP + 2] = (p // HD) % 2 == np.arange(2)
    k[:, K_KP:K_KP + 2] = p % 2 == np.arange(2)
    k[:, K_PR:K_PR + PAIRS] = p // H == np.arange(PAIRS)
    k[:, K_PRIO:K_PRIO + E] = E - np.arange(E)[None, :]
    return k


def vit_kernel(nc, consts, x, cls_tok, W1_w, W1_b, W1_sw, W1_sb, W2_w, W2_b, W2_sw, W2_sb, W3_w, W3_b,
               eps_in1, eps_out1, eps_in2, eps_out2, Wq, bq, Wk, bk, Wv, bv, Wo, bo, rel_k, rel_v,
               Wr, br, fW1, fb1, fW2, fb2, out):
    with ExitStack() as ctx:
        def sb(name, cols, parts=P):
            return ctx.enter_context(nc.sbuf_tensor(name, [parts, cols], F32))

        def sem(name):
            return ctx.enter_context(nc.semaphore(name))

        bank = [ctx.enter_context(nc.psum_tensor(f"bank{i}", [P, 512], F32)) for i in range(8)]

        kc = sb("kc", K_ALL)
        ident = kc[:, K_ID:K_ID + P]
        region_a = sb("region_a", 8192)
        xraw = region_a[:, 0:4096].rearrange("p (s n) -> p s n", s=2)
        xperm = region_a[:, 4096:8192]
        A2 = region_a[:, :].rearrange("p (j b q) -> p j b q", j=PJ, b=IMG)
        w1_sb = region_a[:, 0:E * FH].rearrange("p (e h) -> p e h", e=E)
        w2_sb = region_a[:, E * FH:E * FH + E * 2 * C].rearrange("p (e s d) -> p e s d", e=E, s=2)
        region_b = sb("region_b", 4096)
        xT = region_b[:, :].rearrange("p (r t) -> p r t", r=2)
        KM = region_b[:, :].rearrange("p (t s) -> p t s", s=2)
        region_c = sb("region_c", PJ * IMG * QC)
        PT = region_c[:, :].rearrange("p (j b q) -> p j b q", j=PJ, b=IMG)
        xnTd = region_c[:, 0:2 * TOK].rearrange("p (t s) -> p t s", s=2)
        gate = region_c[:, 2 * TOK:3 * TOK]
        sp = region_c[:, 3 * TOK:4 * TOK]
        region_d = sb("region_d", 2 * 2 * ALL)
        QP = region_d[:, 0:PJ * TOK].rearrange("p (j b q) -> p j b q", j=PJ, b=IMG)
        QPf = region_d[:, 0:PJ * TOK].rearrange("p (j t) -> p j t", j=PJ)
        HB = region_d[:, :].rearrange("p (u s t) -> p u s t", u=2, s=2)
        pc_rep = region_d[:, 0:TOK].rearrange("p (r h d) -> p r h d", r=PAIRS, h=H)
        wprep = region_d[:, 0:1024].rearrange("p (w i) -> p w i", w=4)
        ei = region_d[:, 1024:1536]
        ei_root = region_d[:, 1536:2048]
        ei_sign = region_d[:, 2048:2560]
        wn = region_d[:, 2560:3072].rearrange("p (w i) -> p w i", w=2)
        rvd = region_d[:, 3072:3072 + QC * HD].rearrange("p (q d) -> p q d", q=QC)
        QT = sb("QT", ALL)
        xn2T = QT
        KT = sb("KT", NT * P)
        acc = KT[:, :].rearrange("p (t c) -> p t c", t=NT)
        region_e = sb("region_e", TOK)
        xi = region_e
        tc_ = region_e
        SP = [region_e[:, 520 * i:520 * i + 520] for i in range(3)]
        h0 = sb("h0", TOK)
        xnT = sb("xnT", TOK)
        OT = xnT
        OTc = sb("OTc", IMG)
        vbd = sb("vbd", IMG * C)
        VBD = vbd[:, :].rearrange("p (b c) -> p b c", b=IMG)
        RVBD = sb("RVBD", QC * 32)
        RV = RVBD[:, :].rearrange("p (q s d) -> p q s d", q=QC, s=2)
        stb = sb("stb", 1024)
        ST = [stb[:, 0:512], stb[:, 512:1024]]
        tmpx = sb("tmpx", 512)
        misc = sb("misc", M_ALL)
        W3T = misc[:, M_W3:M_W3 + C]
        WrT = misc[:, M_WR:M_WR + E]
        relkT = misc[:, M_RK:M_RK + 129]
        relvT = misc[:, M_RV:M_RV + 65]
        xcT = misc[:, M_XC:M_XC + 1]
        relk_bd = sb("relk_bd", 258)
        RKB = relk_bd[:, :].rearrange("p (r s) -> p r s", s=2)
        wnT = sb("wnT", 512)
        WnT = wnT[:, :].rearrange("p (w r o) -> p w r o", w=2, r=2)
        w3 = sb("w3", C)
        wqkvo = sb("wqkvo", 4 * C)
        wq, wk, wv, wo = (wqkvo[:, i * C:(i + 1) * C] for i in range(4))
        rows = sb("rows", P)
        vecs = sb("vecs", NVEC)
        rel_rows = sb("rel_rows", 3 * C)
        wr = sb("wr", C)
        posb = sb("posb", C)
        bob = sb("bob", C)
        brb = sb("brb", E)
        b2s = sb("b2s", C)
        clsr = sb("clsr", C)
        clsn = sb("clsn", C)
        eo = sb("eo", 8)
        nb = sb("nb", 4)
        stats = sb("stats", NT * 6)
        mv = sb("mv", NT * 2)
        ve = sb("ve", NT)
        rstd = sb("rstd", NT)
        mhalf = sb("mhalf", 4)
        clsv = sb("clsv", 8)
        kcq = sb("kcq", NPATCH)
        vcq = sb("vcq", NPATCH)
        Sc = sb("Sc", PAIRS * H)
        Sct = sb("Sct", PAIRS * H)
        cx = sb("cx", 2 * QC)
        p0d = sb("p0d", 4 * NPATCH)
        sml = sb("sml", 16)
        p0x = sb("p0x", IMG)
        ptt = sb("ptt", NPATCH)
        mxr = sb("mxr", 6 * H)
        PcA = sb("PcA", PAIRS * H)
        lg = sb("lg", NT * E)
        rt = sb("rt", 4 * NT * E)
        rs_ = sb("rs_", 2 * NT)
        comb = sb("comb", NT * E)
        combT = vbd

        names = """d_const d_rows d_w1 d_w2 d_x0 d_x1 d_small d_rel d_rvd d_attn d_ffn d_out
        vec_ps vecs_ok eo_act ei_act feo_ok wn_ok wnT_ps wnT_ok cls_n misc_ps misc_ok nb_ok
        xperm_ok xT_ps xT_evA xT_evD g_ps gate_ok tmin_ok tanh_ok m_ok in_ps xi_ok y_ps h0_ok ve_ok rstd_ok
        xn_ok xnT_ps xnT_ok xnTd_ok q_ps k_ps v_ps QT_ok KT_ok QP_ok KM_ok VBD_ok cls_ps clsv_ok
        a2_ps a2_evA a2_evD kcq_ok tc_ok ua_ok uc_ok tcT_ps tc_red c0_ps cx_ok cexp_ok p0d_ok p0T_ps ptc_ok
        pc_m ve_c rstd_c
        s1_ps st_ok s_ps sub_ok d_ok e_ok r_ok pn_ok pc_ok pt_ps pt_ok w1_ps w1_ev
        rep_ok pcT_ps pcx_ok w2_ps o_ok p00_ps oc_ok op_ps opc_ps h1_ok ve2_ok rstd2_ok xn2_ok x2T_ps x2T_ok
        lg_ps lg_ok lexp_ok comb_ok cT_ps cT_ok base_ps acc_ok h_ps gelu_ok y2_ps
        rb_ok h0o_ok relbd_ok
        dve_c act_c pool_c""".split()
        S = {n: sem(n) for n in names}

        def chain(eng, name):
            n = [0]

            def link(ins):
                n[0] += 1
                ins.then_inc(S[name], 1)
                eng.wait_ge(S[name], n[0])
            return link

        block = ctx.enter_context(nc.Block())
        relk8 = rel_k.unsqueeze(1)
        relv8 = rel_v.unsqueeze(1)

        @block.sync
        def _(sp_):
            xv = x.rearrange("(s b) o (i r) w -> s (b o i) (r w)", s=2, i=8)
            for s in range(2):
                for half in range(2):
                    sp_.dma_start(xraw[:, s, half * 1024:(half + 1) * 1024],
                                  xv[s, :, half * 1024:(half + 1) * 1024]).then_inc(S[f"d_x{s}"], 16)
            for i, w in enumerate((Wq, Wk, Wv, Wo)):
                sp_.dma_start(wqkvo[:, i * C:(i + 1) * C], w).then_inc(S["d_attn"], 16)
            for par in range(2):
                src = bass.AP(tensor=rel_v.tensor, offset=rel_v.offset + 5 * HD, ap=[[HD, NPATCH], [1, QC * HD]])
                sp_.dma_start(region_d[par:P:2, 3072:3072 + QC * HD], src).then_inc(S["d_rvd"], 16)
            sp_.wait_ge(S["st_ok"], PAIRS)
            sp_.dma_start(w1_sb, fW1.rearrange("e d h -> d e h")).then_inc(S["d_ffn"], 16)
            sp_.dma_start(w2_sb, fW2.rearrange("e (s h) d -> h e s d", s=2)).then_inc(S["d_ffn"], 16)
            ov = out.rearrange("(r b) t c -> b t r c", b=2)
            for g in range(5):
                sp_.wait_ge(S["acc_ok"], 5 + 5 * (E - 1) + g + 1)
                if g < 4:
                    for b2 in range(2):
                        sp_.dma_start(ov[b2, 1:QC, 4 * g:4 * g + 4, :],
                                      acc[64 * b2:64 * b2 + 64, 4 * g:4 * g + 4, :]).then_inc(S["d_out"], 16)
                else:
                    sp_.dma_start(out[:, 0, :], acc[0:IMG, PAIRS, :]).then_inc(S["d_out"], 16)
            sp_.wait_ge(S["d_out"], 16 * 9)

        @block.gpsimd
        def _(pool):
            g = nc.gpsimd
            link = chain(pool, "pool_c")
            g.dma_start(rel_rows[:, 0:C].rearrange("p (h d) -> p h d", h=H),
                        relk8[4:132].to_broadcast([P, H, HD])).then_inc(S["d_rel"], 16)
            g.dma_start(rel_rows[0:1, C:2 * C].rearrange("p (h d) -> p h d", h=H),
                        relk8[132:133].to_broadcast([1, H, HD])).then_inc(S["d_rel"], 16)
            g.dma_start(rel_rows[0:65, 2 * C:3 * C].rearrange("p (h d) -> p h d", h=H),
                        relv8[4:69].to_broadcast([65, H, HD])).then_inc(S["d_rel"], 16)
            g.dma_start(w3[:, :], W3_w).then_inc(S["d_rel"], 16)
            g.dma_start(wr[0:E, :], Wr).then_inc(S["d_rel"], 16)
            g.dma_start(posb[:, :], W3_b.unsqueeze(0).to_broadcast([P, C])).then_inc(S["d_small"], 16)
            g.dma_start(bob[:, :], bo.unsqueeze(0).to_broadcast([P, C])).then_inc(S["d_small"], 16)
            g.dma_start(brb[:, :], br.unsqueeze(0).to_broadcast([P, E])).then_inc(S["d_small"], 16)
            g.dma_start(b2s[0:E, :], fb2).then_inc(S["d_small"], 16)
            link(g.memset(mhalf[:, :], -0.5))
            pool.wait_ge(S["ve_c"], 1)
            g.tensor_tensor(clsn[0:1, 2:3], clsn[0:1, 1:2], mhalf[0:1, 0:1], ALU.pow).then_inc(S["rstd_c"], 1)
            for n in range(NBLK):
                pool.wait_ge(S["tanh_ok"], n + 1)
                b = slice(n * BLK, (n + 1) * BLK)
                g.tensor_tensor(gate[:, b], gate[:, b], sp[:, b], ALU.mult).then_inc(S["m_ok"], 1)
            for n in range(NBLK):
                pool.wait_ge(S["ve_ok"], n + 1)
                g.tensor_tensor(rstd[:, n * TPB:(n + 1) * TPB], ve[:, n * TPB:(n + 1) * TPB], mhalf[:, :],
                                ALU.pow).then_inc(S["rstd_ok"], 1)
            pool.wait_ge(S["kcq_ok"], 1)
            for n in range(NBLK):
                b = slice(n * BLK, (n + 1) * BLK)
                bb = [P, BLK // NPATCH, NPATCH]
                pool.wait_ge(S["QT_ok"], n + 1)
                g.tensor_tensor(tc_[:, b].rearrange("p (b q) -> p b q", q=NPATCH),
                                QT[:, b].rearrange("p (b q) -> p b q", q=NPATCH),
                                kcq[:, :].unsqueeze(1).to_broadcast(bb), ALU.mult).then_inc(S["tc_ok"], 1)
                pool.wait_ge(S["KM_ok"], n + 1)
                kt = KT[:, b].rearrange("p (b q) -> p b q", q=NPATCH)
                g.tensor_tensor(kt, kt, relkT[:, 65:129].unsqueeze(1).to_broadcast(bb), ALU.add)\
                    .then_inc(S["ua_ok"], 1)
            pool.wait_ge(S["d_small"], 64)
            for n in range(NBLK):
                hv = h0[:, n * BLK:(n + 1) * BLK].rearrange("p (t c) -> p t c", c=C)
                ins = g.tensor_tensor(hv, hv, bob[:, :].unsqueeze(1).to_broadcast([P, TPB, C]), ALU.add)
            ins.then_inc(S["h0o_ok"], 1)
            for p in range(PAIRS):
                pool.wait_ge(S["r_ok"], p + 1)
                e_, r_ = SP[p % 3], mxr[:, 16 + 8 * (p % 2):24 + 8 * (p % 2)]
                g.tensor_tensor(PcA[:, p * H:(p + 1) * H], e_[:, 512:520], r_, ALU.mult).then_inc(S["pc_ok"], 1)
                ev = e_[:, 0:512].rearrange("p (j k s) -> p j k s", j=PJ, s=2)
                rv = r_.rearrange("p (j s) -> p j s", j=PJ).unsqueeze(2).to_broadcast([P, PJ, NPATCH, 2])
                g.tensor_tensor(ev, ev, rv, ALU.mult).then_inc(S["pn_ok"], 1)
            for n in range(5):
                m = P if n < NBLK else IMG
                w = TPB if n < NBLK else 1
                pool.wait_ge(S["ve2_ok"], n + 1)
                g.tensor_tensor(rstd[0:m, n * TPB:n * TPB + w], ve[0:m, n * TPB:n * TPB + w], mhalf[0:m, 0:w],
                                ALU.pow).then_inc(S["rstd2_ok"], 1)

        @block.scalar
        def _(act):
            a = nc.scalar
            link = chain(act, "act_c")
            a.dma_start(kc[:, :], consts).then_inc(S["d_const"], 16)
            for r, v in ((V_B1, W1_b), (V_SB1, W1_sb), (V_EO1, eps_out1), (V_B2, W2_b), (V_SB2, W2_sb),
                         (V_EO2, eps_out2), (V_BQ, bq), (V_BK, bk), (V_BV, bv)):
                a.dma_start(rows[r:r + 1, :], v.unsqueeze(0)).then_inc(S["d_rows"], 16)
            a.dma_start(rows[V_FB1:NVEC, :], fb1.rearrange("e (s h) -> (e s) h", s=2)).then_inc(S["d_rows"], 16)
            for i, v in enumerate((eps_in1, eps_in2)):
                a.dma_start(ei[:, i * PIX:(i + 1) * PIX], v.unsqueeze(0).to_broadcast([P, PIX]))\
                    .then_inc(S["d_w1"], 16)
            for i, w in enumerate((W1_w, W1_sw, W2_w, W2_sw)):
                a.dma_start(wprep[:, i, :], w).then_inc(S["d_w2"], 16)
            a.dma_start(clsr[0:IMG, :], cls_tok.rearrange("a b c -> (a b) c").to_broadcast([IMG, C]))\
                .then_inc(S["d_rows"], 16)
            act.wait_ge(S["d_w1"], 32)
            link(a.activation(ei_root, ei, ACT.Abs))
            a.activation(ei_root, ei_root, ACT.Sqrt).then_inc(S["ei_act"], 1)
            a.activation(ei_sign, ei, ACT.Sign).then_inc(S["ei_act"], 1)
            act.wait_ge(S["vecs_ok"], 1)
            link(a.activation(eo[:, 0:2], vecs[:, V_EO1:V_EO2 + 1:3], ACT.Abs))
            a.activation(eo[:, 2:4], eo[:, 0:2], ACT.Sqrt).then_inc(S["eo_act"], 1)
            a.activation(eo[:, 4:6], vecs[:, V_EO1:V_EO2 + 1:3], ACT.Sign).then_inc(S["eo_act"], 1)
            act.wait_ge(S["misc_ps"], 1)
            a.activation(misc[:, :], bank[2][:, 128:128 + M_ALL], ACT.Copy).then_inc(S["misc_ok"], 1)

            def evac_xT(t):
                act.wait_ge(S["xT_ps"], t + 1)
                s, r, jh = t // 4, (t // 2) % 2, t % 2
                dst = xT[:, r, s * 1024:(s + 1) * 1024].rearrange("p (m g j) -> p g m j", g=2, j=4)[:, jh]
                a.activation(dst, bank[t % 2][:, :].rearrange("p (j m) -> p m j", j=4), ACT.Copy)\
                    .then_inc(S["xT_evA"], 1)

            def softplus(n):
                b = slice(n * BLK, (n + 1) * BLK)
                act.wait_ge(S["g_ps"], n + 1)
                if n == 0:
                    act.wait_ge(S["nb_ok"], 1)
                a.activation(gate[:, b], bank[4 + n % 2][:, :], ACT.Identity, bias=nb[:, 0:1])\
                    .then_inc(S["gate_ok"], 1)
                act.wait_ge(S["tmin_ok"], n + 1)
                link(a.activation(sp[:, b], sp[:, b], ACT.Exp))
                link(a.activation(sp[:, b], sp[:, b], ACT.Ln, bias=1.0))

            for s in range(2):
                evac_xT(4 * s)
                evac_xT(4 * s + 2)
                softplus(2 * s)
                softplus(2 * s + 1)
            for n in range(NBLK):
                b = slice(n * BLK, (n + 1) * BLK)
                a.activation(sp[:, b], sp[:, b], ACT.Tanh).then_inc(S["tanh_ok"], 1)

            def evac_xn(n):
                b = slice(n * BLK, (n + 1) * BLK)
                act.wait_ge(S["xnT_ps"], n + 1)
                a.activation(xnT[:, b], bank[2 + n % 2][:, :], ACT.Copy).then_inc(S["xnT_ok"], 1)
                a.activation(xnTd[:, b, :], bank[2 + n % 2][:, :].unsqueeze(2).to_broadcast([P, BLK, 2]),
                             ACT.Copy).then_inc(S["xnTd_ok"], 1)

            def evac_qk(n):
                b = slice(n * BLK, (n + 1) * BLK)
                act.wait_ge(S["q_ps"], n + 1)
                a.activation(QT[:, b], bank[4][:, :], ACT.Identity, bias=vecs[:, V_BQ:V_BQ + 1])\
                    .then_inc(S["QT_ok"], 1)
                act.wait_ge(S["k_ps"], n + 1)
                a.activation(KT[:, b], bank[5][:, :], ACT.Identity, bias=vecs[:, V_BK:V_BK + 1])\
                    .then_inc(S["KT_ok"], 1)

            evac_xn(0)
            evac_xn(1)
            evac_qk(0)
            evac_xn(2)
            evac_qk(1)
            evac_xn(3)
            evac_qk(2)
            evac_qk(3)
            act.wait_ge(S["clsv_ok"], 1)
            for i in range(8):
                act.wait_ge(S["a2_ps"], 2 * i + 1)
                a.activation(A2[:, :, :, 8 * i:8 * i + 4].rearrange("p j b q -> p (j b) q"),
                             bank[(2 * i) % 4][:, :].rearrange("p (q m) -> p m q", q=4), ACT.Copy)\
                    .then_inc(S["a2_evA"], 1)
                if i % 2 == 1:
                    n = i // 2
                    b = slice(n * BLK, (n + 1) * BLK)
                    act.wait_ge(S["ua_ok"], n + 1)
                    a.activation(KT[:, b], KT[:, b], ACT.Copy, scale=clsv[:, 0:1]).then_inc(S["uc_ok"], 1)
            act.wait_ge(S["cx_ok"], 1)
            a.activation(cx[:, :], cx[:, :], ACT.Exp, scale=SCALE).then_inc(S["cexp_ok"], 1)

            for i in range(PAIRS + 5):
                if 1 <= i <= PAIRS:
                    p = i - 1
                    act.wait_ge(S["d_ok"], p + 1)
                    a.activation(SP[p % 3][:, :], SP[p % 3][:, :], ACT.Exp, scale=SCALE).then_inc(S["e_ok"], 1)
                p = i - 3
                if 0 <= p < PAIRS:
                    act.wait_ge(S["pt_ps"], p + 1)
                    a.activation(PT[:, :, 2 * p:2 * p + 2, 0:NPATCH],
                                 bank[4 + p % 2][:, :].rearrange("p (j b q) -> p j b q", j=PJ, b=2), ACT.Copy)\
                        .then_inc(S["pt_ok"], 1)
                p = i - 5
                if 0 <= p < PAIRS and p % 2 == 1:
                    u = p // 2
                    act.wait_ge(S["w1_ps"], u + 1)
                    o = bank[6 + u % 2][:, 0:4 * QC].rearrange("p (b q) -> p b q", b=4)
                    a.activation(OT[:, 256 * u:256 * u + 256].rearrange("p (b q) -> p b q", b=4),
                                 o[:, :, 0:NPATCH], ACT.Copy)
                    a.activation(OTc[:, 4 * u:4 * u + 4], o[:, :, NPATCH], ACT.Copy).then_inc(S["w1_ev"], 1)
            for n in range(5):
                m = BLK if n < NBLK else IMG
                act.wait_ge(S["x2T_ps"], n + 1)
                a.activation(xn2T[:, n * BLK:n * BLK + m], bank[n][:, 0:m], ACT.Copy).then_inc(S["x2T_ok"], 1)

            def gelu(i):
                e, s, blk = i // 10, (i // 5) % 2, i % 5
                act.wait_ge(S["h_ps"], i + 1)
                if e >= 2 and i % 10 == 0:
                    act.wait_ge(S["y2_ps"], 5 * (e - 1))
                v = V_FB1 + 2 * e + s
                a.activation(HB[:, e % 2, s, blk * FB:(blk + 1) * FB], bank[i % 4][:, 0:FB], ACT.Gelu,
                             bias=vecs[:, v:v + 1]).then_inc(S["gelu_ok"], 1)

            act.wait_ge(S["lg_ok"], 1)
            a.activation(lg[:, :], lg[:, :], ACT.Exp).then_inc(S["lexp_ok"], 1)
            for i in range(10):
                gelu(i)
            for n in range(5):
                m = BLK if n < NBLK else IMG
                act.wait_ge(S["cT_ps"], n + 1)
                a.activation(combT[0:E, n * BLK:n * BLK + m], bank[4 + n % 4][0:E, 0:m], ACT.Copy)\
                    .then_inc(S["cT_ok"], 1)
            for i in range(10, 10 * E):
                gelu(i)

        @block.vector
        def _(dve):
            v = nc.vector
            link = chain(dve, "dve_c")
            pred = nc.vector
            dve.wait_ge(S["d_rows"], 16 * 11)
            link(v.bn_stats(stats[0:1, 0:6], clsr[0:1, :]))
            link(v.bn_aggr(mv[0:1, 0:2], stats[0:1, 0:6]))
            v.tensor_scalar(clsn[0:1, 1:2], mv[0:1, 1:2], EPS, None, ALU.add).then_inc(S["ve_c"], 1)
            dve.wait_ge(S["vec_ps"], 1)
            v.tensor_copy(vecs[:, :], bank[2][:, 0:NVEC]).then_inc(S["vecs_ok"], 1)
            dve.wait_ge(S["rstd_c"], 1)
            link(v.tensor_copy(sml[0:1, 0:1], clsn[0:1, 2:3]))
            v.tensor_scalar(clsn[0:1, :], clsr[0:1, :], mv[0:1, 0:1], sml[0:1, 0:1], ALU.subtract, ALU.mult)\
                .then_inc(S["cls_n"], 1)
            dve.wait_ge(S["ei_act"], 2)
            link(v.tensor_tensor(ei, ei_root, ei_sign, ALU.mult))
            dve.wait_ge(S["eo_act"], 2)
            link(v.tensor_tensor(eo[:, 6:8], eo[:, 2:4], eo[:, 4:6], ALU.mult))
            dve.wait_ge(S["d_w2"], 64)
            for w in range(2):
                link(v.scalar_tensor_tensor(wn[:, w, :], wprep[:, 2 * w + 1, :], eo[:, 6 + w:7 + w],
                                            ei[:, w * PIX:(w + 1) * PIX], op0=ALU.mult, op1=ALU.mult))
                v.tensor_tensor(wn[:, w, :], wn[:, w, :], wprep[:, 2 * w, :], ALU.add).then_inc(S["wn_ok"], 1)
            link(v.tensor_tensor(nb[:, 2:4], vecs[:, V_SB1:V_SB2 + 1:3], eo[:, 6:8], ALU.mult))
            v.tensor_tensor(nb[:, 0:2], nb[:, 2:4], vecs[:, V_B1:V_B2 + 1:3], ALU.add).then_inc(S["nb_ok"], 1)

            def permute(s, half):
                dve.wait_ge(S[f"d_x{s}"], 32)
                o = (2 * s + half) * 1024
                v.tensor_copy(xperm[:, o:o + 1024].rearrange("p (j r c) -> p r j c", j=8, r=8),
                              xraw[:, s, half * 1024:(half + 1) * 1024].rearrange("p (r j c) -> p r j c", r=8, j=8))\
                    .then_inc(S["xperm_ok"], 1)

            def evac_xT(t):
                dve.wait_ge(S["xT_ps"], t + 1)
                s, r, jh = t // 4, (t // 2) % 2, t % 2
                dst = xT[:, r, s * 1024:(s + 1) * 1024].rearrange("p (m g j) -> p g m j", g=2, j=4)[:, jh]
                v.tensor_copy(dst, bank[t % 2][:, :].rearrange("p (j m) -> p m j", j=4)).then_inc(S["xT_evD"], 1)

            def clamp(n):
                b = slice(n * BLK, (n + 1) * BLK)
                dve.wait_ge(S["gate_ok"], n + 1)
                v.tensor_scalar(sp[:, b], gate[:, b], 30.0, None, ALU.min).then_inc(S["tmin_ok"], 1)

            permute(0, 0)
            permute(0, 1)
            dve.wait_ge(S["wnT_ps"], 1)
            v.tensor_copy(wnT[:, :], bank[3][:, :]).then_inc(S["wnT_ok"], 1)
            evac_xT(1)
            evac_xT(3)
            permute(1, 0)
            permute(1, 1)
            clamp(0)
            clamp(1)
            evac_xT(5)
            evac_xT(7)
            dve.wait_ge(S["misc_ok"], 1)
            for s in range(2):
                v.tensor_scalar(RKB[:, :, s], relkT, kc[:, K_HP + s:K_HP + s + 1], None, ALU.mult)
            clamp(2)
            dve.wait_ge(S["d_rvd"], 32)
            for s in range(2):
                v.tensor_scalar(RV[:, :, s, :], rvd, kc[:, K_KP + s:K_KP + s + 1], None, ALU.mult)
            dve.wait_ge(S["d_small"], 64)
            link(v.tensor_tensor(posb[:, :], posb[:, :], kc[:, K_PE:K_PE + C], ALU.add))
            clamp(3)

            def inner(n):
                b = slice(n * BLK, (n + 1) * BLK)
                dve.wait_ge(S["in_ps"], n + 1)
                dve.wait_ge(S["m_ok"], n + 1)
                v.scalar_tensor_tensor(xi[:, b], bank[6 + n % 2][:, :], nb[:, 1:2], gate[:, b], op0=ALU.add,
                                       op1=ALU.mult).then_inc(S["xi_ok"], 1)

            def embed(n):
                b = slice(n * BLK, (n + 1) * BLK)
                dve.wait_ge(S["y_ps"], n + 1)
                v.tensor_tensor(h0[:, b].rearrange("p (t c) -> p t c", c=C),
                                bank[n % 2][:, :].rearrange("p (t c) -> p t c", c=C),
                                posb[:, :].unsqueeze(1).to_broadcast([P, TPB, C]), ALU.add)\
                    .then_inc(S["h0_ok"], 1)
                dve.wait_ge(S["h0_ok"], n + 1)
                moments(h0, n, TPB, P, "ve_ok")

            def moments(src, n, w, m, done):
                for t in range(n * TPB, n * TPB + w):
                    last = v.bn_stats(stats[0:m, 6 * t:6 * t + 6], src[0:m, t * C:(t + 1) * C])
                link(last)
                for t in range(n * TPB, n * TPB + w):
                    last = v.bn_aggr(mv[0:m, 2 * t:2 * t + 2], stats[0:m, 6 * t:6 * t + 6])
                link(last)
                v.tensor_scalar(ve[0:m, n * TPB:n * TPB + w],
                                mv[0:m, 2 * n * TPB:2 * (n * TPB + w)].rearrange("p (t s) -> p t s", s=2)[:, :, 1],
                                EPS, None, ALU.add).then_inc(S[done], 1)

            def normalise(src, n, w, m, wait, done, read, count):
                dve.wait_ge(S[wait], n + 1)
                if count > 0:
                    dve.wait_ge(S[read], count)
                for i in range(w):
                    t = n * TPB + i
                    last = v.tensor_scalar(ST[n % 2][0:m, i * C:(i + 1) * C], src[0:m, t * C:(t + 1) * C],
                                           mv[0:m, 2 * t:2 * t + 1], rstd[0:m, t:t + 1], ALU.subtract, ALU.mult)
                last.then_inc(S[done], 1)

            def qkv(n):
                b = slice(n * BLK, (n + 1) * BLK)
                for half in range(2):
                    u = 2 * n + half
                    dve.wait_ge(S["v_ps"], u + 1)
                    v.tensor_tensor(VBD[:, 4 * u:4 * u + 4, :], bank[6 + half][:, :].rearrange("p (b c) -> p b c", b=4),
                                    kc[:, K_VM:K_VM + C].unsqueeze(1).to_broadcast([P, 4, C]), ALU.mult)\
                        .then_inc(S["VBD_ok"], 1)
                dve.wait_ge(S["QT_ok"], n + 1)
                for j in range(PJ):
                    last = v.tensor_scalar(QPf[:, j, b], QT[:, b], kc[:, K_PM + j:K_PM + j + 1], None, ALU.mult)
                last.then_inc(S["QP_ok"], 1)
                dve.wait_ge(S["KT_ok"], n + 1)
                for s in range(2):
                    last = v.tensor_scalar(KM[:, b, s], KT[:, b], kc[:, K_HP + s:K_HP + s + 1], None, ALU.mult)
                last.then_inc(S["KM_ok"], 1)

            def norm1(n):
                normalise(h0, n, TPB, P, "rstd_ok", "xn_ok", "xnT_ps", n - 1)

            inner(0)
            inner(1)
            embed(0)
            inner(2)
            embed(1)
            norm1(0)
            inner(3)
            embed(2)
            norm1(1)
            embed(3)
            norm1(2)
            qkv(0)
            norm1(3)
            qkv(1)
            qkv(2)
            qkv(3)
            dve.wait_ge(S["cls_ps"], 1)
            link(v.tensor_tensor(clsv[:, 0:2], bank[4][:, 0:2], vecs[:, V_BQ:V_BK + 1], ALU.add))
            link(v.tensor_copy(clsv[:, 2:3], bank[4][:, 2:3]))
            link(v.tensor_tensor(clsv[:, 3:4], clsv[:, 1:2], relkT[:, 64:65], ALU.add))
            link(v.tensor_tensor(clsv[:, 4:5], clsv[:, 3:4], clsv[:, 0:1], ALU.mult))
            v.tensor_tensor(clsv[:, 5:6], clsv[:, 2:3], relvT[:, 64:65], ALU.add).then_inc(S["clsv_ok"], 1)
            v.tensor_scalar(kcq[:, :], misc[:, M_RK + 63:M_RK - 1:-1], clsv[:, 1:2], None, ALU.add)\
                .then_inc(S["kcq_ok"], 1)
            v.tensor_scalar(vcq[:, :], misc[:, M_RV + 63:M_RV - 1:-1], clsv[:, 2:3], None, ALU.add)

            def red(g):
                dve.wait_ge(S["tcT_ps"], g + 1)
                dst = (Sc if g < 4 else Sct)[:, (g % 4) * 32:(g % 4) * 32 + 32]
                v.tensor_reduce(dst, bank[4 + g % 4][:, :].rearrange("p (m d) -> p m d", d=HD), axis=AX_X,
                                op=ALU.add).then_inc(S["tc_red"], 1)

            for i in range(8):
                dve.wait_ge(S["a2_ps"], 2 * i + 2)
                v.tensor_copy(A2[:, :, :, 8 * i + 4:8 * i + 8].rearrange("p j b q -> p (j b) q"),
                              bank[(2 * i + 1) % 4][:, :].rearrange("p (q m) -> p m q", q=4))\
                    .then_inc(S["a2_evD"], 1)
                if i >= 4:
                    red(i - 4)
            for g in range(4, 8):
                red(g)

            def add(p):
                dve.wait_ge(S["s1_ps"], p + 1)
                if p >= 2:
                    dve.wait_ge(S["s_ps"], p - 1)
                v.tensor_tensor(ST[p % 2].rearrange("p (j m) -> p j m", j=PJ),
                                bank[p % 2][:, :].rearrange("p (j m) -> p j m", j=PJ),
                                A2[:, :, 2 * p:2 * p + 2, :].rearrange("p j b q -> p j (b q)"), ALU.add)\
                    .then_inc(S["st_ok"], 1)

            def maxsub(p):
                dve.wait_ge(S["s_ps"], p + 1)
                m_ = mxr[:, 8 * (p % 2):8 * (p % 2) + 8]
                sc = Sc[:, p * H:(p + 1) * H]
                sv = bank[2 + p % 2][:, :].rearrange("p (j k s) -> p j s k", j=PJ, s=2)
                link(v.tensor_reduce(m_.rearrange("p (j s) -> p j s", j=PJ), sv, axis=AX_X, op=ALU.max))
                link(v.tensor_tensor(m_, m_, sc, ALU.max))
                if p >= 3:
                    dve.wait_ge(S["pt_ps"], p - 2)
                    dve.wait_ge(S["pc_ok"], p - 2)
                d = SP[p % 3]
                v.tensor_tensor(d[:, 0:512].rearrange("p (j k s) -> p j k s", j=PJ, s=2),
                                bank[2 + p % 2][:, :].rearrange("p (j k s) -> p j k s", j=PJ, s=2),
                                m_.rearrange("p (j s) -> p j s", j=PJ).unsqueeze(2).to_broadcast([P, PJ, NPATCH, 2]),
                                ALU.subtract).then_inc(S["sub_ok"], 1)
                v.tensor_tensor(d[:, 512:520], sc, m_, ALU.subtract).then_inc(S["d_ok"], 1)

            def total(p):
                dve.wait_ge(S["e_ok"], p + 1)
                s_ = mxr[:, 32 + 8 * (p % 2):40 + 8 * (p % 2)]
                link(v.tensor_reduce(s_.rearrange("p (j s) -> p j s", j=PJ),
                                     SP[p % 3][:, 0:512].rearrange("p (j k s) -> p j s k", j=PJ, s=2),
                                     axis=AX_X, op=ALU.add))
                link(v.tensor_tensor(s_, s_, SP[p % 3][:, 512:520], ALU.add))
                if p >= 2:
                    dve.wait_ge(S["pn_ok"], p - 1)
                v.reciprocal(mxr[:, 16 + 8 * (p % 2):24 + 8 * (p % 2)], s_).then_inc(S["r_ok"], 1)

            def class_query():
                cv = cx[:, :].rearrange("p (b k) -> p b k", b=2)
                m2, c00, r2 = sml[:, 2:4], sml[:, 4:5], sml[:, 6:8]
                dve.wait_ge(S["c0_ps"], 1)
                cps = bank[4][:, 0:P].rearrange("p (b k) -> p b k", b=2)
                v.tensor_copy(c00, bank[4][:, P:P + 1])
                link(v.tensor_reduce(m2, cps, axis=AX_X, op=ALU.max))
                link(v.tensor_scalar(m2, m2, c00, None, ALU.max))
                v.tensor_tensor(cv[:, :, 0:NPATCH], cps, m2.unsqueeze(2).to_broadcast([P, 2, NPATCH]), ALU.subtract)
                v.tensor_scalar(cv[:, :, NPATCH], m2, -1.0, c00, ALU.mult, ALU.add).then_inc(S["cx_ok"], 1)
                dve.wait_ge(S["cexp_ok"], 1)
                link(v.tensor_reduce(r2, cv, axis=AX_X, op=ALU.add))
                link(v.reciprocal(sml[:, 8:10], r2))
                v.tensor_tensor(p0d[:, :].rearrange("p (b k s) -> p b k s", b=2, s=2),
                                cv[:, :, 0:NPATCH].unsqueeze(3).to_broadcast([P, 2, NPATCH, 2]),
                                sml[:, 8:10].unsqueeze(2).unsqueeze(3).to_broadcast([P, 2, NPATCH, 2]), ALU.mult)
                link(v.tensor_tensor(sml[:, 10:12], cv[:, :, NPATCH], sml[:, 8:10], ALU.mult))
                v.tensor_tensor(p0x[:, :].rearrange("p (r b) -> p r b", b=2),
                                kc[:, K_PR:K_PR + PAIRS].unsqueeze(2).to_broadcast([P, PAIRS, 2]),
                                sml[:, 10:12].unsqueeze(1).to_broadcast([P, PAIRS, 2]), ALU.mult)\
                    .then_inc(S["p0d_ok"], 1)
                dve.wait_ge(S["p0T_ps"], 1)
                for b2 in range(2):
                    pv = bank[5][:, b2 * P:(b2 + 1) * P].rearrange("p (r j s) -> p r j s", r=PAIRS, j=PJ)
                    tv = ptt[:, :].rearrange("p (r j) -> p r j", j=PJ)
                    link(v.tensor_scalar(tv, pv[:, :, :, 1], kc[:, K_KP + 1:K_KP + 2], None, ALU.mult))
                    last = v.scalar_tensor_tensor(PT[:, :, b2:IMG:2, NPATCH].rearrange("p j r -> p r j"),
                                                  pv[:, :, :, 0], kc[:, K_KP:K_KP + 1], tv, op0=ALU.mult,
                                                  op1=ALU.add)
                    if b2 == 0:
                        link(last)
                last.then_inc(S["ptc_ok"], 1)

            for i in range(PAIRS + 2):
                if i < PAIRS:
                    add(i)
                if 1 <= i <= PAIRS:
                    maxsub(i - 1)
                if i >= 2:
                    total(i - 2)
                if i == 0:
                    class_query()

            dve.wait_ge(S["pc_ok"], PAIRS)
            for n in range(NBLK):
                last = v.tensor_copy(pc_rep[:, 4 * n:4 * n + 4, :, :].rearrange("p r h d -> p (r h) d"),
                                     PcA[:, 32 * n:32 * n + 32].unsqueeze(2).to_broadcast([P, 32, HD]))
                last.then_inc(S["rep_ok"], 1)
            dve.wait_ge(S["w1_ev"], 8)
            for n in range(NBLK):
                b = slice(n * BLK, (n + 1) * BLK)
                dve.wait_ge(S["pcT_ps"], n + 1)
                if n:
                    dve.wait_ge(S["pc_m"], n)
                v.tensor_tensor(tmpx[:, :].rearrange("p (b q) -> p b q", q=NPATCH),
                                bank[5 + n % 3][:, :].rearrange("p (b q) -> p b q", q=NPATCH),
                                vcq[:, :].unsqueeze(1).to_broadcast([P, 8, NPATCH]), ALU.mult)\
                    .then_inc(S["pcx_ok"], 1)
                dve.wait_ge(S["pcx_ok"], n + 1)
                v.tensor_tensor(OT[:, b], OT[:, b], tmpx[:, :], ALU.add).then_inc(S["pc_m"], 1)
            dve.wait_ge(S["pc_m"], NBLK)
            ov = OT[:, :].rearrange("p (b q) -> p b q", q=NPATCH)
            for n in range(4):
                dve.wait_ge(S["w2_ps"], n + 1)
                o = ov[:, :, 16 * n:16 * n + 16]
                v.scalar_tensor_tensor(o, bank[n][:, :].rearrange("p (q b) -> p b q", q=16),
                                       vecs[:, V_BV:V_BV + 1], o, op0=ALU.add, op1=ALU.add).then_inc(S["o_ok"], 1)
            dve.wait_ge(S["w2_ps"], 5)
            link(v.scalar_tensor_tensor(OTc[:, :], bank[4][:, 0:IMG], vecs[:, V_BV:V_BV + 1], OTc[:, :],
                                        op0=ALU.add, op1=ALU.add))
            v.scalar_tensor_tensor(OTc[:, :], bank[4][:, IMG:2 * IMG], clsv[:, 5:6], OTc[:, :], op0=ALU.mult,
                                   op1=ALU.add).then_inc(S["oc_ok"], 1)
            link(v.tensor_tensor(clsr[0:IMG, :], clsr[0:IMG, :], bob[0:IMG, :], ALU.add))
            dve.wait_ge(S["h0o_ok"], 1)
            link(v.memset(lg[:, PAIRS * E:NT * E], 0.0))

            def residual(n):
                if n < NBLK:
                    dve.wait_ge(S["op_ps"], n + 1)
                    b = slice(n * BLK, (n + 1) * BLK)
                    v.tensor_tensor(KT[:, b], bank[5 + n % 3][:, :], h0[:, b], ALU.add).then_inc(S["h1_ok"], 1)
                    dve.wait_ge(S["h1_ok"], n + 1)
                    moments(KT, n, TPB, P, "ve2_ok")
                else:
                    dve.wait_ge(S["opc_ps"], 1)
                    v.tensor_tensor(KT[0:IMG, TOK:TOK + C], bank[4][0:IMG, 128:256], clsr[0:IMG, :], ALU.add)\
                        .then_inc(S["h1_ok"], 1)
                    dve.wait_ge(S["h1_ok"], n + 1)
                    moments(KT, n, 1, IMG, "ve2_ok")

            def norm2(n):
                full = n < NBLK
                normalise(KT, n, TPB if full else 1, P if full else IMG, "rstd2_ok", "xn2_ok", "x2T_ps", n - 1)

            residual(0)
            for n in range(1, 5):
                residual(n)
                norm2(n - 1)
            norm2(4)
            lv = lg[:, :].rearrange("p (t e) -> p t e", e=E)
            full = [P, NT, E]
            ra, rb, rc, rd = (rt[:, i * NT * E:(i + 1) * NT * E].rearrange("p (t e) -> p t e", e=E) for i in range(4))
            cb = comb[:, :].rearrange("p (t e) -> p t e", e=E)
            m1 = rs_[:, 0:NT]
            prio = kc[:, K_PRIO:K_PRIO + E].unsqueeze(1).to_broadcast(full)

            def over(r):
                return r.unsqueeze(2).to_broadcast(full)
            dve.wait_ge(S["lg_ps"], 1)
            lp = bank[5][:, 0:NT * E].rearrange("p (t e) -> p t e", e=E)
            v.tensor_tensor(lv[:, 0:PAIRS, :], lp[:, 0:PAIRS, :],
                            brb[:, :].unsqueeze(1).to_broadcast([P, PAIRS, E]), ALU.add)
            link(v.tensor_tensor(lv[0:IMG, PAIRS, :], lp[0:IMG, PAIRS, :], brb[0:IMG, :], ALU.add))
            link(v.tensor_reduce(m1, lv, axis=AX_X, op=ALU.max))
            v.tensor_tensor(lv, lv, over(m1), ALU.subtract).then_inc(S["lg_ok"], 1)
            dve.wait_ge(S["lexp_ok"], 1)
            link(v.tensor_reduce(m1, lv, axis=AX_X, op=ALU.add))
            link(v.reciprocal(rs_[:, NT:2 * NT], m1))
            link(v.tensor_tensor(ra, lv, over(rs_[:, NT:2 * NT]), ALU.mult))
            link(v.tensor_reduce(m1, ra, axis=AX_X, op=ALU.max))
            link(v.tensor_tensor(rb, ra, over(m1), ALU.is_equal))
            link(v.tensor_tensor(rb, rb, prio, ALU.mult))
            link(v.tensor_reduce(m1, rb, axis=AX_X, op=ALU.max))
            link(v.tensor_tensor(rb, rb, over(m1), ALU.is_equal))
            link(v.scalar_tensor_tensor(rc, rb, -2.0, ra, op0=ALU.mult, op1=ALU.add))
            link(v.tensor_reduce(m1, rc, axis=AX_X, op=ALU.max))
            link(v.tensor_tensor(rc, rc, over(m1), ALU.is_equal))
            link(v.tensor_tensor(rc, rc, prio, ALU.mult))
            link(v.tensor_reduce(m1, rc, axis=AX_X, op=ALU.max))
            link(v.tensor_tensor(rc, rc, over(m1), ALU.is_equal))
            link(v.tensor_tensor(rd, rb, rc, ALU.add))
            v.tensor_tensor(cb, ra, rd, ALU.mult).then_inc(S["comb_ok"], 1)
            for g in range(5):
                dve.wait_ge(S["base_ps"], g + 1)
                if g < NBLK:
                    b = slice(g * BLK, (g + 1) * BLK)
                    v.tensor_tensor(KT[:, b], bank[4 + (5 + g) % 4][:, :], KT[:, b], ALU.add)\
                        .then_inc(S["acc_ok"], 1)
                else:
                    v.tensor_tensor(KT[0:IMG, TOK:TOK + C], bank[4 + (5 + g) % 4][0:IMG, 0:C],
                                    KT[0:IMG, TOK:TOK + C], ALU.add).then_inc(S["acc_ok"], 1)
            for e in range(E):
                for g in range(5):
                    u = 5 * e + g
                    dve.wait_ge(S["y2_ps"], u + 1)
                    dve.wait_ge(S["acc_ok"], u + 1)
                    for i in range(4 if g < 4 else 1):
                        t = 4 * g + i
                        m = P if t < PAIRS else IMG
                        last = v.scalar_tensor_tensor(acc[0:m, t, :], bank[4 + (10 + u) % 4][0:m, i * C:(i + 1) * C],
                                                      comb[0:m, t * E + e:t * E + e + 1], acc[0:m, t, :],
                                                      op0=ALU.mult, op1=ALU.add)
                    last.then_inc(S["acc_ok"], 1)

        @block.tensor
        def _(pe):
            t_ = nc.tensor

            def mm(o, l, r, start=True, stop=True):
                return t_.matmul(o, l, r, start=start, stop=stop)

            pe.wait_ge(S["d_const"], 16)
            pe.wait_ge(S["d_rows"], 16 * 11)
            t_.transpose(bank[2][:, 0:NVEC], rows[0:NVEC, :], ident[0:NVEC, 0:NVEC]).then_inc(S["vec_ps"], 1)
            pe.wait_ge(S["vecs_ok"], 1)
            pe.wait_ge(S["d_rel"], 80)
            pe.wait_ge(S["cls_n"], 1)
            o = bank[2][:, 128:128 + M_ALL]
            t_.transpose(o[:, M_W3:M_W3 + C], w3[:, :], ident)
            t_.transpose(o[:, M_WR:M_WR + E], wr[0:E, :], ident[0:E, 0:E])
            t_.transpose(o[:, M_RK:M_RK + P], rel_rows[:, 0:C], ident)
            t_.transpose(o[:, M_RK + P:M_RK + P + 1], rel_rows[0:1, C:2 * C], ident[0:1, 0:1])
            t_.transpose(o[:, M_RV:M_RV + 65], rel_rows[0:65, 2 * C:3 * C], ident[0:65, 0:65])
            t_.transpose(o[:, M_XC:M_XC + 1], clsn[0:1, :], ident[0:1, 0:1]).then_inc(S["misc_ps"], 1)
            pe.wait_ge(S["wn_ok"], 2)
            for w in range(2):
                for r in range(2):
                    last = t_.transpose(bank[3][:, (2 * w + r) * P:(2 * w + r + 1) * P],
                                        wn[:, w, r * P:(r + 1) * P], ident)
            last.then_inc(S["wnT_ps"], 1)

            def patches(t):
                s, r, jh = t // 4, (t // 2) % 2, t % 2
                pe.wait_ge(S["xperm_ok"], 2 * s + r + 1)
                if t >= 2:
                    pe.wait_ge(S["xT_evA" if t % 2 == 0 else "xT_evD"], t // 2)
                for j in range(4):
                    src = (2 * s + r) * 1024 + (4 * jh + j) * P
                    last = t_.transpose(bank[t % 2][:, j * P:(j + 1) * P], xperm[:, src:src + P], ident)
                last.then_inc(S["xT_ps"], 1)

            def embed1(w, n):
                b = slice(n * BLK, (n + 1) * BLK)
                if n >= 2:
                    pe.wait_ge(S["gate_ok" if w == 0 else "xi_ok"], n - 1)
                mm(bank[4 + 2 * w + n % 2][:, :], WnT[:, w, 0, :], xT[:, 0, b], True, False)
                mm(bank[4 + 2 * w + n % 2][:, :], WnT[:, w, 1, :], xT[:, 1, b], False, True)\
                    .then_inc(S["g_ps" if w == 0 else "in_ps"], 1)

            for s in range(2):
                for t in range(4 * s, 4 * s + 4):
                    patches(t)
                if s == 0:
                    pe.wait_ge(S["wnT_ok"], 1)
                pe.wait_ge(S["xT_evA"], 2 * s + 2)
                pe.wait_ge(S["xT_evD"], 2 * s + 2)
                embed1(0, 2 * s)
                embed1(0, 2 * s + 1)

            def embed3(n):
                pe.wait_ge(S["xi_ok"], n + 1)
                if n == 0:
                    pe.wait_ge(S["misc_ok"], 1)
                if n >= 2:
                    pe.wait_ge(S["h0_ok"], n - 1)
                for i in range(TPB):
                    t = n * TPB + i
                    last = mm(bank[n % 2][:, i * C:(i + 1) * C], xi[:, t * P:(t + 1) * P], W3T)
                last.then_inc(S["y_ps"], 1)

            def turn1(n):
                pe.wait_ge(S["xn_ok"], n + 1)
                if n >= 2:
                    pe.wait_ge(S["xnTd_ok"], n - 1)
                for i in range(TPB):
                    last = t_.transpose(bank[2 + n % 2][:, i * P:(i + 1) * P], ST[n % 2][:, i * C:(i + 1) * C], ident)
                last.then_inc(S["xnT_ps"], 1)

            def qkv(n):
                b = slice(n * BLK, (n + 1) * BLK)
                pe.wait_ge(S["xnT_ok"], n + 1)
                if n == 0:
                    pe.wait_ge(S["d_attn"], 64)
                    pe.wait_ge(S["gate_ok"], 4)
                    pe.wait_ge(S["xi_ok"], 4)
                else:
                    pe.wait_ge(S["QT_ok"], n)
                mm(bank[4][:, :], wq, xnT[:, b]).then_inc(S["q_ps"], 1)
                if n:
                    pe.wait_ge(S["KT_ok"], n)
                mm(bank[5][:, :], wk, xnT[:, b]).then_inc(S["k_ps"], 1)
                pe.wait_ge(S["xnTd_ok"], n + 1)
                for half in range(2):
                    if n:
                        pe.wait_ge(S["VBD_ok"], 2 * n - 1 + half)
                    for i in range(4):
                        im = 8 * n + 4 * half + i
                        last = mm(bank[6 + half][:, i * C:(i + 1) * C],
                                  xnTd[:, im * NPATCH:(im + 1) * NPATCH, :].rearrange("p t s -> p (t s)"), wv)
                    last.then_inc(S["v_ps"], 1)

            embed1(1, 0)
            embed1(1, 1)
            embed3(0)
            embed1(1, 2)
            embed3(1)
            turn1(0)
            embed1(1, 3)
            embed3(2)
            turn1(1)
            qkv(0)
            embed3(3)
            turn1(2)
            qkv(1)
            turn1(3)
            qkv(2)
            qkv(3)
            pe.wait_ge(S["QT_ok"], 4)
            mm(bank[4][:, 0:1], wq, xcT)
            mm(bank[4][:, 1:2], wk, xcT)
            mm(bank[4][:, 2:3], wv, xcT).then_inc(S["cls_ps"], 1)

            def turn_cls(g):
                n = g % 4
                src = tc_ if g < 4 else KT
                pe.wait_ge(S["tc_ok" if g < 4 else "uc_ok"], n + 1)
                if g >= 4:
                    pe.wait_ge(S["tc_red"], g - 3)
                for i in range(TPB):
                    t = n * TPB + i
                    last = t_.transpose(bank[4 + n][:, i * P:(i + 1) * P], src[:, t * P:(t + 1) * P], ident)
                last.then_inc(S["tcT_ps"], 1)

            pe.wait_ge(S["QP_ok"], 4)
            pe.wait_ge(S["h0_ok"], 4)
            for a in range(16):
                if a >= 4:
                    pe.wait_ge(S["a2_evA" if a % 2 == 0 else "a2_evD"], (a - 4) // 2 + 1)
                elif a >= 2:
                    pe.wait_ge(S["xnTd_ok"], 4)
                for i in range(4):
                    q = 4 * a + i
                    last = mm(bank[a % 4][:, i * P:(i + 1) * P], relk_bd[:, 2 * (64 - q):2 * (64 - q) + P],
                              QP[:, :, :, q])
                last.then_inc(S["a2_ps"], 1)
                if a == 7:
                    pe.wait_ge(S["clsv_ok"], 1)
                    pe.wait_ge(S["VBD_ok"], 8)
                    pe.wait_ge(S["KT_ok"], 4)
                if a >= 8 and a % 2 == 1:
                    turn_cls((a - 8) // 2)
            for g in range(4, 8):
                turn_cls(g)

            def scores(p):
                if p < 2:
                    pe.wait_ge(S["a2_evA"], 8)
                    pe.wait_ge(S["a2_evD"], 8)
                    pe.wait_ge(S["KM_ok"], 4)
                else:
                    pe.wait_ge(S["st_ok"], p - 1)
                o = bank[p % 2][:, :].rearrange("p (j b q) -> p j b q", j=PJ, b=2)
                for b2 in range(2):
                    im = 2 * p + b2
                    last = mm(o[:, :, b2, :], KM[:, im * NPATCH:(im + 1) * NPATCH, :].rearrange("p t s -> p (t s)"),
                              QP[:, :, im, :])
                last.then_inc(S["s1_ps"], 1)

            def turn_scores(p):
                pe.wait_ge(S["st_ok"], p + 1)
                if p >= 2:
                    pe.wait_ge(S["sub_ok"], p - 1)
                for j in range(PJ):
                    last = t_.transpose(bank[2 + p % 2][:, j * P:(j + 1) * P], ST[p % 2][:, j * P:(j + 1) * P], ident)
                last.then_inc(S["s_ps"], 1)

            def turn_probs(p):
                pe.wait_ge(S["pn_ok"], p + 1)
                if p >= 2:
                    pe.wait_ge(S["pt_ok"], p - 1)
                elif p == 0:
                    pe.wait_ge(S["cx_ok"], 1)
                else:
                    pe.wait_ge(S["ptc_ok"], 1)
                for j in range(PJ):
                    last = t_.transpose(bank[4 + p % 2][:, j * P:(j + 1) * P], SP[p % 3][:, j * P:(j + 1) * P], ident)
                last.then_inc(S["pt_ps"], 1)

            def values(p):
                u = p // 2
                pe.wait_ge(S["pt_ok"], p + 1)
                if p == 0:
                    pe.wait_ge(S["ptc_ok"], 1)
                if u >= 2:
                    pe.wait_ge(S["w1_ev"], u - 1)
                for b2 in range(2):
                    im = 2 * p + b2
                    c0 = (im % 4) * QC
                    for j in range(PJ):
                        last = mm(bank[6 + u % 2][32 * j:32 * j + 32, c0:c0 + QC], VBD[:, im, 32 * j:32 * j + 32],
                                  PT[:, j, im, :])
                if p % 2 == 1:
                    last.then_inc(S["w1_ps"], 1)

            scores(0)
            pe.wait_ge(S["tc_red"], 8)
            t_.transpose(bank[4][:, 0:P], Sct[:, :], ident)
            mm(bank[4][:, P:P + 1], kc[:, K_E8:K_E8 + P], clsv[:, 4:5]).then_inc(S["c0_ps"], 1)
            scores(1)
            turn_scores(0)
            pe.wait_ge(S["p0d_ok"], 1)
            for b2 in range(2):
                last = t_.transpose(bank[5][:, b2 * P:(b2 + 1) * P], p0d[:, b2 * P:(b2 + 1) * P], ident)
            last.then_inc(S["p0T_ps"], 1)
            for i in range(2, PAIRS + 4):
                if i < PAIRS:
                    scores(i)
                if i - 1 < PAIRS:
                    turn_scores(i - 1)
                if 0 <= i - 3 < PAIRS:
                    turn_probs(i - 3)
                if 0 <= i - 4 < PAIRS:
                    values(i - 4)

            def turn_pc(n):
                pe.wait_ge(S["rep_ok"], n + 1)
                if n == 0:
                    pe.wait_ge(S["pt_ok"], PAIRS)
                if n in (1, 2):
                    pe.wait_ge(S["w1_ev"], 8)
                if n == 3:
                    pe.wait_ge(S["pcx_ok"], 1)
                for i in range(TPB):
                    last = t_.transpose(bank[5 + n % 3][:, i * P:(i + 1) * P],
                                        pc_rep[:, n * TPB + i, :, :].rearrange("p h d -> p (h d)"), ident)
                last.then_inc(S["pcT_ps"], 1)

            for n in range(4):
                if n == 2:
                    pe.wait_ge(S["sub_ok"], PAIRS)
                for i in range(16):
                    q = 16 * n + i
                    for j in range(PJ):
                        last = mm(bank[n][32 * j:32 * j + 32, i * IMG:(i + 1) * IMG],
                                  RVBD[:, 32 * (63 - q):32 * (63 - q) + 32], PT[:, j, :, q])
                last.then_inc(S["w2_ps"], 1)
                turn_pc(n)
            mm(bank[4][:, IMG:2 * IMG], kc[:, K_E8T:K_E8T + P], p0x[:, :])
            for j in range(PJ):
                last = mm(bank[4][32 * j:32 * j + 32, 0:IMG], RVBD[:, 32 * NPATCH:32 * NPATCH + 32], PT[:, j, :, NPATCH])
            last.then_inc(S["w2_ps"], 1)

            pe.wait_ge(S["pcx_ok"], 4)
            pe.wait_ge(S["o_ok"], 4)
            for n in range(NBLK):
                if n == 3:
                    pe.wait_ge(S["h1_ok"], 1)
                for i in range(TPB):
                    t = n * TPB + i
                    last = mm(bank[5 + n % 3][:, i * C:(i + 1) * C], OT[:, t * P:(t + 1) * P], wo)
                last.then_inc(S["op_ps"], 1)
                if n == 2:
                    pe.wait_ge(S["oc_ok"], 1)
                    mm(bank[4][0:IMG, 128:256], OTc[:, :], wo).then_inc(S["opc_ps"], 1)
            for n in range(5):
                pe.wait_ge(S["xn2_ok"], n + 1)
                if n == 4:
                    pe.wait_ge(S["h1_ok"], 5)
                for i in range(TPB if n < 4 else 1):
                    m = P if n < 4 else IMG
                    last = t_.transpose(bank[n][:, i * P:i * P + m], ST[n % 2][0:m, i * C:(i + 1) * C], ident[0:m, 0:m])
                last.then_inc(S["x2T_ps"], 1)
            for t in range(NT):
                if t % TPB == 0:
                    pe.wait_ge(S["x2T_ok"], t // TPB + 1)
                m = P if t < PAIRS else IMG
                last = mm(bank[5][0:m, t * E:(t + 1) * E], xn2T[:, t * P:t * P + m], WrT)
            last.then_inc(S["lg_ps"], 1)

            def up(e):
                for s in range(2):
                    for blk in range(5):
                        i = 10 * e + 5 * s + blk
                        if i >= 4:
                            pe.wait_ge(S["gelu_ok"], i - 3)
                        mm(bank[i % 4][:, 0:FB], w1_sb[:, e, s * P:(s + 1) * P], xn2T[:, blk * FB:(blk + 1) * FB])\
                            .then_inc(S["h_ps"], 1)

            def down(e):
                pe.wait_ge(S["gelu_ok"], 10 * (e + 1))
                for g in range(5):
                    u = 5 * e + g
                    pe.wait_ge(S["acc_ok"], 5 + u - 3 if 5 + u - 3 < 5 + u else 0)
                    for i in range(4 if g < 4 else 1):
                        t = 4 * g + i
                        m = P if t < PAIRS else IMG
                        for s in range(2):
                            last = mm(bank[4 + (10 + u) % 4][0:m, i * C:(i + 1) * C], HB[:, e % 2, s, t * P:t * P + m],
                                      w2_sb[:, e, s, :], s == 0, s == 1)
                    last.then_inc(S["y2_ps"], 1)

            pe.wait_ge(S["d_ffn"], 32)
            up(0)
            pe.wait_ge(S["comb_ok"], 1)
            pe.wait_ge(S["x2T_ok"], 5)
            pe.wait_ge(S["h1_ok"], 5)
            for g in range(5):
                if g == 4:
                    pe.wait_ge(S["cT_ok"], 1)
                for i in range(4 if g < 4 else 1):
                    t = 4 * g + i
                    m = P if t < PAIRS else IMG
                    last = t_.transpose(bank[4 + g % 4][0:E, i * P:i * P + m], comb[0:m, t * E:(t + 1) * E],
                                        ident[0:m, 0:m])
                last.then_inc(S["cT_ps"], 1)
            pe.wait_ge(S["d_small"], 64)
            for g in range(5):
                u = 5 + g
                pe.wait_ge(S["cT_ok"], 5 if u == 8 else min(u - 3, 5))
                pe.wait_ge(S["cT_ok"], g + 1)
                if u >= 9:
                    pe.wait_ge(S["acc_ok"], u - 8)
                for i in range(4 if g < 4 else 1):
                    t = 4 * g + i
                    m = P if t < PAIRS else IMG
                    last = mm(bank[4 + u % 4][0:m, i * C:(i + 1) * C], combT[0:E, t * P:t * P + m], b2s[0:E, :])
                last.then_inc(S["base_ps"], 1)
            for e in range(1, E):
                up(e)
                down(e - 1)
            down(E - 1)


_NAMES = ['x', 'cls_tok'] + ['L0_tok_' + n for n in (
    'W1_w', 'W1_b', 'W1_sw', 'W1_sb', 'W2_w', 'W2_b', 'W2_sw', 'W2_sb', 'W3_w', 'W3_b', 'eps_in1', 'eps_out1',
    'eps_in2', 'eps_out2')] + ['L0_attn_' + n for n in (
        'Wq', 'bq', 'Wk', 'bk', 'Wv', 'bv', 'Wo', 'bo', 'rel_k', 'rel_v')] + ['L0_ffn_' + n for n in (
            'Wr', 'br', 'W1', 'b1', 'W2', 'b2')]


def kernel(**inputs):
    import numpy as _np
    import concourse.bacc as _bacc
    from concourse import mybir as _mybir
    from concourse.bass_utils import run_bass_kernel_spmd as _run

    nc = _bacc.Bacc("TRN2", target_bir_lowering=False, num_devices=1)
    arrays, args = {}, []
    for name in ["consts"] + _NAMES:
        a = constants() if name == "consts" else _np.ascontiguousarray(inputs[name])
        arrays[f"in_{name}"] = a
        args.append(nc.dram_tensor(f"in_{name}", a.shape, _mybir.dt.from_np(a.dtype), kind="ExternalInput").ap())
    args.append(nc.dram_tensor("out_0", (IMG, QC, C), _mybir.dt.float32, kind="ExternalOutput").ap())
    vit_kernel(nc, *args)
    r = _run(nc, [arrays], core_ids=[0])
    return r.results[0]["out_0"]
```

```python
from contextlib import ExitStack

import numpy as np

import concourse.bass as bass
from concourse import mybir

ALU = mybir.AluOpType
ACT = mybir.ActivationFunctionType
AX_X = mybir.AxisListType.X
F32 = mybir.dt.float32
F32R = mybir.dt.float32r

P = 128
IMG = 32
NPATCH = 64
PAIRS = IMG // 2
TOK = IMG * NPATCH
C = 128
PIX = 256
H, HD = 8, 16
PJ = H // 2
QC = NPATCH + 1
E = 8
FH = 256
BLK = 512
NBLK = TOK // BLK
TPB = BLK // P
MAX_REL = 68
SCALE = 1.0 / float(np.sqrt(C))
EPS = 1e-5
ALL = TOK + IMG
NT = PAIRS + 1
FB = ALL // 5

K_ID, K_PE, K_E8, K_VM, K_E8T = 0, 128, 256, 384, 512
K_PM, K_HP, K_KP, K_PR, K_PRIO = 640, 644, 646, 648, 664
K_ALL = 672

V_B1, V_SB1, V_EO1, V_B2, V_SB2, V_EO2, V_BQ, V_BK, V_BV, V_FB1 = 0, 1, 2, 3, 4, 5, 6, 7, 8, 9
NVEC = V_FB1 + E * FH // P

M_W3, M_WR, M_RK, M_RV, M_XC = 0, 128, 136, 265, 330
M_ALL = 331
IN_BANKS = (6, 7, 0, 1)
Y_BANKS = (3, 5, 4, 5)
CLS = 128 + M_ALL


def constants():
    p = np.arange(P)[:, None]
    c = np.arange(P)[None, :]
    k = np.zeros((P, K_ALL), np.float32)
    k[:, K_ID:K_ID + P] = p == c
    pos = np.arange(NPATCH, dtype=np.float32)[:, None]
    div = np.exp(np.arange(0, C, 2, dtype=np.float32) * np.float32(-np.log(10000.0) / C))
    ang = pos * div
    pe = np.stack([np.sin(ang), np.cos(ang)], axis=-1).reshape(NPATCH, C)
    k[:, K_PE:K_PE + C] = np.concatenate([pe, pe], axis=0)
    k[:, K_E8:K_E8 + P] = p // HD == c % H
    k[:, K_VM:K_VM + P] = p % 2 == (c // HD) % 2
    k[:, K_E8T:K_E8T + P] = p % H == c // HD
    k[:, K_PM:K_PM + PJ] = p // 32 == np.arange(PJ)
    k[:, K_HP:K_HP + 2] = (p // HD) % 2 == np.arange(2)
    k[:, K_KP:K_KP + 2] = p % 2 == np.arange(2)
    k[:, K_PR:K_PR + PAIRS] = p // H == np.arange(PAIRS)
    k[:, K_PRIO:K_PRIO + E] = E - np.arange(E)[None, :]
    return k


def vit_kernel(nc, consts, x, cls_tok, W1_w, W1_b, W1_sw, W1_sb, W2_w, W2_b, W2_sw, W2_sb, W3_w, W3_b,
               eps_in1, eps_out1, eps_in2, eps_out2, Wq, bq, Wk, bk, Wv, bv, Wo, bo, rel_k, rel_v,
               Wr, br, fW1, fb1, fW2, fb2, out):
    with ExitStack() as ctx:
        def sb(name, cols, parts=P):
            return ctx.enter_context(nc.sbuf_tensor(name, [parts, cols], F32))

        def sem(name):
            return ctx.enter_context(nc.semaphore(name))

        bank = [ctx.enter_context(nc.psum_tensor(f"bank{i}", [P, 512], F32)) for i in range(8)]

        kc = sb("kc", K_ALL)
        ident = kc[:, K_ID:K_ID + P]
        region_c = sb("region_c", PJ * IMG * QC)
        PT = region_c[:, :].rearrange("p (j b q) -> p j b q", j=PJ, b=IMG)
        xnTd = region_c[:, 0:2 * TOK].rearrange("p (t s) -> p t s", s=2)
        gate = region_c[:, 2 * TOK:3 * TOK]
        sp = region_c[:, 3 * TOK:4 * TOK]
        region_d = sb("region_d", 2 * 2 * ALL)
        QP = region_d[:, 0:PJ * TOK].rearrange("p (j b q) -> p j b q", j=PJ, b=IMG)
        QPf = region_d[:, 0:PJ * TOK].rearrange("p (j t) -> p j t", j=PJ)
        HB = region_d[:, :].rearrange("p (u s t) -> p u s t", u=2, s=2)
        pc_rep = region_d[:, 0:TOK].rearrange("p (r h d) -> p r h d", r=PAIRS, h=H)
        wprep = region_d[:, 0:1024].rearrange("p (w i) -> p w i", w=4)
        ei = region_d[:, 1024:1536]
        ei_root = region_d[:, 1536:2048]
        ei_sign = region_d[:, 2048:2560]
        wn = region_d[:, 2560:3072].rearrange("p (w i) -> p w i", w=2)
        rvd = region_d[:, 3072:3072 + QC * HD].rearrange("p (q d) -> p q d", q=QC)
        QT = sb("QT", ALL)
        xn2T = QT
        KT = sb("KT", NT * P)
        acc = KT[:, :].rearrange("p (t c) -> p t c", t=NT)
        region_e = sb("region_e", 4 * 520)
        xi = region_e
        tc_ = region_e
        SP = [region_e[:, 520 * i:520 * i + 520] for i in range(4)]
        h0 = sb("h0", TOK)
        xnT = sb("xnT", TOK)
        OT = xnT
        OTc = sb("OTc", IMG)
        vbd = sb("vbd", IMG * C)
        VBD = vbd[:, :].rearrange("p (b c) -> p b c", b=IMG)
        RVBD = sb("RVBD", QC * 32)
        RV = RVBD[:, :].rearrange("p (q s d) -> p q s d", q=QC, s=2)
        stb = sb("stb", 1024)
        ST = [stb[:, 0:512], stb[:, 512:1024]]
        tmpx = sb("tmpx", 512)
        misc = sb("misc", M_ALL)
        W3T = misc[:, M_W3:M_W3 + C]
        WrT = misc[:, M_WR:M_WR + E]
        relkT = misc[:, M_RK:M_RK + 129]
        relvT = misc[:, M_RV:M_RV + 65]
        xcT = misc[:, M_XC:M_XC + 1]
        relk_bd = sb("relk_bd", 258)
        RKB = relk_bd[:, :].rearrange("p (r s) -> p r s", s=2)
        wnT = sb("wnT", 512)
        WnT = wnT[:, :].rearrange("p (w r o) -> p w r o", w=2, r=2)
        w3 = sb("w3", C)
        wqkvo = sb("wqkvo", 4 * C)
        wq, wk, wv, wo = (wqkvo[:, i * C:(i + 1) * C] for i in range(4))
        rows = sb("rows", P)
        vecs = sb("vecs", NVEC)
        rel_rows = sb("rel_rows", 3 * C)
        wr = sb("wr", C)
        posb = sb("posb", C)
        bob = sb("bob", C)
        brb = sb("brb", E)
        b2s = sb("b2s", C)
        clsr = sb("clsr", C)
        clsn = sb("clsn", C)
        eo = sb("eo", 8)
        nb = sb("nb", 4)
        stats = sb("stats", NT * 6)
        mv = sb("mv", NT * 2)
        ve = sb("ve", NT)
        rstd = sb("rstd", NT)
        mhalf = sb("mhalf", 4)
        clsv = sb("clsv", 8)
        kcq = sb("kcq", NPATCH)
        vcq = sb("vcq", NPATCH)
        Sc = sb("Sc", PAIRS * H)
        Sct = sb("Sct", PAIRS * H)
        cx = sb("cx", 2 * QC)
        p0d = sb("p0d", 4 * NPATCH)
        sml = sb("sml", 16)
        p0x = sb("p0x", IMG)
        ptt = sb("ptt", NPATCH)
        top = sb("top", 2 * H)
        ntop = sb("ntop", 2 * H)
        esum = sb("esum", 2 * H)
        rsum = sb("rsum", 2 * H)
        nSc = sb("nSc", PAIRS * H)
        PcA = sb("PcA", PAIRS * H)
        lg = sb("lg", NT * E)
        rt = sb("rt", 4 * NT * E)
        rs_ = sb("rs_", 2 * NT)
        comb = sb("comb", NT * E)
        combT = vbd

        early = ExitStack()
        region_a = early.enter_context(nc.sbuf_tensor("region_a", [P, 8192], F32))
        xraw = region_a[:, 0:4096].rearrange("p (s n) -> p s n", s=2)
        xperm = region_a[:, 4096:8192]
        A2 = region_a[:, :].rearrange("p (j b q) -> p j b q", j=PJ, b=IMG)
        region_b = early.enter_context(nc.sbuf_tensor("region_b", [P, 4096], F32))
        xT = region_b[:, :].rearrange("p (r t) -> p r t", r=2)
        KM = region_b[:, :].rearrange("p (t s) -> p t s", s=2)
        early.close()
        w1_sb = sb("w1_sb", E * FH)
        w2_all = sb("w2_all", E * 2 * C)
        w2_sb = w2_all[:, :].rearrange("p (e s d) -> p e s d", e=E, s=2)
        w1_hi, w1_lo, x_hi, x_lo = (ctx.enter_context(nc.sbuf_tensor(n, [P, w], F32R)) for n, w in (
            ("w1_hi", E * FH), ("w1_lo", E * FH), ("x_hi", ALL), ("x_lo", ALL)))

        names = """d_const d_rows d_bias d_w1 d_w2 d_x0 d_x1 d_x2 d_small d_rel d_rvd d_attn d_ffn d_fw1 d_out w1hi_ok w1_split xlo_ok xhi_ok
        vec_ps vecs_ok eo_act ei_act feo_ok wn_ok wnT_ps wnT_okA wnT_ok cls_n misc_ps misc_ok nb_ok
        d_cls d_w3 xperm_ok xT_ps xT_evA xT_evD g_ps gate_ok tmin_ok tanh_ok m_ok in_ps xi_ok y_ps h0_ok ve_ok rstd_ok
        xn_ok xnT_ps xnT_ok xnTd_ok q_ps k_ps v_ps QT_ok KT_ok QP_ok KM_ok VBD_ok cls_ps clsv_ok
        a2_ps a2_evA a2_evD kcq_ok tc_ok ua_ok uc_ok tcT_ps tc_red c0_ps cx_ok cexp_ok p0d_ok p0T_ps ptc_ok
        pc_m ve_c rstd_c
        s1_ps st_ok s_ps top_ok e_ok r_ok pn_ok pc_ok pt_ps pt_ok w1_ps w1_ev
        rep_ok pcT_ps pcx_ok w2_ps o_ok p00_ps oc_ok op_ps opc_ps h1_ok h1c_ok ve2_ok rstd2_ok xn2_ok x2T_ps x2T_ok
        lg_ps lg_ok lexp_ok comb_ok cT_ps cT_ok base_ps acc_ok h_ps gelu_ok y2_ps
        h0o_ok relkb_ok QP0_ok
        dve_c dve_m act_c pool_c""".split()
        S = {n: sem(n) for n in names}

        def chain(eng, name):
            n = [0]

            def link(ins):
                n[0] += 1
                ins.then_inc(S[name], 1)
                eng.wait_ge(S[name], n[0])
            return link

        block = ctx.enter_context(nc.Block())
        relk8 = rel_k.unsqueeze(1)
        relv8 = rel_v.unsqueeze(1)

        @block.sync
        def _(sp_):
            xv = x.rearrange("(s b) o (i r) w -> s (b o i) (r w)", s=2, i=8)
            for half in range(2):
                sp_.dma_start(xraw[:, 0, half * 1024:(half + 1) * 1024],
                              xv[0, :, half * 1024:(half + 1) * 1024]).then_inc(S[f"d_x{half}"], 16)
            for r, b in ((V_EO1, eps_out1), (V_EO2, eps_out2), (V_B1, W1_b), (V_SB1, W1_sb), (V_B2, W2_b),
                         (V_SB2, W2_sb)):
                sp_.dma_start(rows[r:r + 1, :], b.unsqueeze(0)).then_inc(S["d_rows"], 16)
            for i, w in enumerate((W1_w, W1_sw, W2_w, W2_sw)):
                sp_.dma_start(wprep[:, i, :], w).then_inc(S["d_w2"], 16)
            sp_.dma_start(xraw[:, 1, :], xv[1]).then_inc(S["d_x2"], 16)
            for i, w in enumerate((Wq, Wk, Wv, Wo)):
                sp_.dma_start(wqkvo[:, i * C:(i + 1) * C], w).then_inc(S["d_attn"], 16)
            for par in range(2):
                src = bass.AP(tensor=rel_v.tensor, offset=rel_v.offset + 5 * HD, ap=[[HD, NPATCH], [1, QC * HD]])
                sp_.dma_start(region_d[par:P:2, 3072:3072 + QC * HD], src).then_inc(S["d_rvd"], 16)
            sp_.wait_ge(S["st_ok"], PAIRS)
            sp_.dma_start(w1_sb[:, :].rearrange("p (e h) -> p e h", e=E), fW1.rearrange("e d h -> d e h"))\
                .then_inc(S["d_fw1"], 16)
            sp_.dma_start(w2_sb, fW2.rearrange("e (s h) d -> h e s d", s=2)).then_inc(S["d_ffn"], 16)
            ov = out.rearrange("(r b) t c -> b t r c", b=2)
            for g in range(5):
                sp_.wait_ge(S["acc_ok"], 5 + 5 * (E - 1) + g + 1)
                if g < 4:
                    for b2 in range(2):
                        sp_.dma_start(ov[b2, 1:QC, 4 * g:4 * g + 4, :],
                                      acc[64 * b2:64 * b2 + 64, 4 * g:4 * g + 4, :]).then_inc(S["d_out"], 16)
                else:
                    sp_.dma_start(out[:, 0, :], acc[0:IMG, PAIRS, :]).then_inc(S["d_out"], 16)
            sp_.wait_ge(S["d_out"], 16 * 9)

        @block.gpsimd
        def _(pool):
            g = nc.gpsimd
            link = chain(pool, "pool_c")
            g.dma_start(rows[V_FB1:NVEC, :], fb1.rearrange("e (s h) -> (e s) h", s=2)).then_inc(S["d_bias"], 16)
            for r, b in ((V_BQ, bq), (V_BK, bk), (V_BV, bv)):
                g.dma_start(rows[r:r + 1, :], b.unsqueeze(0)).then_inc(S["d_bias"], 16)
            g.dma_start(clsr[0:IMG, :], cls_tok.rearrange("a b c -> (a b) c").to_broadcast([IMG, C]))\
                .then_inc(S["d_cls"], 16)
            g.dma_start(w3[:, :], W3_w).then_inc(S["d_w3"], 16)
            g.dma_start(rel_rows[:, 0:C].rearrange("p (h d) -> p h d", h=H),
                        relk8[4:132].to_broadcast([P, H, HD])).then_inc(S["d_rel"], 16)
            g.dma_start(rel_rows[0:1, C:2 * C].rearrange("p (h d) -> p h d", h=H),
                        relk8[132:133].to_broadcast([1, H, HD])).then_inc(S["d_rel"], 16)
            g.dma_start(rel_rows[0:65, 2 * C:3 * C].rearrange("p (h d) -> p h d", h=H),
                        relv8[4:69].to_broadcast([65, H, HD])).then_inc(S["d_rel"], 16)
            g.dma_start(wr[0:E, :], Wr).then_inc(S["d_rel"], 16)
            g.dma_start(posb[:, :], W3_b.unsqueeze(0).to_broadcast([P, C])).then_inc(S["d_small"], 16)
            g.dma_start(bob[:, :], bo.unsqueeze(0).to_broadcast([P, C])).then_inc(S["d_small"], 16)
            g.dma_start(brb[:, :], br.unsqueeze(0).to_broadcast([P, E])).then_inc(S["d_small"], 16)
            g.dma_start(b2s[0:E, :], fb2).then_inc(S["d_small"], 16)
            link(g.memset(mhalf[:, :], -0.5))
            pool.wait_ge(S["ve_c"], 1)
            g.tensor_tensor(clsn[0:1, 2:3], clsn[0:1, 1:2], mhalf[0:1, 0:1], ALU.pow).then_inc(S["rstd_c"], 1)
            bb = [P, BLK // NPATCH, NPATCH]

            def gated(n):
                pool.wait_ge(S["tanh_ok"], n + 1)
                b = slice(n * BLK, (n + 1) * BLK)
                g.tensor_tensor(gate[:, b], gate[:, b], sp[:, b], ALU.mult).then_inc(S["m_ok"], 1)

            def deviation(n):
                pool.wait_ge(S["ve_ok"], n + 1)
                g.tensor_tensor(rstd[:, n * TPB:(n + 1) * TPB], ve[:, n * TPB:(n + 1) * TPB], mhalf[:, :],
                                ALU.pow).then_inc(S["rstd_ok"], 1)

            def queries(n):
                b = slice(n * BLK, (n + 1) * BLK)
                pool.wait_ge(S["QT_ok"], n + 1)
                g.tensor_tensor(QPf[:, 0, b], QT[:, b], kc[:, K_PM:K_PM + 1].to_broadcast([P, BLK]), ALU.mult)\
                    .then_inc(S["QP0_ok"], 1)
                if n == 0:
                    pool.wait_ge(S["kcq_ok"], 1)
                g.tensor_tensor(tc_[:, b].rearrange("p (b q) -> p b q", q=NPATCH),
                                QT[:, b].rearrange("p (b q) -> p b q", q=NPATCH),
                                kcq[:, :].unsqueeze(1).to_broadcast(bb), ALU.mult).then_inc(S["tc_ok"], 1)

            gated(0)
            gated(1)
            deviation(0)
            gated(2)
            gated(3)
            deviation(1)
            deviation(2)
            deviation(3)
            for n in range(NBLK):
                queries(n)
            for n in range(NBLK):
                b = slice(n * BLK, (n + 1) * BLK)
                pool.wait_ge(S["KM_ok"], n + 1)
                kt = KT[:, b].rearrange("p (b q) -> p b q", q=NPATCH)
                g.tensor_tensor(kt, kt, relkT[:, 65:129].unsqueeze(1).to_broadcast(bb), ALU.add)\
                    .then_inc(S["ua_ok"], 1)
            pool.wait_ge(S["d_small"], 64)
            for n in range(NBLK):
                hv = h0[:, n * BLK:(n + 1) * BLK].rearrange("p (t c) -> p t c", c=C)
                ins = g.tensor_tensor(hv, hv, bob[:, :].unsqueeze(1).to_broadcast([P, TPB, C]), ALU.add)
            ins.then_inc(S["h0o_ok"], 1)
            for p in range(PAIRS):
                pool.wait_ge(S["r_ok"], p + 1)
                e_, r_ = SP[p % 4], rsum[:, 8 * (p % 2):8 * (p % 2) + 8]
                ev = e_[:, 0:512].rearrange("p (j k s) -> p j k s", j=PJ, s=2)
                rv = r_.rearrange("p (j s) -> p j s", j=PJ).unsqueeze(2).to_broadcast([P, PJ, NPATCH, 2])
                g.tensor_tensor(ev, ev, rv, ALU.mult).then_inc(S["pn_ok"], 1)
                g.tensor_tensor(PcA[:, p * H:(p + 1) * H], e_[:, 512:520], r_, ALU.mult).then_inc(S["pc_ok"], 1)
            pool.wait_ge(S["w1hi_ok"], 1)
            g.tensor_tensor(w1_lo[:, :], w1_sb[:, :], w1_hi[:, :].bitcast(F32), ALU.subtract).then_inc(S["w1_split"], 1)

            def low(n):
                b = slice(n * BLK, n * BLK + (BLK if n < NBLK else IMG))
                pool.wait_ge(S["xhi_ok"], n + 1)
                pool.wait_ge(S["x2T_ok"], n + 1)
                g.tensor_tensor(x_lo[:, b], xn2T[:, b], x_hi[:, b].bitcast(F32), ALU.subtract).then_inc(S["xlo_ok"], 1)

            for n in range(5):
                m = P if n < NBLK else IMG
                w = TPB if n < NBLK else 1
                if n >= 2:
                    low(n - 2)
                pool.wait_ge(S["ve2_ok"], n + 1)
                g.tensor_tensor(rstd[0:m, n * TPB:n * TPB + w], ve[0:m, n * TPB:n * TPB + w], mhalf[0:m, 0:w],
                                ALU.pow).then_inc(S["rstd2_ok"], 1)
            low(3)
            low(4)

        @block.scalar
        def _(act):
            a = nc.scalar
            link = chain(act, "act_c")
            a.dma_start(kc[:, :], consts).then_inc(S["d_const"], 16)
            for i, v in enumerate((eps_in1, eps_in2)):
                a.dma_start(ei[:, i * PIX:(i + 1) * PIX], v.unsqueeze(0).to_broadcast([P, PIX]))\
                    .then_inc(S["d_w1"], 16)
            def evac_xT(t):
                act.wait_ge(S["xT_ps"], t + 1)
                s, r, jh = t // 4, (t // 2) % 2, t % 2
                dst = xT[:, r, s * 1024:(s + 1) * 1024].rearrange("p (m g j) -> p g m j", g=2, j=4)[:, jh]
                a.activation(dst, bank[t % 2][:, :].rearrange("p (j m) -> p m j", j=4), ACT.Copy)\
                    .then_inc(S["xT_evA"], 1)

            def softplus(n):
                b = slice(n * BLK, (n + 1) * BLK)
                if n == 0:
                    act.wait_ge(S["nb_ok"], 1)
                act.wait_ge(S["tmin_ok"], n + 1)
                a.activation(gate[:, b], bank[4 + n % 2][:, :], ACT.Identity, bias=nb[:, 0:1])\
                    .then_inc(S["gate_ok"], 1)
                link(a.activation(sp[:, b], sp[:, b], ACT.Exp))
                link(a.activation(sp[:, b], sp[:, b], ACT.Ln, bias=1.0))

            def tanh(n):
                b = slice(n * BLK, (n + 1) * BLK)
                a.activation(sp[:, b], sp[:, b], ACT.Tanh).then_inc(S["tanh_ok"], 1)

            a.preload_act_table_set("sqrt_and_others")
            act.wait_ge(S["d_w1"], 32)
            link(a.activation(ei_root, ei, ACT.Abs))
            a.activation(ei_root, ei_root, ACT.Sqrt).then_inc(S["ei_act"], 1)
            a.activation(ei_sign, ei, ACT.Sign).then_inc(S["ei_act"], 1)
            evac_xT(0)
            act.wait_ge(S["vecs_ok"], 1)
            link(a.activation(eo[:, 0:2], vecs[:, V_EO1:V_EO2 + 1:3], ACT.Abs))
            a.activation(eo[:, 2:4], eo[:, 0:2], ACT.Sqrt).then_inc(S["eo_act"], 1)
            a.activation(eo[:, 4:6], vecs[:, V_EO1:V_EO2 + 1:3], ACT.Sign).then_inc(S["eo_act"], 1)
            a.preload_act_table_set("natural_log_exp_and_others")
            evac_xT(2)
            act.wait_ge(S["wnT_ps"], 1)
            a.activation(wnT[:, 0:256], bank[3][:, 0:256], ACT.Copy).then_inc(S["wnT_okA"], 1)
            softplus(0)
            evac_xT(4)
            softplus(1)
            evac_xT(6)
            a.preload_act_table_set("exp_and_others")
            tanh(0)
            tanh(1)
            act.wait_ge(S["misc_ps"], 1)
            a.activation(misc[:, :], bank[2][:, 128:128 + M_ALL], ACT.Copy).then_inc(S["misc_ok"], 1)
            a.preload_act_table_set("natural_log_exp_and_others")
            softplus(2)
            softplus(3)
            a.preload_act_table_set("exp_and_others")
            tanh(2)
            tanh(3)

            def evac_xn(n):
                b = slice(n * BLK, (n + 1) * BLK)
                act.wait_ge(S["xnT_ps"], n + 1)
                a.activation(xnT[:, b], bank[2 + n % 2][:, :], ACT.Copy).then_inc(S["xnT_ok"], 1)
                a.activation(xnTd[:, b, :], bank[2 + n % 2][:, :].unsqueeze(2).to_broadcast([P, BLK, 2]),
                             ACT.Copy).then_inc(S["xnTd_ok"], 1)

            def evac_qk(n):
                b = slice(n * BLK, (n + 1) * BLK)
                act.wait_ge(S["q_ps"], n + 1)
                a.activation(QT[:, b], bank[6][:, :], ACT.Identity, bias=vecs[:, V_BQ:V_BQ + 1])\
                    .then_inc(S["QT_ok"], 1)
                act.wait_ge(S["k_ps"], n + 1)
                a.activation(KT[:, b], bank[7][:, :], ACT.Identity, bias=vecs[:, V_BK:V_BK + 1])\
                    .then_inc(S["KT_ok"], 1)

            def evac_v(n):
                for half in range(2):
                    u = 2 * n + half
                    act.wait_ge(S["v_ps"], u + 1)
                    for s in range(2):
                        last = a.activation(
                            VBD[:, 4 * u:4 * u + 4, :].rearrange("p b (j s d) -> p (b j) s d", s=2, d=HD)[:, :, s],
                            bank[half][:, :].rearrange("p (m s d) -> p m s d", s=2, d=HD)[:, :, s],
                            ACT.Copy, scale=kc[:, K_KP + s:K_KP + s + 1])
                    last.then_inc(S["VBD_ok"], 1)

            for n in range(NBLK):
                evac_xn(n)
                if n:
                    evac_v(n - 1)
                evac_qk(n)
            evac_v(3)
            act.wait_ge(S["clsv_ok"], 1)
            for i in range(8):
                act.wait_ge(S["a2_ps"], 2 * i + 1)
                a.activation(A2[:, :, :, 8 * i:8 * i + 4].rearrange("p j b q -> p (j b) q"),
                             bank[(2 * i) % 4][:, :].rearrange("p (q m) -> p m q", q=4), ACT.Copy)\
                    .then_inc(S["a2_evA"], 1)
                if i % 2 == 1:
                    n = i // 2
                    b = slice(n * BLK, (n + 1) * BLK)
                    act.wait_ge(S["ua_ok"], n + 1)
                    a.activation(KT[:, b], KT[:, b], ACT.Copy, scale=clsv[:, 0:1]).then_inc(S["uc_ok"], 1)
            for i in range(1, PAIRS + 1):
                if i == 4:
                    act.wait_ge(S["cx_ok"], 1)
                    a.activation(cx[:, :], cx[:, :], ACT.Exp, scale=SCALE).then_inc(S["cexp_ok"], 1)
                if 1 <= i <= PAIRS:
                    p = i - 1
                    act.wait_ge(S["top_ok"], p + 1)
                    if p >= 4:
                        act.wait_ge(S["pt_ps"], p - 3)
                        act.wait_ge(S["pc_ok"], p - 3)
                    if p >= 2:
                        act.wait_ge(S["r_ok"], p - 1)
                    o = 8 * (p % 2)
                    a.activation(SP[p % 4][:, 512:520], SP[p % 4][:, 512:520], ACT.Exp)
                    src = bank[2 + p % 2][:, :].rearrange("p (j k s) -> p j s k", j=PJ, s=2)
                    dst = SP[p % 4][:, 0:512].rearrange("p (j k s) -> p j s k", j=PJ, s=2)
                    for h in range(H):
                        last = a.activation(dst[:, h // 2, h % 2], src[:, h // 2, h % 2], ACT.Exp, scale=SCALE,
                                            bias=ntop[:, o + h:o + h + 1], accum_out=esum[:, o + h:o + h + 1])
                    last.then_inc(S["e_ok"], 1)
            a.preload_act_table_set("gelu_and_others")

            def evac_x2(n):
                m = BLK if n < NBLK else IMG
                act.wait_ge(S["x2T_ps"], n + 1)
                a.activation(x_hi[:, n * BLK:n * BLK + m], bank[7][:, 0:m], ACT.Copy).then_inc(S["xhi_ok"], 1)
                a.activation(xn2T[:, n * BLK:n * BLK + m], bank[7][:, 0:m], ACT.Copy).then_inc(S["x2T_ok"], 1)

            def gelu(i):
                e, s, blk = i // 10, i % 2, (i // 2) % 5
                act.wait_ge(S["h_ps"], i + 1)
                if e >= 2 and i % 10 == 0:
                    act.wait_ge(S["y2_ps"], 5 * (e - 1))
                v = V_FB1 + 2 * e + s
                a.activation(HB[:, e % 2, s, blk * FB:(blk + 1) * FB], bank[i % 4][:, 0:FB], ACT.Gelu,
                             bias=vecs[:, v:v + 1]).then_inc(S["gelu_ok"], 1)

            for n in range(5):
                evac_x2(n)
                if n:
                    gelu(2 * n - 2)
                    gelu(2 * n - 1)
            act.wait_ge(S["lg_ok"], 1)
            a.activation(lg[:, :], lg[:, :], ACT.Exp).then_inc(S["lexp_ok"], 1)
            a.preload_act_table_set("gelu_and_others")
            for i in range(8, 20):
                gelu(i)
            for n in range(5):
                m = BLK if n < NBLK else IMG
                act.wait_ge(S["cT_ps"], n + 1)
                a.activation(combT[0:E, n * BLK:n * BLK + m], bank[4 + n % 4][0:E, 0:m], ACT.Copy)\
                    .then_inc(S["cT_ok"], 1)
            for i in range(20, 10 * E):
                gelu(i)

        @block.vector
        def _(dve):
            v = nc.vector
            link = chain(dve, "dve_c")

            def mark(ins):
                marks[0] += 1
                ins.then_inc(S["dve_m"], 1)
                return marks[0]

            def after(n):
                dve.wait_ge(S["dve_m"], n)
            marks = [0]
            def permute(s, half):
                dve.wait_ge(S[f"d_x{half if s == 0 else 2}"], 16)
                o = (2 * s + half) * 1024
                v.tensor_copy(xperm[:, o:o + 1024].rearrange("p (j r c) -> p r j c", j=8, r=8),
                              xraw[:, s, half * 1024:(half + 1) * 1024].rearrange("p (r j c) -> p r j c", r=8, j=8))\
                    .then_inc(S["xperm_ok"], 1)

            def evac_xT(t):
                dve.wait_ge(S["xT_ps"], t + 1)
                s, r, jh = t // 4, (t // 2) % 2, t % 2
                dst = xT[:, r, s * 1024:(s + 1) * 1024].rearrange("p (m g j) -> p g m j", g=2, j=4)[:, jh]
                v.tensor_copy(dst, bank[t % 2][:, :].rearrange("p (j m) -> p m j", j=4)).then_inc(S["xT_evD"], 1)

            def clamp(n):
                b = slice(n * BLK, (n + 1) * BLK)
                dve.wait_ge(S["g_ps"], n + 1)
                v.tensor_scalar(sp[:, b], bank[4 + n % 2][:, :], nb[:, 0:1], 30.0, ALU.add, ALU.min).then_inc(S["tmin_ok"], 1)

            permute(0, 0)
            permute(0, 1)
            dve.wait_ge(S["vec_ps"], 1)
            v.tensor_copy(vecs[:, :], bank[2][:, 0:NVEC]).then_inc(S["vecs_ok"], 1)
            evac_xT(1)
            dve.wait_ge(S["ei_act"], 2)
            v.tensor_tensor(ei[:, 0:PIX], ei_root[:, 0:PIX], ei_sign[:, 0:PIX], ALU.mult)
            dve.wait_ge(S["eo_act"], 2)
            link(v.tensor_tensor(eo[:, 6:8], eo[:, 2:4], eo[:, 4:6], ALU.mult))
            dve.wait_ge(S["d_w2"], 64)
            for w in range(2):
                if w == 1:
                    link(v.tensor_tensor(ei[:, PIX:2 * PIX], ei_root[:, PIX:2 * PIX], ei_sign[:, PIX:2 * PIX],
                                         ALU.mult))
                link(v.scalar_tensor_tensor(wn[:, w, :], wprep[:, 2 * w + 1, :], eo[:, 6 + w:7 + w],
                                            ei[:, w * PIX:(w + 1) * PIX], op0=ALU.mult, op1=ALU.mult))
                v.tensor_tensor(wn[:, w, :], wn[:, w, :], wprep[:, 2 * w, :], ALU.add).then_inc(S["wn_ok"], 1)
            link(v.tensor_tensor(nb[:, 2:4], vecs[:, V_SB1:V_SB2 + 1:3], eo[:, 6:8], ALU.mult))
            v.tensor_tensor(nb[:, 0:2], nb[:, 2:4], vecs[:, V_B1:V_B2 + 1:3], ALU.add).then_inc(S["nb_ok"], 1)
            dve.wait_ge(S["wnT_ps"], 2)
            v.tensor_copy(wnT[:, 256:512], bank[3][:, 256:512]).then_inc(S["wnT_ok"], 1)
            evac_xT(3)
            permute(1, 0)
            permute(1, 1)
            dve.wait_ge(S["d_cls"], 16)
            link(v.bn_stats(stats[0:1, 0:6], clsr[0:1, :]))
            link(v.bn_aggr(mv[0:1, 0:2], stats[0:1, 0:6]))
            v.tensor_scalar(clsn[0:1, 1:2], mv[0:1, 1:2], EPS, None, ALU.add).then_inc(S["ve_c"], 1)
            dve.wait_ge(S["rstd_c"], 1)
            link(v.tensor_copy(sml[0:1, 0:1], clsn[0:1, 2:3]))
            v.tensor_scalar(clsn[0:1, :], clsr[0:1, :], mv[0:1, 0:1], sml[0:1, 0:1], ALU.subtract, ALU.mult)\
                .then_inc(S["cls_n"], 1)
            clamp(0)
            evac_xT(5)
            clamp(1)
            evac_xT(7)
            dve.wait_ge(S["d_rvd"], 32)
            for s in range(2):
                v.tensor_scalar(RV[:, :, s, :], rvd, kc[:, K_KP + s:K_KP + s + 1], None, ALU.mult)
                if s == 0:
                    clamp(2)
            dve.wait_ge(S["d_small"], 64)
            link(v.tensor_tensor(posb[:, :], posb[:, :], kc[:, K_PE:K_PE + C], ALU.add))

            def inner(n):
                b = slice(n * BLK, (n + 1) * BLK)
                dve.wait_ge(S["in_ps"], n + 1)
                dve.wait_ge(S["m_ok"], n + 1)
                v.scalar_tensor_tensor(xi[:, b], bank[IN_BANKS[n]][:, :], nb[:, 1:2], gate[:, b], op0=ALU.add,
                                       op1=ALU.mult).then_inc(S["xi_ok"], 1)

            def embed(n):
                b = slice(n * BLK, (n + 1) * BLK)
                dve.wait_ge(S["y_ps"], n + 1)
                v.tensor_tensor(h0[:, b].rearrange("p (t c) -> p t c", c=C),
                                bank[Y_BANKS[n]][:, :].rearrange("p (t c) -> p t c", c=C),
                                posb[:, :].unsqueeze(1).to_broadcast([P, TPB, C]), ALU.add)\
                    .then_inc(S["h0_ok"], 1)
                dve.wait_ge(S["h0_ok"], n + 1)
                moments(h0, n, TPB, P, "ve_ok")

            def moments(src, n, w, m, done):
                for t in range(n * TPB, n * TPB + w):
                    last = v.bn_stats(stats[0:m, 6 * t:6 * t + 6], src[0:m, t * C:(t + 1) * C])
                link(last)
                for t in range(n * TPB, n * TPB + w):
                    last = v.bn_aggr(mv[0:m, 2 * t:2 * t + 2], stats[0:m, 6 * t:6 * t + 6])
                link(last)
                v.tensor_scalar(ve[0:m, n * TPB:n * TPB + w],
                                mv[0:m, 2 * n * TPB:2 * (n * TPB + w)].rearrange("p (t s) -> p t s", s=2)[:, :, 1],
                                EPS, None, ALU.add).then_inc(S[done], 1)

            def normalise(src, n, w, m, wait, done, read, count):
                dve.wait_ge(S[wait], n + 1)
                if count > 0:
                    dve.wait_ge(S[read], count)
                for i in range(w):
                    t = n * TPB + i
                    last = v.tensor_scalar(ST[n % 2][0:m, i * C:(i + 1) * C], src[0:m, t * C:(t + 1) * C],
                                           mv[0:m, 2 * t:2 * t + 1], rstd[0:m, t:t + 1], ALU.subtract, ALU.mult)
                last.then_inc(S[done], 1)

            def masked_queries(n):
                b = slice(n * BLK, (n + 1) * BLK)
                dve.wait_ge(S["QT_ok"], n + 1)
                for j in range(1, PJ):
                    last = v.tensor_scalar(QPf[:, j, b], QT[:, b], kc[:, K_PM + j:K_PM + j + 1], None, ALU.mult)
                last.then_inc(S["QP_ok"], 1)

            def masked_keys(n):
                b = slice(n * BLK, (n + 1) * BLK)
                dve.wait_ge(S["KT_ok"], n + 1)
                for s in range(2):
                    last = v.tensor_scalar(KM[:, b, s], KT[:, b], kc[:, K_HP + s:K_HP + s + 1], None, ALU.mult)
                last.then_inc(S["KM_ok"], 1)

            def norm1(n):
                normalise(h0, n, TPB, P, "rstd_ok", "xn_ok", "xnT_ps", n - 1)

            inner(0)
            clamp(3)
            dve.wait_ge(S["misc_ok"], 1)
            for s in range(2):
                v.tensor_scalar(RKB[:, :, s], relkT, kc[:, K_HP + s:K_HP + s + 1], None, ALU.mult)\
                    .then_inc(S["relkb_ok"], 1)
            dve.wait_ge(S["cls_ps"], 1)
            link(v.tensor_tensor(clsv[:, 0:2], bank[2][:, CLS:CLS + 2], vecs[:, V_BQ:V_BK + 1], ALU.add))
            link(v.tensor_copy(clsv[:, 2:3], bank[2][:, CLS + 2:CLS + 3]))
            link(v.tensor_tensor(clsv[:, 3:4], clsv[:, 1:2], relkT[:, 64:65], ALU.add))
            link(v.tensor_tensor(clsv[:, 4:5], clsv[:, 3:4], clsv[:, 0:1], ALU.mult))
            v.tensor_tensor(clsv[:, 5:6], clsv[:, 2:3], relvT[:, 64:65], ALU.add).then_inc(S["clsv_ok"], 1)
            v.tensor_scalar(kcq[:, :], misc[:, M_RK + 63:M_RK - 1:-1], clsv[:, 1:2], None, ALU.add)\
                .then_inc(S["kcq_ok"], 1)
            v.tensor_scalar(vcq[:, :], misc[:, M_RV + 63:M_RV - 1:-1], clsv[:, 2:3], None, ALU.add)

            embed(0)
            inner(1)
            norm1(0)
            inner(2)
            embed(1)
            inner(3)
            norm1(1)
            embed(2)
            masked_queries(0)
            norm1(2)
            embed(3)
            masked_queries(1)
            norm1(3)
            masked_queries(2)
            masked_queries(3)

            def red(g):
                dve.wait_ge(S["tcT_ps"], g + 1)
                dst = (Sc if g < 4 else Sct)[:, (g % 4) * 32:(g % 4) * 32 + 32]
                v.tensor_reduce(dst, bank[4 + g % 4][:, :].rearrange("p (m d) -> p m d", d=HD), axis=AX_X,
                                op=ALU.add).then_inc(S["tc_red"], 1)

            for i in range(8):
                if i < 4:
                    masked_keys(i)
                dve.wait_ge(S["a2_ps"], 2 * i + 2)
                v.tensor_copy(A2[:, :, :, 8 * i + 4:8 * i + 8].rearrange("p j b q -> p (j b) q"),
                              bank[(2 * i + 1) % 4][:, :].rearrange("p (q m) -> p m q", q=4))\
                    .then_inc(S["a2_evD"], 1)
                if i >= 4:
                    red(i - 4)
            dve.wait_ge(S["tc_red"], 4)
            link(v.tensor_scalar(nSc[:, :], Sc[:, :], -SCALE, None, ALU.mult))

            def add(p):
                dve.wait_ge(S["s1_ps"], p + 1)
                if p >= 2:
                    dve.wait_ge(S["s_ps"], p - 1)
                v.tensor_tensor(ST[p % 2].rearrange("p (j m) -> p j m", j=PJ),
                                bank[p % 2][:, :].rearrange("p (j m) -> p j m", j=PJ),
                                A2[:, :, 2 * p:2 * p + 2, :].rearrange("p j b q -> p j (b q)"), ALU.add)\
                    .then_inc(S["st_ok"], 1)

            def softmax(p, r, new):
                if r is not None:
                    q = slice(8 * (r % 2), 8 * (r % 2) + 8)
                    dve.wait_ge(S["e_ok"], r + 1)
                    total = mark(v.tensor_tensor(esum[:, q], esum[:, q], SP[r % 4][:, 512:520], ALU.add))
                if p is not None:
                    o = slice(8 * (p % 2), 8 * (p % 2) + 8)
                    dve.wait_ge(S["s_ps"], p + 1)
                    most = mark(v.tensor_reduce(top[:, o].rearrange("p (j s) -> p j s", j=PJ),
                                                bank[2 + p % 2][:, :].rearrange("p (j k s) -> p j s k", j=PJ, s=2),
                                                axis=AX_X, op=ALU.max))
                if r is not None:
                    after(total)
                    if r >= 2:
                        dve.wait_ge(S["pc_ok"], r - 1)
                    v.reciprocal(rsum[:, q], esum[:, q]).then_inc(S["r_ok"], 1)
                if p is not None:
                    after(most)
                    if p >= 2:
                        dve.wait_ge(S["e_ok"], p - 1)
                    most = mark(v.scalar_tensor_tensor(ntop[:, o], top[:, o], -SCALE, nSc[:, p * H:(p + 1) * H],
                                                       op0=ALU.mult, op1=ALU.min))
                if new is not None:
                    add(new)
                if p is not None:
                    after(most)
                    if p >= 4:
                        dve.wait_ge(S["pc_ok"], p - 3)
                    v.tensor_tensor(SP[p % 4][:, 512:520], ntop[:, o], nSc[:, p * H:(p + 1) * H], ALU.subtract)\
                        .then_inc(S["top_ok"], 1)

            def probs(p):
                dve.wait_ge(S["pt_ps"], p + 1)
                v.tensor_copy(PT[:, :, 2 * p:2 * p + 2, 0:NPATCH],
                              bank[4 + p % 2][:, :].rearrange("p (j b q) -> p j b q", j=PJ, b=2)).then_inc(S["pt_ok"], 1)

            cv = cx[:, :].rearrange("p (b k) -> p b k", b=2)
            m2, c00, r2 = sml[:, 2:4], sml[:, 4:5], sml[:, 6:8]

            def class_scores():
                dve.wait_ge(S["c0_ps"], 1)
                cps = bank[7][:, 0:P].rearrange("p (b k) -> p b k", b=2)
                v.tensor_copy(c00, bank[7][:, P:P + 1])
                link(v.tensor_reduce(m2, cps, axis=AX_X, op=ALU.max))
                link(v.tensor_scalar(m2, m2, c00, None, ALU.max))
                v.tensor_tensor(cv[:, :, 0:NPATCH], cps, m2.unsqueeze(2).to_broadcast([P, 2, NPATCH]), ALU.subtract)
                v.tensor_scalar(cv[:, :, NPATCH], m2, -1.0, c00, ALU.mult, ALU.add).then_inc(S["cx_ok"], 1)

            def class_probs():
                dve.wait_ge(S["cexp_ok"], 1)
                link(v.tensor_reduce(r2, cv, axis=AX_X, op=ALU.add))
                link(v.reciprocal(sml[:, 8:10], r2))
                v.tensor_tensor(p0d[:, :].rearrange("p (b k s) -> p b k s", b=2, s=2),
                                cv[:, :, 0:NPATCH].unsqueeze(3).to_broadcast([P, 2, NPATCH, 2]),
                                sml[:, 8:10].unsqueeze(2).unsqueeze(3).to_broadcast([P, 2, NPATCH, 2]), ALU.mult)
                link(v.tensor_tensor(sml[:, 10:12], cv[:, :, NPATCH], sml[:, 8:10], ALU.mult))
                v.tensor_tensor(p0x[:, :].rearrange("p (r b) -> p r b", b=2),
                                kc[:, K_PR:K_PR + PAIRS].unsqueeze(2).to_broadcast([P, PAIRS, 2]),
                                sml[:, 10:12].unsqueeze(1).to_broadcast([P, PAIRS, 2]), ALU.mult)\
                    .then_inc(S["p0d_ok"], 1)

            def class_turned():
                dve.wait_ge(S["p0T_ps"], 1)
                for b2 in range(2):
                    pv = bank[6][:, b2 * P:(b2 + 1) * P].rearrange("p (r j s) -> p r j s", r=PAIRS, j=PJ)
                    tv = ptt[:, :].rearrange("p (r j) -> p r j", j=PJ)
                    link(v.tensor_scalar(tv, pv[:, :, :, 1], kc[:, K_KP + 1:K_KP + 2], None, ALU.mult))
                    last = v.scalar_tensor_tensor(PT[:, :, b2:IMG:2, NPATCH].rearrange("p j r -> p r j"),
                                                  pv[:, :, :, 0], kc[:, K_KP:K_KP + 1], tv, op0=ALU.mult,
                                                  op1=ALU.add)
                    if b2 == 0:
                        link(last)
                last.then_inc(S["ptc_ok"], 1)

            add(0)
            def outputs(u):
                dve.wait_ge(S["w1_ps"], u + 1)
                o = bank[6 + u % 2][:, 0:4 * QC].rearrange("p (b q) -> p b q", b=4)
                v.tensor_copy(OT[:, 256 * u:256 * u + 256].rearrange("p (b q) -> p b q", b=4), o[:, :, 0:NPATCH])
                v.tensor_copy(OTc[:, 4 * u:4 * u + 4], o[:, :, NPATCH]).then_inc(S["w1_ev"], 1)

            for p in range(PAIRS + 6):
                softmax(p if p < PAIRS else None, p - 2 if 0 <= p - 2 < PAIRS else None,
                        p + 1 if p + 1 < PAIRS else None)
                if 3 <= p < PAIRS + 3:
                    probs(p - 3)
                if p < 2:
                    red(4 + 2 * p)
                    red(5 + 2 * p)
                if p == 2:
                    class_scores()
                if p == 3:
                    class_probs()
                if p == 4:
                    class_turned()
                if p >= 6 and p % 2 == 1:
                    outputs((p - 7) // 2)

            dve.wait_ge(S["pc_ok"], PAIRS)
            for n in range(NBLK):
                last = v.tensor_copy(pc_rep[:, 4 * n:4 * n + 4, :, :].rearrange("p r h d -> p (r h) d"),
                                     PcA[:, 32 * n:32 * n + 32].unsqueeze(2).to_broadcast([P, 32, HD]))
                last.then_inc(S["rep_ok"], 1)
            dve.wait_ge(S["w1_ev"], 8)
            for n in range(NBLK):
                b = slice(n * BLK, (n + 1) * BLK)
                dve.wait_ge(S["pcT_ps"], n + 1)
                if n:
                    dve.wait_ge(S["pc_m"], n)
                v.tensor_tensor(tmpx[:, :].rearrange("p (b q) -> p b q", q=NPATCH),
                                bank[5 + n % 3][:, :].rearrange("p (b q) -> p b q", q=NPATCH),
                                vcq[:, :].unsqueeze(1).to_broadcast([P, 8, NPATCH]), ALU.mult)\
                    .then_inc(S["pcx_ok"], 1)
                dve.wait_ge(S["pcx_ok"], n + 1)
                v.tensor_tensor(OT[:, b], OT[:, b], tmpx[:, :], ALU.add).then_inc(S["pc_m"], 1)
            dve.wait_ge(S["d_fw1"], 16)
            v.tensor_copy(w1_hi[:, :], w1_sb[:, :]).then_inc(S["w1hi_ok"], 1)
            dve.wait_ge(S["pc_m"], NBLK)
            ov = OT[:, :].rearrange("p (b q) -> p b q", q=NPATCH)
            for n in range(4):
                dve.wait_ge(S["w2_ps"], n + 1)
                o = ov[:, :, 16 * n:16 * n + 16]
                v.scalar_tensor_tensor(o, bank[n][:, :].rearrange("p (q b) -> p b q", q=16),
                                       vecs[:, V_BV:V_BV + 1], o, op0=ALU.add, op1=ALU.add).then_inc(S["o_ok"], 1)
            dve.wait_ge(S["w2_ps"], 5)
            link(v.scalar_tensor_tensor(OTc[:, :], bank[4][:, 0:IMG], vecs[:, V_BV:V_BV + 1], OTc[:, :],
                                        op0=ALU.add, op1=ALU.add))
            v.scalar_tensor_tensor(OTc[:, :], bank[4][:, IMG:2 * IMG], clsv[:, 5:6], OTc[:, :], op0=ALU.mult,
                                   op1=ALU.add).then_inc(S["oc_ok"], 1)
            link(v.tensor_tensor(clsr[0:IMG, :], clsr[0:IMG, :], bob[0:IMG, :], ALU.add))
            dve.wait_ge(S["h0o_ok"], 1)
            link(v.memset(lg[:, PAIRS * E:NT * E], 0.0))

            def residual(n):
                if n < NBLK:
                    dve.wait_ge(S["op_ps"], n + 1)
                    b = slice(n * BLK, (n + 1) * BLK)
                    v.tensor_tensor(KT[:, b], bank[5 + n % 2][:, :], h0[:, b], ALU.add).then_inc(S["h1_ok"], 1)
                    dve.wait_ge(S["h1_ok"], n + 1)
                    moments(KT, n, TPB, P, "ve2_ok")
                else:
                    dve.wait_ge(S["h1c_ok"], 1)
                    moments(KT, n, 1, IMG, "ve2_ok")

            def norm2(n):
                full = n < NBLK
                normalise(KT, n, TPB if full else 1, P if full else IMG, "rstd2_ok", "xn2_ok", "x2T_ps", n - 1)

            residual(0)
            dve.wait_ge(S["opc_ps"], 1)
            v.tensor_tensor(KT[0:IMG, TOK:TOK + C], bank[4][0:IMG, 128:256], clsr[0:IMG, :], ALU.add)\
                .then_inc(S["h1c_ok"], 1)
            for n in range(1, 5):
                residual(n)
                norm2(n - 1)
            norm2(4)
            lv = lg[:, :].rearrange("p (t e) -> p t e", e=E)
            full = [P, NT, E]
            ra, rb, rc, rd = (rt[:, i * NT * E:(i + 1) * NT * E].rearrange("p (t e) -> p t e", e=E) for i in range(4))
            cb = comb[:, :].rearrange("p (t e) -> p t e", e=E)
            m1 = rs_[:, 0:NT]
            prio = kc[:, K_PRIO:K_PRIO + E].unsqueeze(1).to_broadcast(full)

            def over(r):
                return r.unsqueeze(2).to_broadcast(full)
            dve.wait_ge(S["lg_ps"], 5)
            lp = bank[4][:, 256:256 + NT * E].rearrange("p (t e) -> p t e", e=E)
            v.tensor_tensor(lv[:, 0:PAIRS, :], lp[:, 0:PAIRS, :],
                            brb[:, :].unsqueeze(1).to_broadcast([P, PAIRS, E]), ALU.add)
            link(v.tensor_tensor(lv[0:IMG, PAIRS, :], lp[0:IMG, PAIRS, :], brb[0:IMG, :], ALU.add))
            link(v.tensor_reduce(m1, lv, axis=AX_X, op=ALU.max))
            v.tensor_tensor(lv, lv, over(m1), ALU.subtract).then_inc(S["lg_ok"], 1)
            dve.wait_ge(S["lexp_ok"], 1)
            link(v.tensor_reduce(m1, lv, axis=AX_X, op=ALU.add))
            link(v.reciprocal(rs_[:, NT:2 * NT], m1))
            link(v.tensor_tensor(ra, lv, over(rs_[:, NT:2 * NT]), ALU.mult))
            link(v.tensor_reduce(m1, ra, axis=AX_X, op=ALU.max))
            link(v.tensor_tensor(rb, ra, over(m1), ALU.is_equal))
            link(v.tensor_tensor(rb, rb, prio, ALU.mult))
            link(v.tensor_reduce(m1, rb, axis=AX_X, op=ALU.max))
            link(v.tensor_tensor(rb, rb, over(m1), ALU.is_equal))
            link(v.scalar_tensor_tensor(rc, rb, -2.0, ra, op0=ALU.mult, op1=ALU.add))
            link(v.tensor_reduce(m1, rc, axis=AX_X, op=ALU.max))
            link(v.tensor_tensor(rc, rc, over(m1), ALU.is_equal))
            link(v.tensor_tensor(rc, rc, prio, ALU.mult))
            link(v.tensor_reduce(m1, rc, axis=AX_X, op=ALU.max))
            link(v.tensor_tensor(rc, rc, over(m1), ALU.is_equal))
            link(v.tensor_tensor(rd, rb, rc, ALU.add))
            v.tensor_tensor(cb, ra, rd, ALU.mult).then_inc(S["comb_ok"], 1)
            for g in range(5):
                dve.wait_ge(S["base_ps"], g + 1)
                if g < NBLK:
                    b = slice(g * BLK, (g + 1) * BLK)
                    v.tensor_tensor(KT[:, b], bank[4 + (5 + g) % 4][:, :], KT[:, b], ALU.add)\
                        .then_inc(S["acc_ok"], 1)
                else:
                    v.tensor_tensor(KT[0:IMG, TOK:TOK + C], bank[4 + (5 + g) % 4][0:IMG, 0:C],
                                    KT[0:IMG, TOK:TOK + C], ALU.add).then_inc(S["acc_ok"], 1)
            for e in range(E):
                for g in range(5):
                    u = 5 * e + g
                    dve.wait_ge(S["y2_ps"], u + 1)
                    dve.wait_ge(S["acc_ok"], u + 1)
                    for i in range(4 if g < 4 else 1):
                        t = 4 * g + i
                        m = P if t < PAIRS else IMG
                        last = v.scalar_tensor_tensor(acc[0:m, t, :], bank[4 + (10 + u) % 4][0:m, i * C:(i + 1) * C],
                                                      comb[0:m, t * E + e:t * E + e + 1], acc[0:m, t, :],
                                                      op0=ALU.mult, op1=ALU.add)
                    last.then_inc(S["acc_ok"], 1)

        @block.tensor
        def _(pe):
            t_ = nc.tensor

            def mm(o, l, r, start=True, stop=True):
                return t_.matmul(o, l, r, start=start, stop=stop)

            def patches(t):
                s, r, jh = t // 4, (t // 2) % 2, t % 2
                pe.wait_ge(S["xperm_ok"], 2 * s + r + 1)
                if t >= 2:
                    pe.wait_ge(S["xT_evA" if t % 2 == 0 else "xT_evD"], t // 2)
                for j in range(4):
                    src = (2 * s + r) * 1024 + (4 * jh + j) * P
                    last = t_.transpose(bank[t % 2][:, j * P:(j + 1) * P], xperm[:, src:src + P], ident)
                last.then_inc(S["xT_ps"], 1)

            def embed1(w, n):
                b = slice(n * BLK, (n + 1) * BLK)
                if n >= 2 and w == 0:
                    pe.wait_ge(S["gate_ok"], n - 1)
                    pe.wait_ge(S["tmin_ok"], n - 1)
                if w == 0 and n % 2 == 0:
                    pe.wait_ge(S["xT_evA"], n + 2)
                    pe.wait_ge(S["xT_evD"], n + 2)
                o = bank[4 + n % 2] if w == 0 else bank[IN_BANKS[n]]
                mm(o[:, :], WnT[:, w, 0, :], xT[:, 0, b], True, False)
                mm(o[:, :], WnT[:, w, 1, :], xT[:, 1, b], False, True)\
                    .then_inc(S["g_ps" if w == 0 else "in_ps"], 1)

            def keep_warm(times):
                for _ in range(times):
                    mm(bank[7][:, 0:P], ident, ident)

            pe.wait_ge(S["d_const"], 16)
            keep_warm(2)
            for t in range(2):
                patches(t)
            pe.wait_ge(S["d_rows"], 16 * 6)
            pe.wait_ge(S["d_bias"], 16 * 4)
            t_.transpose(bank[2][:, 0:NVEC], rows[0:NVEC, :], ident[0:NVEC, 0:NVEC]).then_inc(S["vec_ps"], 1)
            keep_warm(5)
            for t in range(2, 4):
                patches(t)
            for w in range(2):
                pe.wait_ge(S["wn_ok"], w + 1)
                if w == 1:
                    pe.wait_ge(S["wnT_okA"], 1)
                for r in range(2):
                    last = t_.transpose(bank[3][:, (2 * w + r) * P:(2 * w + r + 1) * P],
                                        wn[:, w, r * P:(r + 1) * P], ident)
                last.then_inc(S["wnT_ps"], 1)
            keep_warm(1)
            embed1(0, 0)
            patches(4)
            patches(5)
            embed1(0, 1)
            patches(6)
            patches(7)
            pe.wait_ge(S["d_w3"], 16)
            pe.wait_ge(S["d_rel"], 64)
            pe.wait_ge(S["cls_n"], 1)
            o = bank[2][:, 128:128 + M_ALL]
            t_.transpose(o[:, M_W3:M_W3 + C], w3[:, :], ident)
            t_.transpose(o[:, M_WR:M_WR + E], wr[0:E, :], ident[0:E, 0:E])
            t_.transpose(o[:, M_RK:M_RK + P], rel_rows[:, 0:C], ident)
            t_.transpose(o[:, M_RK + P:M_RK + P + 1], rel_rows[0:1, C:2 * C], ident[0:1, 0:1])
            t_.transpose(o[:, M_RV:M_RV + 65], rel_rows[0:65, 2 * C:3 * C], ident[0:65, 0:65])
            t_.transpose(o[:, M_XC:M_XC + 1], clsn[0:1, :], ident[0:1, 0:1]).then_inc(S["misc_ps"], 1)
            embed1(0, 2)
            pe.wait_ge(S["wnT_ok"], 1)
            embed1(1, 0)
            embed1(0, 3)

            def embed3(n):
                pe.wait_ge(S["xi_ok"], n + 1)
                if n:
                    pe.wait_ge(S["gate_ok"], (4, 3, 4)[n - 1])
                if n == 3:
                    pe.wait_ge(S["h0_ok"], 2)
                for i in range(TPB):
                    t = n * TPB + i
                    last = mm(bank[Y_BANKS[n]][:, i * C:(i + 1) * C], xi[:, t * P:(t + 1) * P], W3T)
                last.then_inc(S["y_ps"], 1)

            def turn1(n):
                pe.wait_ge(S["xn_ok"], n + 1)
                if n == 0:
                    pe.wait_ge(S["clsv_ok"], 1)
                if n == 1:
                    pe.wait_ge(S["h0_ok"], 1)
                if n >= 2:
                    pe.wait_ge(S["xnTd_ok"], n - 1)
                for i in range(TPB):
                    last = t_.transpose(bank[2 + n % 2][:, i * P:(i + 1) * P], ST[n % 2][:, i * C:(i + 1) * C], ident)
                last.then_inc(S["xnT_ps"], 1)

            def queries_keys(n):
                b = slice(n * BLK, (n + 1) * BLK)
                pe.wait_ge(S["xnT_ok"], n + 1)
                if n:
                    pe.wait_ge(S["QT_ok"], n)
                mm(bank[6][:, :], wq, xnT[:, b]).then_inc(S["q_ps"], 1)
                if n:
                    pe.wait_ge(S["KT_ok"], n)
                mm(bank[7][:, :], wk, xnT[:, b]).then_inc(S["k_ps"], 1)

            def values_of(n):
                pe.wait_ge(S["xnTd_ok"], n + 1)
                if n == 0:
                    pe.wait_ge(S["xi_ok"], 4)
                for half in range(2):
                    if n:
                        pe.wait_ge(S["VBD_ok"], 2 * n - 1 + half)
                    for i in range(4):
                        im = 8 * n + 4 * half + i
                        last = mm(bank[half][:, i * C:(i + 1) * C],
                                  xnTd[:, im * NPATCH:(im + 1) * NPATCH, :].rearrange("p t s -> p (t s)"), wv)
                    last.then_inc(S["v_ps"], 1)

            pe.wait_ge(S["misc_ok"], 1)
            pe.wait_ge(S["d_attn"], 64)
            mm(bank[2][:, CLS:CLS + 1], wq, xcT)
            mm(bank[2][:, CLS + 1:CLS + 2], wk, xcT)
            mm(bank[2][:, CLS + 2:CLS + 3], wv, xcT).then_inc(S["cls_ps"], 1)
            embed3(0)
            embed1(1, 1)
            embed1(1, 2)
            embed3(1)
            turn1(0)
            embed1(1, 3)
            embed3(2)
            queries_keys(0)
            turn1(1)
            values_of(0)
            embed3(3)
            queries_keys(1)
            turn1(2)
            values_of(1)
            queries_keys(2)
            turn1(3)
            values_of(2)
            queries_keys(3)
            values_of(3)

            def turn_cls(g):
                n = g % 4
                src = tc_ if g < 4 else KT
                pe.wait_ge(S["tc_ok" if g < 4 else "uc_ok"], n + 1)
                if g >= 4:
                    pe.wait_ge(S["tc_red"], g - 3)
                for i in range(TPB):
                    t = n * TPB + i
                    last = t_.transpose(bank[4 + n][:, i * P:(i + 1) * P], src[:, t * P:(t + 1) * P], ident)
                last.then_inc(S["tcT_ps"], 1)

            pe.wait_ge(S["QP_ok"], 4)
            pe.wait_ge(S["QP0_ok"], 4)
            pe.wait_ge(S["VBD_ok"], 8)
            pe.wait_ge(S["relkb_ok"], 2)
            for a in range(16):
                if a >= 4:
                    pe.wait_ge(S["a2_evA" if a % 2 == 0 else "a2_evD"], (a - 4) // 2 + 1)
                elif a >= 2:
                    pe.wait_ge(S["xnTd_ok"], 4)
                for i in range(4):
                    q = 4 * a + i
                    last = mm(bank[a % 4][:, i * P:(i + 1) * P], relk_bd[:, 2 * (64 - q):2 * (64 - q) + P],
                              QP[:, :, :, q])
                last.then_inc(S["a2_ps"], 1)
                if a == 7:
                    pe.wait_ge(S["h0_ok"], 4)
                    pe.wait_ge(S["KT_ok"], 4)
                if a >= 8 and a % 2 == 1:
                    turn_cls((a - 8) // 2)

            def scores(p):
                if p < 2:
                    pe.wait_ge(S["a2_evA"], 8)
                    pe.wait_ge(S["a2_evD"], 8)
                    pe.wait_ge(S["KM_ok"], 4)
                else:
                    pe.wait_ge(S["st_ok"], p - 1)
                o = bank[p % 2][:, :].rearrange("p (j b q) -> p j b q", j=PJ, b=2)
                for b2 in range(2):
                    im = 2 * p + b2
                    last = mm(o[:, :, b2, :], KM[:, im * NPATCH:(im + 1) * NPATCH, :].rearrange("p t s -> p (t s)"),
                              QP[:, :, im, :])
                last.then_inc(S["s1_ps"], 1)

            def turn_scores(p):
                pe.wait_ge(S["st_ok"], p + 1)
                if p >= 2:
                    pe.wait_ge(S["top_ok"], p - 1)
                    pe.wait_ge(S["e_ok"], p - 1)
                for j in range(PJ):
                    last = t_.transpose(bank[2 + p % 2][:, j * P:(j + 1) * P], ST[p % 2][:, j * P:(j + 1) * P], ident)
                last.then_inc(S["s_ps"], 1)

            def turn_probs(p):
                pe.wait_ge(S["pn_ok"], p + 1)
                if p >= 2:
                    pe.wait_ge(S["pt_ok"], p - 1)
                else:
                    pe.wait_ge(S["tc_red"], 5 + p)
                for j in range(PJ):
                    last = t_.transpose(bank[4 + p % 2][:, j * P:(j + 1) * P], SP[p % 4][:, j * P:(j + 1) * P], ident)
                last.then_inc(S["pt_ps"], 1)

            def values(p):
                u = p // 2
                pe.wait_ge(S["pt_ok"], p + 1)
                if p == 0:
                    pe.wait_ge(S["ptc_ok"], 1)
                if u >= 2:
                    pe.wait_ge(S["w1_ev"], u - 1)
                for b2 in range(2):
                    im = 2 * p + b2
                    c0 = (im % 4) * QC
                    for j in range(PJ):
                        last = mm(bank[6 + u % 2][32 * j:32 * j + 32, c0:c0 + QC], VBD[:, im, 32 * j:32 * j + 32],
                                  PT[:, j, im, :])
                if p % 2 == 1:
                    last.then_inc(S["w1_ps"], 1)

            scores(0)
            for p in range(PAIRS + 5):
                if p < PAIRS:
                    turn_scores(p)
                if p + 1 < PAIRS:
                    scores(p + 1)
                if p < 2:
                    turn_cls(4 + 2 * p)
                    turn_cls(5 + 2 * p)
                if p == 2:
                    pe.wait_ge(S["tc_red"], 8)
                    t_.transpose(bank[7][:, 0:P], Sct[:, :], ident)
                    mm(bank[7][:, P:P + 1], kc[:, K_E8:K_E8 + P], clsv[:, 4:5]).then_inc(S["c0_ps"], 1)
                if p == 4:
                    pe.wait_ge(S["p0d_ok"], 1)
                    for b2 in range(2):
                        last = t_.transpose(bank[6][:, b2 * P:(b2 + 1) * P], p0d[:, b2 * P:(b2 + 1) * P], ident)
                    last.then_inc(S["p0T_ps"], 1)
                if 0 <= p - 3 < PAIRS:
                    turn_probs(p - 3)
                if p >= 5:
                    values(p - 5)

            def turn_pc(n):
                pe.wait_ge(S["rep_ok"], n + 1)
                if n == 0:
                    pe.wait_ge(S["pt_ok"], PAIRS)
                if n in (1, 2):
                    pe.wait_ge(S["w1_ev"], 8)
                if n == 3:
                    pe.wait_ge(S["pcx_ok"], 1)
                for i in range(TPB):
                    last = t_.transpose(bank[5 + n % 3][:, i * P:(i + 1) * P],
                                        pc_rep[:, n * TPB + i, :, :].rearrange("p h d -> p (h d)"), ident)
                last.then_inc(S["pcT_ps"], 1)

            for n in range(4):
                if n == 2:
                    pe.wait_ge(S["e_ok"], PAIRS)
                for i in range(16):
                    q = 16 * n + i
                    for j in range(PJ):
                        last = mm(bank[n][32 * j:32 * j + 32, i * IMG:(i + 1) * IMG],
                                  RVBD[:, 32 * (63 - q):32 * (63 - q) + 32], PT[:, j, :, q])
                last.then_inc(S["w2_ps"], 1)
                for t in {0: (0, 1, 2), 1: (3,)}.get(n, ()):
                    turn_pc(t)
            mm(bank[4][:, IMG:2 * IMG], kc[:, K_E8T:K_E8T + P], p0x[:, :])
            for j in range(PJ):
                last = mm(bank[4][32 * j:32 * j + 32, 0:IMG], RVBD[:, 32 * NPATCH:32 * NPATCH + 32], PT[:, j, :, NPATCH])
            last.then_inc(S["w2_ps"], 1)

            pe.wait_ge(S["pcx_ok"], 4)
            pe.wait_ge(S["oc_ok"], 1)
            for n in range(NBLK):
                if n >= 2:
                    pe.wait_ge(S["h1_ok"], n - 1)
                for i in range(TPB):
                    t = n * TPB + i
                    last = mm(bank[5 + n % 2][:, i * C:(i + 1) * C], OT[:, t * P:(t + 1) * P], wo)
                last.then_inc(S["op_ps"], 1)
                if n == 1:
                    mm(bank[4][0:IMG, 128:256], OTc[:, :], wo).then_inc(S["opc_ps"], 1)

            def turn2(n):
                pe.wait_ge(S["xn2_ok"], n + 1)
                if n:
                    pe.wait_ge(S["x2T_ok"], n)
                for i in range(TPB if n < 4 else 1):
                    m = P if n < 4 else IMG
                    last = t_.transpose(bank[7][:, i * P:i * P + m], ST[n % 2][0:m, i * C:(i + 1) * C], ident[0:m, 0:m])
                last.then_inc(S["x2T_ps"], 1)

            def up(e, blk):
                for s in range(2):
                    i = 10 * e + 2 * blk + s
                    if i >= 4:
                        pe.wait_ge(S["gelu_ok"], i - 3)
                    w = slice(e * FH + s * P, e * FH + (s + 1) * P)
                    t = slice(blk * FB, (blk + 1) * FB)
                    o = bank[i % 4][:, 0:FB]
                    mm(o, w1_hi[:, w], x_hi[:, t], True, False)
                    mm(o, w1_lo[:, w], x_hi[:, t], False, False)
                    mm(o, w1_hi[:, w], x_lo[:, t], False, True).then_inc(S["h_ps"], 1)

            def router(n):
                pe.wait_ge(S["x2T_ok"], n + 1)
                if n == 0:
                    pe.wait_ge(S["h1c_ok"], 1)
                for t in range(4 * n, 4 * n + TPB if n < NBLK else NT):
                    m = P if t < PAIRS else IMG
                    last = mm(bank[4][0:m, 256 + t * E:256 + (t + 1) * E], xn2T[:, t * P:t * P + m], WrT)
                last.then_inc(S["lg_ps"], 1)

            turn2(0)
            pe.wait_ge(S["w1_split"], 1)
            for n in range(1, 5):
                turn2(n)
                router(n - 1)
                pe.wait_ge(S["xlo_ok"], n)
                if n == 1:
                    pe.wait_ge(S["o_ok"], 4)
                up(0, n - 1)
            router(4)
            pe.wait_ge(S["xlo_ok"], 5)
            up(0, 4)
            for blk in range(5):
                up(1, blk)

            def down(e):
                for g in range(5):
                    u = 5 * e + g
                    need = min(5, ((g + 1) * BLK + FB - 1) // FB)
                    pe.wait_ge(S["gelu_ok"], 10 * e + 2 * need)
                    pe.wait_ge(S["acc_ok"], u + 2)
                    for i in range(4 if g < 4 else 1):
                        t = 4 * g + i
                        m = P if t < PAIRS else IMG
                        for s in range(2):
                            last = mm(bank[4 + (10 + u) % 4][0:m, i * C:(i + 1) * C], HB[:, e % 2, s, t * P:t * P + m],
                                      w2_sb[:, e, s, :], s == 0, s == 1)
                    last.then_inc(S["y2_ps"], 1)

            pe.wait_ge(S["d_ffn"], 16)
            pe.wait_ge(S["comb_ok"], 1)
            pe.wait_ge(S["x2T_ok"], 5)
            pe.wait_ge(S["h1_ok"], 4)
            for g in range(5):
                if g == 4:
                    pe.wait_ge(S["cT_ok"], 1)
                for i in range(4 if g < 4 else 1):
                    t = 4 * g + i
                    m = P if t < PAIRS else IMG
                    last = t_.transpose(bank[4 + g % 4][0:E, i * P:i * P + m], comb[0:m, t * E:(t + 1) * E],
                                        ident[0:m, 0:m])
                last.then_inc(S["cT_ps"], 1)
            pe.wait_ge(S["d_small"], 64)
            for g in range(5):
                u = 5 + g
                pe.wait_ge(S["cT_ok"], 5 if u == 8 else min(u - 3, 5))
                pe.wait_ge(S["cT_ok"], g + 1)
                if u >= 9:
                    pe.wait_ge(S["acc_ok"], u - 8)
                for i in range(4 if g < 4 else 1):
                    t = 4 * g + i
                    m = P if t < PAIRS else IMG
                    last = mm(bank[4 + u % 4][0:m, i * C:(i + 1) * C], combT[0:E, t * P:t * P + m], b2s[0:E, :])
                last.then_inc(S["base_ps"], 1)
            for e in range(E):
                down(e)
                if e + 2 < E:
                    for blk in range(5):
                        up(e + 2, blk)


_NAMES = ['x', 'cls_tok'] + ['L0_tok_' + n for n in (
    'W1_w', 'W1_b', 'W1_sw', 'W1_sb', 'W2_w', 'W2_b', 'W2_sw', 'W2_sb', 'W3_w', 'W3_b', 'eps_in1', 'eps_out1',
    'eps_in2', 'eps_out2')] + ['L0_attn_' + n for n in (
        'Wq', 'bq', 'Wk', 'bk', 'Wv', 'bv', 'Wo', 'bo', 'rel_k', 'rel_v')] + ['L0_ffn_' + n for n in (
            'Wr', 'br', 'W1', 'b1', 'W2', 'b2')]


def kernel(**inputs):
    import numpy as _np
    import concourse.bacc as _bacc
    from concourse import mybir as _mybir
    from concourse.bass_utils import run_bass_kernel_spmd as _run

    nc = _bacc.Bacc("TRN2", target_bir_lowering=False, num_devices=1)
    arrays, args = {}, []
    for name in ["consts"] + _NAMES:
        a = constants() if name == "consts" else _np.ascontiguousarray(inputs[name])
        arrays[f"in_{name}"] = a
        args.append(nc.dram_tensor(f"in_{name}", a.shape, _mybir.dt.from_np(a.dtype), kind="ExternalInput").ap())
    args.append(nc.dram_tensor("out_0", (IMG, QC, C), _mybir.dt.float32, kind="ExternalOutput").ap())
    vit_kernel(nc, *args)
    r = _run(nc, [arrays], core_ids=[0])
    return r.results[0]["out_0"]
```

```python
from contextlib import ExitStack

import numpy as np

import concourse.bass as bass
from concourse import mybir

ALU = mybir.AluOpType
ACT = mybir.ActivationFunctionType
AX_X = mybir.AxisListType.X
F32 = mybir.dt.float32
F32R = mybir.dt.float32r

P = 128
IMG = 32
NPATCH = 64
PAIRS = IMG // 2
TOK = IMG * NPATCH
C = 128
PIX = 256
H, HD = 8, 16
PJ = H // 2
QC = NPATCH + 1
E = 8
FH = 256
BLK = 512
NBLK = TOK // BLK
TPB = BLK // P
MAX_REL = 68
SCALE = 1.0 / float(np.sqrt(C))
EPS = 1e-5
ALL = TOK + IMG
NT = PAIRS + 1
FB = ALL // 5

K_ID, K_PE, K_E8, K_VM, K_E8T = 0, 128, 256, 384, 512
K_PM, K_HP, K_KP, K_PR, K_PRIO = 640, 644, 646, 648, 664
K_ALL = 672

V_B1, V_SB1, V_EO1, V_B2, V_SB2, V_EO2, V_BQ, V_BK, V_BV, V_FB1 = 0, 1, 2, 3, 4, 5, 6, 7, 8, 9
NVEC = V_FB1 + E * FH // P

M_W3, M_WR, M_RK, M_RV, M_XC = 0, 128, 136, 265, 330
M_ALL = 331
IN_BANKS = (6, 7, 0, 1)
Y_BANKS = (3, 5, 4, 5)
OP_BANKS = (5, 6, 2, 3)
CLS = 128 + M_ALL


def constants():
    p = np.arange(P)[:, None]
    c = np.arange(P)[None, :]
    k = np.zeros((P, K_ALL), np.float32)
    k[:, K_ID:K_ID + P] = p == c
    pos = np.arange(NPATCH, dtype=np.float32)[:, None]
    div = np.exp(np.arange(0, C, 2, dtype=np.float32) * np.float32(-np.log(10000.0) / C))
    ang = pos * div
    pe = np.stack([np.sin(ang), np.cos(ang)], axis=-1).reshape(NPATCH, C)
    k[:, K_PE:K_PE + C] = np.concatenate([pe, pe], axis=0)
    k[:, K_E8:K_E8 + P] = p // HD == c % H
    k[:, K_VM:K_VM + P] = p % 2 == (c // HD) % 2
    k[:, K_E8T:K_E8T + P] = p % H == c // HD
    k[:, K_PM:K_PM + PJ] = p // 32 == np.arange(PJ)
    k[:, K_HP:K_HP + 2] = (p // HD) % 2 == np.arange(2)
    k[:, K_KP:K_KP + 2] = p % 2 == np.arange(2)
    k[:, K_PR:K_PR + PAIRS] = p // H == np.arange(PAIRS)
    k[:, K_PRIO:K_PRIO + E] = E - np.arange(E)[None, :]
    return k


def vit_kernel(nc, consts, x, cls_tok, W1_w, W1_b, W1_sw, W1_sb, W2_w, W2_b, W2_sw, W2_sb, W3_w, W3_b,
               eps_in1, eps_out1, eps_in2, eps_out2, Wq, bq, Wk, bk, Wv, bv, Wo, bo, rel_k, rel_v,
               Wr, br, fW1, fb1, fW2, fb2, out):
    with ExitStack() as ctx:
        def sb(name, cols, parts=P):
            return ctx.enter_context(nc.sbuf_tensor(name, [parts, cols], F32))

        def sem(name):
            return ctx.enter_context(nc.semaphore(name))

        bank = [ctx.enter_context(nc.psum_tensor(f"bank{i}", [P, 512], F32)) for i in range(8)]

        kc = sb("kc", K_ALL)
        ident = kc[:, K_ID:K_ID + P]
        region_c = sb("region_c", PJ * IMG * QC)
        PT = region_c[:, :].rearrange("p (j b q) -> p j b q", j=PJ, b=IMG)
        xnTd = region_c[:, 0:2 * TOK].rearrange("p (t s) -> p t s", s=2)
        gate = region_c[:, 2 * TOK:3 * TOK]
        sp = region_c[:, 3 * TOK:4 * TOK]
        region_d = sb("region_d", 2 * 2 * ALL)
        QP = region_d[:, 0:PJ * TOK].rearrange("p (j b q) -> p j b q", j=PJ, b=IMG)
        QPf = region_d[:, 0:PJ * TOK].rearrange("p (j t) -> p j t", j=PJ)
        HB = region_d[:, :].rearrange("p (u s t) -> p u s t", u=2, s=2)
        pc_rep = region_d[:, 0:TOK].rearrange("p (r h d) -> p r h d", r=PAIRS, h=H)
        wprep = region_d[:, 0:1024].rearrange("p (w i) -> p w i", w=4)
        ei = region_d[:, 1024:1536]
        ei_root = region_d[:, 1536:2048]
        ei_sign = region_d[:, 2048:2560]
        wn = region_d[:, 2560:3072].rearrange("p (w i) -> p w i", w=2)
        rvd = region_d[:, 3072:3072 + QC * HD].rearrange("p (q d) -> p q d", q=QC)
        QT = sb("QT", ALL)
        xn2T = QT
        KT = sb("KT", NT * P)
        acc = KT[:, :].rearrange("p (t c) -> p t c", t=NT)
        region_e = sb("region_e", 4 * 520)
        xi = region_e
        tc_ = region_e
        LR = region_e[0:E, 0:ALL]
        SP = [region_e[:, 520 * i:520 * i + 520] for i in range(4)]
        h0 = sb("h0", TOK)
        xnT = sb("xnT", TOK)
        OT = xnT
        OTc = sb("OTc", IMG)
        vbd = sb("vbd", IMG * C)
        VBD = vbd[:, :].rearrange("p (b c) -> p b c", b=IMG)
        RVBD = sb("RVBD", QC * 32)
        RV = RVBD[:, :].rearrange("p (q s d) -> p q s d", q=QC, s=2)
        stb = sb("stb", 1024)
        ST = [stb[:, 0:512], stb[:, 512:1024]]
        tmpx = sb("tmpx", 512)
        misc = sb("misc", M_ALL)
        W3T = misc[:, M_W3:M_W3 + C]
        WrT = misc[:, M_WR:M_WR + E]
        relkT = misc[:, M_RK:M_RK + 129]
        relvT = misc[:, M_RV:M_RV + 65]
        xcT = misc[:, M_XC:M_XC + 1]
        relk_bd = sb("relk_bd", 258)
        RKB = relk_bd[:, :].rearrange("p (r s) -> p r s", s=2)
        wnT = sb("wnT", 512)
        WnT = wnT[:, :].rearrange("p (w r o) -> p w r o", w=2, r=2)
        w3 = sb("w3", C)
        wqkvo = sb("wqkvo", 4 * C)
        wq, wk, wv, wo = (wqkvo[:, i * C:(i + 1) * C] for i in range(4))
        rows = sb("rows", P)
        vecs = sb("vecs", NVEC)
        rel_rows = sb("rel_rows", 3 * C)
        wr = sb("wr", C)
        posb = sb("posb", C)
        bob = sb("bob", C)
        brb = sb("brb", E)
        b2s = sb("b2s", C)
        clsr = sb("clsr", C)
        clsn = sb("clsn", C)
        eo = sb("eo", 8)
        nb = sb("nb", 4)
        stats = sb("stats", NT * 6)
        mv = sb("mv", NT * 2)
        ve = sb("ve", NT)
        rstd = sb("rstd", NT)
        mhalf = sb("mhalf", 4)
        clsv = sb("clsv", 8)
        kcq = sb("kcq", NPATCH)
        vcq = sb("vcq", NPATCH)
        Sc = sb("Sc", PAIRS * H)
        Sct = sb("Sct", PAIRS * H)
        cx = sb("cx", 2 * QC)
        p0d = sb("p0d", 4 * NPATCH)
        sml = sb("sml", 16)
        p0x = sb("p0x", IMG)
        ptt = sb("ptt", NPATCH)
        top = sb("top", 2 * H)
        ntop = sb("ntop", 2 * H)
        esum = sb("esum", 2 * H)
        rsum = sb("rsum", 2 * H)
        nSc = sb("nSc", PAIRS * H)
        PcA = sb("PcA", PAIRS * H)
        lg = sb("lg", NT * E)
        rt = sb("rt", 4 * NT * E)
        rs_ = sb("rs_", 2 * NT)
        comb = sb("comb", NT * E)
        combT = vbd

        early = ExitStack()
        region_a = early.enter_context(nc.sbuf_tensor("region_a", [P, 8192], F32))
        xraw = region_a[:, 0:4096].rearrange("p (s n) -> p s n", s=2)
        xperm = region_a[:, 4096:8192]
        A2 = region_a[:, :].rearrange("p (j b q) -> p j b q", j=PJ, b=IMG)
        region_b = early.enter_context(nc.sbuf_tensor("region_b", [P, 4096], F32))
        xT = region_b[:, :].rearrange("p (r t) -> p r t", r=2)
        KM = region_b[:, :].rearrange("p (t s) -> p t s", s=2)
        early.close()
        w1_sb = sb("w1_sb", E * FH)
        w2_all = sb("w2_all", E * 2 * C)
        w2_sb = w2_all[:, :].rearrange("p (e s d) -> p e s d", e=E, s=2)
        w1_hi, w1_lo, x_hi, x_lo = (ctx.enter_context(nc.sbuf_tensor(n, [P, w], F32R)) for n, w in (
            ("w1_hi", E * FH), ("w1_lo", E * FH), ("x_hi", ALL), ("x_lo", ALL)))

        names = """d_const d_rows d_bias d_w1 d_w2 d_x0 d_x1 d_x2 d_small d_rel d_rvd d_attn d_ffn d_fw1 d_out w1hi_ok w1_split
        xlo_ok xloD_ok xhi_ok vec_ps vecs_ok eo_act ei_act wn_ok wnT_ps wnT_okA wnT_ok cls_n misc_ps misc_ok nb_ok d_w0
        d_cls d_w3 xperm_ok xT_ps xT_evA xT_evD g_ps gate_ok tmin_ok tanh_ok m_ok in_ps xi_ok y_ps h0_ok ve_ok
        rstd_ok xn_ok xnT_ps xnT_ok xnTd_ok q_ps k_ps v_ps QT_ok KT_ok QP_ok KM_ok VBD_ok cls_ps clsv_ok a2_ps
        a2_evA a2_evD kcq_ok tc_ok ua_ok uc_ok tcT_ps tc_red c0_ps cx_ok cexp_ok p0d_ok p0T_ps ptc_ok pc_m ve_c
        rstd_c s1_ps st_ok s_ps top_ok dc_ok e_ok r_ok half_ok pn_ok pc_ok pt_ps pt_ok w1_ps w1_ev rep_ok pcT_ps pcx_ok
        w2_ps o_ok oc_ok op_ps opc_ps h1_ok h1a_ok h1c_ok ve2_ok rstd2_ok xn2_ok x2T_ps x2T_ok lr_ps lr_ok lg_ps
        lg_ok lexp_ok comb_ok cT_ps cT_ok base_ps acc_ok h_ps gelu_ok y2_ps h0o_ok relkb_ok QP0_ok dve_c dve_m act_c
        pool_c""".split()
        S = {n: sem(n) for n in names}

        def chain(eng, name):
            n = [0]

            def link(ins):
                n[0] += 1
                ins.then_inc(S[name], 1)
                eng.wait_ge(S[name], n[0])
            return link

        def h_bank(i):
            return i % 4 if i < 12 else 5 + i - 12 if i < 14 else (i - 2) % 4

        def h_before(i):
            return i - 3 if i < 12 else 0 if i < 14 else i - 5 if i < 18 else i - 3

        def out_base(g):
            return 2 * g

        def out_expert(e, g):
            return 2 * g + 1 if e == 0 else 5 + 5 * e + g

        def out_bank(u):
            return 4 + (u + 1) % 4

        block = ctx.enter_context(nc.Block())
        relk8 = rel_k.unsqueeze(1)
        relv8 = rel_v.unsqueeze(1)

        @block.sync
        def _(sp_):
            xv = x.rearrange("(s b) o (i r) w -> s (b o i) (r w)", s=2, i=8)
            for half in range(2):
                sp_.dma_start(xraw[:, 0, half * 1024:(half + 1) * 1024],
                              xv[0, :, half * 1024:(half + 1) * 1024]).then_inc(S[f"d_x{half}"], 16)
            for r, b in ((V_EO1, eps_out1), (V_EO2, eps_out2), (V_B1, W1_b), (V_SB1, W1_sb), (V_B2, W2_b),
                         (V_SB2, W2_sb)):
                sp_.dma_start(rows[r:r + 1, :], b.unsqueeze(0)).then_inc(S["d_rows"], 16)
            for i, w in enumerate((W2_w, W2_sw)):
                sp_.dma_start(wprep[:, 2 + i, :], w).then_inc(S["d_w2"], 16)
            sp_.dma_start(xraw[:, 1, :], xv[1]).then_inc(S["d_x2"], 16)
            for i, w in enumerate((Wq, Wk, Wv, Wo)):
                sp_.dma_start(wqkvo[:, i * C:(i + 1) * C], w).then_inc(S["d_attn"], 16)
            for par in range(2):
                src = bass.AP(tensor=rel_v.tensor, offset=rel_v.offset + 5 * HD, ap=[[HD, NPATCH], [1, QC * HD]])
                sp_.dma_start(region_d[par:P:2, 3072:3072 + QC * HD], src).then_inc(S["d_rvd"], 16)
            sp_.wait_ge(S["st_ok"], PAIRS)
            sp_.dma_start(w1_sb[:, :].rearrange("p (e h) -> p e h", e=E), fW1.rearrange("e d h -> d e h"))\
                .then_inc(S["d_fw1"], 16)
            sp_.dma_start(w2_sb, fW2.rearrange("e (s h) d -> h e s d", s=2)).then_inc(S["d_ffn"], 16)
            ov = out.rearrange("(r b) t c -> b t r c", b=2)
            for g in range(5):
                sp_.wait_ge(S["acc_ok"], 5 + 5 * (E - 1) + g + 1)
                if g < 4:
                    for b2 in range(2):
                        sp_.dma_start(ov[b2, 1:QC, 4 * g:4 * g + 4, :],
                                      acc[64 * b2:64 * b2 + 64, 4 * g:4 * g + 4, :]).then_inc(S["d_out"], 16)
                else:
                    sp_.dma_start(out[:, 0, :], acc[0:IMG, PAIRS, :]).then_inc(S["d_out"], 16)
            sp_.wait_ge(S["d_out"], 16 * 9)

        @block.gpsimd
        def _(pool):
            g = nc.gpsimd
            link = chain(pool, "pool_c")
            g.dma_start(rows[V_FB1:NVEC, :], fb1.rearrange("e (s h) -> (e s) h", s=2)).then_inc(S["d_bias"], 16)
            for r, b in ((V_BQ, bq), (V_BK, bk), (V_BV, bv)):
                g.dma_start(rows[r:r + 1, :], b.unsqueeze(0)).then_inc(S["d_bias"], 16)
            g.dma_start(clsr[0:IMG, :], cls_tok.rearrange("a b c -> (a b) c").to_broadcast([IMG, C]))\
                .then_inc(S["d_cls"], 16)
            g.dma_start(w3[:, :], W3_w).then_inc(S["d_w3"], 16)
            g.dma_start(rel_rows[:, 0:C].rearrange("p (h d) -> p h d", h=H),
                        relk8[4:132].to_broadcast([P, H, HD])).then_inc(S["d_rel"], 16)
            g.dma_start(rel_rows[0:1, C:2 * C].rearrange("p (h d) -> p h d", h=H),
                        relk8[132:133].to_broadcast([1, H, HD])).then_inc(S["d_rel"], 16)
            g.dma_start(rel_rows[0:65, 2 * C:3 * C].rearrange("p (h d) -> p h d", h=H),
                        relv8[4:69].to_broadcast([65, H, HD])).then_inc(S["d_rel"], 16)
            g.dma_start(wr[0:E, :], Wr).then_inc(S["d_rel"], 16)
            g.dma_start(posb[:, :], W3_b.unsqueeze(0).to_broadcast([P, C])).then_inc(S["d_small"], 16)
            g.dma_start(bob[:, :], bo.unsqueeze(0).to_broadcast([P, C])).then_inc(S["d_small"], 16)
            g.dma_start(brb[:, :], br.unsqueeze(0).to_broadcast([P, E])).then_inc(S["d_small"], 16)
            g.dma_start(b2s[0:E, :], fb2).then_inc(S["d_small"], 16)
            link(g.memset(mhalf[:, :], -0.5))
            pool.wait_ge(S["ve_c"], 1)
            g.tensor_tensor(clsn[0:1, 2:3], clsn[0:1, 1:2], mhalf[0:1, 0:1], ALU.pow).then_inc(S["rstd_c"], 1)
            bb = [P, BLK // NPATCH, NPATCH]

            def gated(n):
                pool.wait_ge(S["tanh_ok"], n + 1)
                b = slice(n * BLK, (n + 1) * BLK)
                g.tensor_tensor(gate[:, b], gate[:, b], sp[:, b], ALU.mult).then_inc(S["m_ok"], 1)

            def deviation(n):
                pool.wait_ge(S["ve_ok"], n + 1)
                g.tensor_tensor(rstd[:, n * TPB:(n + 1) * TPB], ve[:, n * TPB:(n + 1) * TPB], mhalf[:, :],
                                ALU.pow).then_inc(S["rstd_ok"], 1)

            def masked_queries(n):
                b = slice(n * BLK, (n + 1) * BLK)
                pool.wait_ge(S["QT_ok"], n + 1)
                g.tensor_tensor(QPf[:, 0, b], QT[:, b], kc[:, K_PM:K_PM + 1].to_broadcast([P, BLK]), ALU.mult)\
                    .then_inc(S["QP0_ok"], 1)

            def class_key(n):
                b = slice(n * BLK, (n + 1) * BLK)
                if n == 0:
                    pool.wait_ge(S["kcq_ok"], 1)
                g.tensor_tensor(tc_[:, b].rearrange("p (b q) -> p b q", q=NPATCH),
                                QT[:, b].rearrange("p (b q) -> p b q", q=NPATCH),
                                kcq[:, :].unsqueeze(1).to_broadcast(bb), ALU.mult).then_inc(S["tc_ok"], 1)

            gated(0)
            gated(1)
            deviation(0)
            gated(2)
            gated(3)
            deviation(1)
            deviation(2)
            deviation(3)
            masked_queries(0)
            class_key(0)
            masked_queries(1)
            class_key(1)
            masked_queries(2)
            masked_queries(3)
            class_key(2)
            class_key(3)
            for n in range(NBLK):
                b = slice(n * BLK, (n + 1) * BLK)
                pool.wait_ge(S["KM_ok"], n + 1)
                kt = KT[:, b].rearrange("p (b q) -> p b q", q=NPATCH)
                g.tensor_tensor(kt, kt, relkT[:, 65:129].unsqueeze(1).to_broadcast(bb), ALU.add)\
                    .then_inc(S["ua_ok"], 1)
            pool.wait_ge(S["d_small"], 64)
            for n in range(NBLK):
                hv = h0[:, n * BLK:(n + 1) * BLK].rearrange("p (t c) -> p t c", c=C)
                ins = g.tensor_tensor(hv, hv, bob[:, :].unsqueeze(1).to_broadcast([P, TPB, C]), ALU.add)
            ins.then_inc(S["h0o_ok"], 1)
            for p in range(PAIRS):
                pool.wait_ge(S["r_ok"], p + 1)
                e_, r_ = SP[p % 4], rsum[:, 8 * (p % 2):8 * (p % 2) + 8]
                js = PJ if p < PAIRS - 1 else PJ // 2
                ev = e_[:, 0:P * js].rearrange("p (j k s) -> p j k s", j=js, s=2)
                rv = r_[:, 0:2 * js].rearrange("p (j s) -> p j s", j=js).unsqueeze(2).to_broadcast([P, js, NPATCH, 2])
                g.tensor_tensor(ev, ev, rv, ALU.mult).then_inc(S["pn_ok"], 1)
                g.tensor_tensor(PcA[:, p * H:(p + 1) * H], e_[:, 512:520], r_, ALU.mult).then_inc(S["pc_ok"], 1)
            pool.wait_ge(S["w1hi_ok"], 1)
            g.tensor_tensor(w1_lo[:, :], w1_sb[:, :], w1_hi[:, :].bitcast(F32), ALU.subtract).then_inc(S["w1_split"], 1)

            def low(n):
                b = slice(n * BLK, n * BLK + (BLK if n < NBLK else IMG))
                pool.wait_ge(S["xhi_ok"], n + 1)
                pool.wait_ge(S["x2T_ok"], n + 1)
                g.tensor_tensor(x_lo[:, b], xn2T[:, b], x_hi[:, b].bitcast(F32), ALU.subtract).then_inc(S["xlo_ok"], 1)

            def deviation2(n):
                m, w = (P, TPB) if n < NBLK else (IMG, 1)
                pool.wait_ge(S["ve2_ok"], n + 1)
                g.tensor_tensor(rstd[0:m, n * TPB:n * TPB + w], ve[0:m, n * TPB:n * TPB + w], mhalf[0:m, 0:w],
                                ALU.pow).then_inc(S["rstd2_ok"], 1)

            deviation2(0)
            deviation2(1)
            deviation2(2)
            low(0)
            deviation2(3)
            low(1)
            deviation2(4)

        @block.scalar
        def _(act):
            a = nc.scalar
            link = chain(act, "act_c")
            a.dma_start(kc[:, :], consts).then_inc(S["d_const"], 16)
            for i, v in enumerate((eps_in1, eps_in2)):
                a.dma_start(ei[:, i * PIX:(i + 1) * PIX], v.unsqueeze(0).to_broadcast([P, PIX]))\
                    .then_inc(S["d_w1"], 16)
            def evac_xT(t):
                act.wait_ge(S["xT_ps"], t + 1)
                s, r, jh = t // 4, (t // 2) % 2, t % 2
                dst = xT[:, r, s * 1024:(s + 1) * 1024].rearrange("p (m g j) -> p g m j", g=2, j=4)[:, jh]
                a.activation(dst, bank[t % 2][:, :].rearrange("p (j m) -> p m j", j=4), ACT.Copy)\
                    .then_inc(S["xT_evA"], 1)

            def softplus(n):
                b = slice(n * BLK, (n + 1) * BLK)
                if n == 0:
                    act.wait_ge(S["nb_ok"], 1)
                act.wait_ge(S["tmin_ok"], n + 1)
                a.activation(gate[:, b], bank[4 + n % 2][:, :], ACT.Identity, bias=nb[:, 0:1])\
                    .then_inc(S["gate_ok"], 1)
                link(a.activation(sp[:, b], sp[:, b], ACT.Exp))
                link(a.activation(sp[:, b], sp[:, b], ACT.Ln, bias=1.0))

            def tanh(n):
                b = slice(n * BLK, (n + 1) * BLK)
                a.activation(sp[:, b], sp[:, b], ACT.Tanh).then_inc(S["tanh_ok"], 1)

            def root_sign(i):
                b = slice(i * PIX, (i + 1) * PIX)
                link(a.activation(ei_root[:, b], ei[:, b], ACT.Abs))
                a.activation(ei_root[:, b], ei_root[:, b], ACT.Sqrt).then_inc(S["ei_act"], 1)
                a.activation(ei_sign[:, b], ei[:, b], ACT.Sign).then_inc(S["ei_act"], 1)

            a.preload_act_table_set("sqrt_and_others")
            for i, w in enumerate((W1_w, W1_sw)):
                a.dma_start(wprep[:, i, :], w).then_inc(S["d_w0"], 16)
            act.wait_ge(S["d_w1"], 32)
            root_sign(0)
            act.wait_ge(S["vecs_ok"], 1)
            link(a.activation(eo[:, 0:2], vecs[:, V_EO1:V_EO2 + 1:3], ACT.Abs))
            a.activation(eo[:, 2:4], eo[:, 0:2], ACT.Sqrt).then_inc(S["eo_act"], 1)
            a.activation(eo[:, 4:6], vecs[:, V_EO1:V_EO2 + 1:3], ACT.Sign).then_inc(S["eo_act"], 1)
            evac_xT(0)
            root_sign(1)
            evac_xT(2)
            act.wait_ge(S["wnT_ps"], 1)
            a.activation(wnT[:, 0:256], bank[3][:, 0:256], ACT.Copy).then_inc(S["wnT_okA"], 1)
            a.preload_act_table_set("natural_log_exp_and_others")
            evac_xT(4)
            softplus(0)
            evac_xT(6)
            softplus(1)
            a.preload_act_table_set("exp_and_others")
            tanh(0)
            tanh(1)
            act.wait_ge(S["misc_ps"], 1)
            a.activation(misc[:, :], bank[2][:, 128:128 + M_ALL], ACT.Copy).then_inc(S["misc_ok"], 1)
            a.preload_act_table_set("natural_log_exp_and_others")
            softplus(2)
            softplus(3)
            a.preload_act_table_set("exp_and_others")
            tanh(2)
            tanh(3)

            def evac_xn(n):
                b = slice(n * BLK, (n + 1) * BLK)
                act.wait_ge(S["xnT_ps"], n + 1)
                a.activation(xnT[:, b], bank[2 + n % 2][:, :], ACT.Copy).then_inc(S["xnT_ok"], 1)
                a.activation(xnTd[:, b, :], bank[2 + n % 2][:, :].unsqueeze(2).to_broadcast([P, BLK, 2]),
                             ACT.Copy).then_inc(S["xnTd_ok"], 1)

            def evac_qk(n):
                b = slice(n * BLK, (n + 1) * BLK)
                act.wait_ge(S["q_ps"], n + 1)
                a.activation(QT[:, b], bank[6][:, :], ACT.Identity, bias=vecs[:, V_BQ:V_BQ + 1])\
                    .then_inc(S["QT_ok"], 1)
                act.wait_ge(S["k_ps"], n + 1)
                a.activation(KT[:, b], bank[7][:, :], ACT.Identity, bias=vecs[:, V_BK:V_BK + 1])\
                    .then_inc(S["KT_ok"], 1)

            def evac_v(n):
                for half in range(2):
                    u = 2 * n + half
                    act.wait_ge(S["v_ps"], u + 1)
                    for s in range(2):
                        last = a.activation(
                            VBD[:, 4 * u:4 * u + 4, :].rearrange("p b (j s d) -> p (b j) s d", s=2, d=HD)[:, :, s],
                            bank[half][:, :].rearrange("p (m s d) -> p m s d", s=2, d=HD)[:, :, s],
                            ACT.Copy, scale=kc[:, K_KP + s:K_KP + s + 1])
                    last.then_inc(S["VBD_ok"], 1)

            for n in range(NBLK):
                evac_xn(n)
                if n:
                    evac_v(n - 1)
                evac_qk(n)
            evac_v(3)
            act.wait_ge(S["clsv_ok"], 1)
            for i in range(8):
                act.wait_ge(S["a2_ps"], 2 * i + 1)
                a.activation(A2[:, :, :, 8 * i:8 * i + 4].rearrange("p j b q -> p (j b) q"),
                             bank[(2 * i + 2) % 4][:, :].rearrange("p (q m) -> p m q", q=4), ACT.Copy)\
                    .then_inc(S["a2_evA"], 1)
                if i % 2 == 1:
                    n = i // 2
                    b = slice(n * BLK, (n + 1) * BLK)
                    act.wait_ge(S["ua_ok"], n + 1)
                    a.activation(KT[:, b], KT[:, b], ACT.Copy, scale=clsv[:, 0:1]).then_inc(S["uc_ok"], 1)
            for i in range(1, PAIRS + 1):
                if i == 4:
                    act.wait_ge(S["cx_ok"], 1)
                    a.activation(cx[:, :], cx[:, :], ACT.Exp, scale=SCALE).then_inc(S["cexp_ok"], 1)
                p = i - 1
                act.wait_ge(S["top_ok"], p + 1)
                if p >= 4:
                    act.wait_ge(S["pt_ps"], p - 3)
                    act.wait_ge(S["pc_ok"], p - 3)
                if p >= 2:
                    act.wait_ge(S["r_ok"], p - 1)
                o = 8 * (p % 2)
                src = bank[2 + p % 2][:, :].rearrange("p (j k s) -> p j s k", j=PJ, s=2)
                dst = SP[p % 4][:, 0:512].rearrange("p (j k s) -> p j s k", j=PJ, s=2)
                for h in range(H):
                    a.activation(dst[:, h // 2, h % 2], src[:, h // 2, h % 2], ACT.Exp, scale=SCALE,
                                 bias=ntop[:, o + h:o + h + 1], accum_out=esum[:, o + h:o + h + 1])
                act.wait_ge(S["dc_ok"], p + 1)
                a.activation(SP[p % 4][:, 512:520], SP[p % 4][:, 512:520], ACT.Exp).then_inc(S["e_ok"], 1)
            a.preload_act_table_set("gelu_and_others")
            act.wait_ge(S["d_fw1"], 16)
            a.activation(w1_hi[:, :], w1_sb[:, :], ACT.Copy).then_inc(S["w1hi_ok"], 1)

            def evac_logits(n):
                m = BLK if n < NBLK else IMG
                act.wait_ge(S["lr_ps"], n + 1)
                a.activation(LR[:, n * BLK:n * BLK + m], bank[5 + n % 2][0:E, 0:m], ACT.Copy).then_inc(S["lr_ok"], 1)

            def evac_x2(n):
                m = BLK if n < NBLK else IMG
                act.wait_ge(S["x2T_ps"], n + 1)
                a.activation(x_hi[:, n * BLK:n * BLK + m], bank[7][:, 0:m], ACT.Copy).then_inc(S["xhi_ok"], 1)
                a.activation(xn2T[:, n * BLK:n * BLK + m], bank[7][:, 0:m], ACT.Copy).then_inc(S["x2T_ok"], 1)

            def gelu(i):
                e, s, blk = i // 10, i % 2, (i // 2) % 5
                act.wait_ge(S["h_ps"], i + 1)
                if e >= 2 and i % 10 == 0:
                    act.wait_ge(S["y2_ps"], 5 * (e - 1))
                v = V_FB1 + 2 * e + s
                a.activation(HB[:, e % 2, s, blk * FB:(blk + 1) * FB], bank[h_bank(i)][:, 0:FB], ACT.Gelu,
                             bias=vecs[:, v:v + 1]).then_inc(S["gelu_ok"], 1)

            for n in (2, 3):
                act.wait_ge(S["op_ps"], n + 1)
                a.activation(KT[:, n * BLK:(n + 1) * BLK], bank[OP_BANKS[n]][:, :], ACT.Copy).then_inc(S["h1a_ok"], 1)
            for n in range(5):
                evac_x2(n)
                if n:
                    evac_logits(n - 1)
                    if n == 4:
                        evac_logits(4)
                    gelu(2 * n - 2)
                    gelu(2 * n - 1)
            act.wait_ge(S["lg_ok"], 1)
            a.activation(lg[:, :], lg[:, :], ACT.Exp).then_inc(S["lexp_ok"], 1)
            a.preload_act_table_set("gelu_and_others")
            for i in range(8, 20):
                gelu(i)
            for n in range(5):
                m = BLK if n < NBLK else IMG
                act.wait_ge(S["cT_ps"], n + 1)
                a.activation(combT[0:E, n * BLK:n * BLK + m], bank[4 + n % 4][0:E, 0:m], ACT.Copy)\
                    .then_inc(S["cT_ok"], 1)
            for i in range(20, 10 * E):
                gelu(i)

        @block.vector
        def _(dve):
            v = nc.vector
            link = chain(dve, "dve_c")

            def mark(ins):
                marks[0] += 1
                ins.then_inc(S["dve_m"], 1)
                return marks[0]

            def after(n):
                dve.wait_ge(S["dve_m"], n)
            marks = [0]
            def permute(s, half):
                dve.wait_ge(S[f"d_x{half if s == 0 else 2}"], 16)
                o = (2 * s + half) * 1024
                v.tensor_copy(xperm[:, o:o + 1024].rearrange("p (j r c) -> p r j c", j=8, r=8),
                              xraw[:, s, half * 1024:(half + 1) * 1024].rearrange("p (r j c) -> p r j c", r=8, j=8))\
                    .then_inc(S["xperm_ok"], 1)

            def evac_xT(t):
                dve.wait_ge(S["xT_ps"], t + 1)
                s, r, jh = t // 4, (t // 2) % 2, t % 2
                dst = xT[:, r, s * 1024:(s + 1) * 1024].rearrange("p (m g j) -> p g m j", g=2, j=4)[:, jh]
                v.tensor_copy(dst, bank[t % 2][:, :].rearrange("p (j m) -> p m j", j=4)).then_inc(S["xT_evD"], 1)

            def clamp(n):
                b = slice(n * BLK, (n + 1) * BLK)
                dve.wait_ge(S["g_ps"], n + 1)
                v.tensor_scalar(sp[:, b], bank[4 + n % 2][:, :], nb[:, 0:1], 30.0, ALU.add, ALU.min).then_inc(S["tmin_ok"], 1)

            permute(0, 0)
            permute(0, 1)
            dve.wait_ge(S["vec_ps"], 1)
            v.tensor_copy(vecs[:, :], bank[2][:, 0:NVEC]).then_inc(S["vecs_ok"], 1)
            evac_xT(1)
            dve.wait_ge(S["ei_act"], 2)
            v.tensor_tensor(ei[:, 0:PIX], ei_root[:, 0:PIX], ei_sign[:, 0:PIX], ALU.mult)
            dve.wait_ge(S["eo_act"], 2)
            link(v.tensor_tensor(eo[:, 6:8], eo[:, 2:4], eo[:, 4:6], ALU.mult))
            for w in range(2):
                dve.wait_ge(S["d_w2" if w else "d_w0"], 32)
                if w == 1:
                    evac_xT(3)
                    dve.wait_ge(S["ei_act"], 4)
                    link(v.tensor_tensor(ei[:, PIX:2 * PIX], ei_root[:, PIX:2 * PIX], ei_sign[:, PIX:2 * PIX],
                                         ALU.mult))
                link(v.scalar_tensor_tensor(wn[:, w, :], wprep[:, 2 * w + 1, :], eo[:, 6 + w:7 + w],
                                            ei[:, w * PIX:(w + 1) * PIX], op0=ALU.mult, op1=ALU.mult))
                v.tensor_tensor(wn[:, w, :], wn[:, w, :], wprep[:, 2 * w, :], ALU.add).then_inc(S["wn_ok"], 1)
            link(v.tensor_tensor(nb[:, 2:4], vecs[:, V_SB1:V_SB2 + 1:3], eo[:, 6:8], ALU.mult))
            v.tensor_tensor(nb[:, 0:2], nb[:, 2:4], vecs[:, V_B1:V_B2 + 1:3], ALU.add).then_inc(S["nb_ok"], 1)
            permute(1, 0)
            permute(1, 1)
            dve.wait_ge(S["d_cls"], 16)
            link(v.bn_stats(stats[0:1, 0:6], clsr[0:1, :]))
            link(v.bn_aggr(mv[0:1, 0:2], stats[0:1, 0:6]))
            v.tensor_scalar(clsn[0:1, 1:2], mv[0:1, 1:2], EPS, None, ALU.add).then_inc(S["ve_c"], 1)
            clamp(0)
            evac_xT(5)
            dve.wait_ge(S["wnT_ps"], 2)
            v.tensor_copy(wnT[:, 256:512], bank[3][:, 256:512]).then_inc(S["wnT_ok"], 1)
            dve.wait_ge(S["rstd_c"], 1)
            link(v.tensor_copy(sml[0:1, 0:1], clsn[0:1, 2:3]))
            v.tensor_scalar(clsn[0:1, :], clsr[0:1, :], mv[0:1, 0:1], sml[0:1, 0:1], ALU.subtract, ALU.mult)\
                .then_inc(S["cls_n"], 1)
            clamp(1)
            evac_xT(7)
            dve.wait_ge(S["d_rvd"], 32)
            for s in range(2):
                v.tensor_scalar(RV[:, :, s, :], rvd, kc[:, K_KP + s:K_KP + s + 1], None, ALU.mult)
                if s == 0:
                    clamp(2)
            dve.wait_ge(S["d_small"], 64)
            link(v.tensor_tensor(posb[:, :], posb[:, :], kc[:, K_PE:K_PE + C], ALU.add))

            def inner(n):
                b = slice(n * BLK, (n + 1) * BLK)
                dve.wait_ge(S["in_ps"], n + 1)
                dve.wait_ge(S["m_ok"], n + 1)
                v.scalar_tensor_tensor(xi[:, b], bank[IN_BANKS[n]][:, :], nb[:, 1:2], gate[:, b], op0=ALU.add,
                                       op1=ALU.mult).then_inc(S["xi_ok"], 1)

            def embed(n):
                b = slice(n * BLK, (n + 1) * BLK)
                dve.wait_ge(S["y_ps"], n + 1)
                v.tensor_tensor(h0[:, b].rearrange("p (t c) -> p t c", c=C),
                                bank[Y_BANKS[n]][:, :].rearrange("p (t c) -> p t c", c=C),
                                posb[:, :].unsqueeze(1).to_broadcast([P, TPB, C]), ALU.add)\
                    .then_inc(S["h0_ok"], 1)
                dve.wait_ge(S["h0_ok"], n + 1)
                moments(h0, n, TPB, P, "ve_ok")

            def moments(src, n, w, m, done):
                for t in range(n * TPB, n * TPB + w):
                    last = v.bn_stats(stats[0:m, 6 * t:6 * t + 6], src[0:m, t * C:(t + 1) * C])
                link(last)
                for t in range(n * TPB, n * TPB + w):
                    last = v.bn_aggr(mv[0:m, 2 * t:2 * t + 2], stats[0:m, 6 * t:6 * t + 6])
                link(last)
                v.tensor_scalar(ve[0:m, n * TPB:n * TPB + w],
                                mv[0:m, 2 * n * TPB:2 * (n * TPB + w)].rearrange("p (t s) -> p t s", s=2)[:, :, 1],
                                EPS, None, ALU.add).then_inc(S[done], 1)

            def normalise(src, n, w, m, wait, done, read, count):
                dve.wait_ge(S[wait], n + 1)
                if count > 0:
                    dve.wait_ge(S[read], count)
                for i in range(w):
                    t = n * TPB + i
                    last = v.tensor_scalar(ST[n % 2][0:m, i * C:(i + 1) * C], src[0:m, t * C:(t + 1) * C],
                                           mv[0:m, 2 * t:2 * t + 1], rstd[0:m, t:t + 1], ALU.subtract, ALU.mult)
                last.then_inc(S[done], 1)

            def masked_queries(n):
                b = slice(n * BLK, (n + 1) * BLK)
                dve.wait_ge(S["QT_ok"], n + 1)
                for j in range(1, PJ):
                    last = v.tensor_scalar(QPf[:, j, b], QT[:, b], kc[:, K_PM + j:K_PM + j + 1], None, ALU.mult)
                last.then_inc(S["QP_ok"], 1)

            def masked_keys(n):
                b = slice(n * BLK, (n + 1) * BLK)
                dve.wait_ge(S["KT_ok"], n + 1)
                for s in range(2):
                    last = v.tensor_scalar(KM[:, b, s], KT[:, b], kc[:, K_HP + s:K_HP + s + 1], None, ALU.mult)
                last.then_inc(S["KM_ok"], 1)

            def norm1(n):
                normalise(h0, n, TPB, P, "rstd_ok", "xn_ok", "xnT_ps", n - 1)

            inner(0)
            clamp(3)
            dve.wait_ge(S["misc_ok"], 1)
            for s in range(2):
                v.tensor_scalar(RKB[:, :, s], relkT, kc[:, K_HP + s:K_HP + s + 1], None, ALU.mult)\
                    .then_inc(S["relkb_ok"], 1)
            dve.wait_ge(S["cls_ps"], 1)
            link(v.tensor_tensor(clsv[:, 0:2], bank[2][:, CLS:CLS + 2], vecs[:, V_BQ:V_BK + 1], ALU.add))
            link(v.tensor_copy(clsv[:, 2:3], bank[2][:, CLS + 2:CLS + 3]))
            link(v.tensor_tensor(clsv[:, 3:4], clsv[:, 1:2], relkT[:, 64:65], ALU.add))
            link(v.tensor_tensor(clsv[:, 4:5], clsv[:, 3:4], clsv[:, 0:1], ALU.mult))
            v.tensor_tensor(clsv[:, 5:6], clsv[:, 2:3], relvT[:, 64:65], ALU.add).then_inc(S["clsv_ok"], 1)
            v.tensor_scalar(kcq[:, :], misc[:, M_RK + 63:M_RK - 1:-1], clsv[:, 1:2], None, ALU.add)\
                .then_inc(S["kcq_ok"], 1)
            v.tensor_scalar(vcq[:, :], misc[:, M_RV + 63:M_RV - 1:-1], clsv[:, 2:3], None, ALU.add)

            embed(0)
            inner(1)
            norm1(0)
            inner(2)
            embed(1)
            inner(3)
            norm1(1)
            embed(2)
            masked_queries(0)
            norm1(2)
            embed(3)
            masked_queries(1)
            norm1(3)
            masked_queries(2)
            masked_queries(3)

            def red(g):
                dve.wait_ge(S["tcT_ps"], g + 1)
                dst = (Sc if g < 4 else Sct)[:, (g % 4) * 32:(g % 4) * 32 + 32]
                v.tensor_reduce(dst, bank[4 + g % 4][:, :].rearrange("p (m d) -> p m d", d=HD), axis=AX_X,
                                op=ALU.add).then_inc(S["tc_red"], 1)

            for i in range(8):
                if i < 4:
                    masked_keys(i)
                dve.wait_ge(S["a2_ps"], 2 * i + 2)
                v.tensor_copy(A2[:, :, :, 8 * i + 4:8 * i + 8].rearrange("p j b q -> p (j b) q"),
                              bank[(2 * i + 3) % 4][:, :].rearrange("p (q m) -> p m q", q=4))\
                    .then_inc(S["a2_evD"], 1)
                if 4 <= i < 7:
                    red(i - 4)

            def add(p):
                dve.wait_ge(S["s1_ps"], p + 1)
                if p == 0:
                    dve.wait_ge(S["a2_evA"], 8)
                    dve.wait_ge(S["a2_evD"], 8)
                if p >= 2:
                    dve.wait_ge(S["s_ps"], p - 1)
                v.tensor_tensor(ST[p % 2].rearrange("p (j m) -> p j m", j=PJ),
                                bank[p % 2][:, :].rearrange("p (j m) -> p j m", j=PJ),
                                A2[:, :, 2 * p:2 * p + 2, :].rearrange("p j b q -> p j (b q)"), ALU.add)\
                    .then_inc(S["st_ok"], 1)

            def softmax(p, r, new):
                if r is not None:
                    q = slice(8 * (r % 2), 8 * (r % 2) + 8)
                    dve.wait_ge(S["e_ok"], r + 1)
                    total = mark(v.tensor_tensor(esum[:, q], esum[:, q], SP[r % 4][:, 512:520], ALU.add))
                if p is not None:
                    o = slice(8 * (p % 2), 8 * (p % 2) + 8)
                    dve.wait_ge(S["s_ps"], p + 1)
                    most = mark(v.tensor_reduce(top[:, o].rearrange("p (j s) -> p j s", j=PJ),
                                                bank[2 + p % 2][:, :].rearrange("p (j k s) -> p j s k", j=PJ, s=2),
                                                axis=AX_X, op=ALU.max))
                if r is not None:
                    after(total)
                    if r >= 2:
                        dve.wait_ge(S["pc_ok"], r - 1)
                    v.reciprocal(rsum[:, q], esum[:, q]).then_inc(S["r_ok"], 1)
                if p is not None:
                    after(most)
                    if p >= 2:
                        dve.wait_ge(S["e_ok"], p - 1)
                    v.scalar_tensor_tensor(ntop[:, o], top[:, o], -SCALE, nSc[:, p * H:(p + 1) * H], op0=ALU.mult,
                                           op1=ALU.min).then_inc(S["top_ok"], 1)
                if new is not None:
                    add(new)
                if p is not None:
                    dve.wait_ge(S["top_ok"], p + 1)
                    if p >= 4:
                        dve.wait_ge(S["pc_ok"], p - 3)
                    v.tensor_tensor(SP[p % 4][:, 512:520], ntop[:, o], nSc[:, p * H:(p + 1) * H], ALU.subtract)\
                        .then_inc(S["dc_ok"], 1)

            def probs(p):
                dve.wait_ge(S["pt_ps"], p + 1)
                v.tensor_copy(PT[:, :, 2 * p:2 * p + 2, 0:NPATCH],
                              bank[4 + p % 2][:, :].rearrange("p (j b q) -> p j b q", j=PJ, b=2)).then_inc(S["pt_ok"], 1)

            cv = cx[:, :].rearrange("p (b k) -> p b k", b=2)
            m2, c00, r2 = sml[:, 2:4], sml[:, 4:5], sml[:, 6:8]

            def class_scores():
                dve.wait_ge(S["c0_ps"], 1)
                cps = bank[7][:, 0:P].rearrange("p (b k) -> p b k", b=2)
                v.tensor_copy(c00, bank[7][:, P:P + 1])
                link(v.tensor_reduce(m2, cps, axis=AX_X, op=ALU.max))
                link(v.tensor_scalar(m2, m2, c00, None, ALU.max))
                v.tensor_tensor(cv[:, :, 0:NPATCH], cps, m2.unsqueeze(2).to_broadcast([P, 2, NPATCH]), ALU.subtract)
                v.tensor_scalar(cv[:, :, NPATCH], m2, -1.0, c00, ALU.mult, ALU.add).then_inc(S["cx_ok"], 1)

            def class_probs():
                dve.wait_ge(S["cexp_ok"], 1)
                link(v.tensor_reduce(r2, cv, axis=AX_X, op=ALU.add))
                link(v.reciprocal(sml[:, 8:10], r2))
                v.tensor_tensor(p0d[:, :].rearrange("p (b k s) -> p b k s", b=2, s=2),
                                cv[:, :, 0:NPATCH].unsqueeze(3).to_broadcast([P, 2, NPATCH, 2]),
                                sml[:, 8:10].unsqueeze(2).unsqueeze(3).to_broadcast([P, 2, NPATCH, 2]), ALU.mult)
                link(v.tensor_tensor(sml[:, 10:12], cv[:, :, NPATCH], sml[:, 8:10], ALU.mult))
                v.tensor_tensor(p0x[:, :].rearrange("p (r b) -> p r b", b=2),
                                kc[:, K_PR:K_PR + PAIRS].unsqueeze(2).to_broadcast([P, PAIRS, 2]),
                                sml[:, 10:12].unsqueeze(1).to_broadcast([P, PAIRS, 2]), ALU.mult)\
                    .then_inc(S["p0d_ok"], 1)

            def class_turned():
                dve.wait_ge(S["p0T_ps"], 1)
                for b2 in range(2):
                    pv = bank[6][:, b2 * P:(b2 + 1) * P].rearrange("p (r j s) -> p r j s", r=PAIRS, j=PJ)
                    tv = ptt[:, :].rearrange("p (r j) -> p r j", j=PJ)
                    link(v.tensor_scalar(tv, pv[:, :, :, 1], kc[:, K_KP + 1:K_KP + 2], None, ALU.mult))
                    last = v.scalar_tensor_tensor(PT[:, :, b2:IMG:2, NPATCH].rearrange("p j r -> p r j"),
                                                  pv[:, :, :, 0], kc[:, K_KP:K_KP + 1], tv, op0=ALU.mult,
                                                  op1=ALU.add)
                    if b2 == 0:
                        link(last)
                last.then_inc(S["ptc_ok"], 1)

            add(0)
            red(3)
            dve.wait_ge(S["tc_red"], 4)
            link(v.tensor_scalar(nSc[:, :], Sc[:, :], -SCALE, None, ALU.mult))
            def outputs(u):
                dve.wait_ge(S["w1_ps"], u + 1)
                o = bank[6 + u % 2][:, 0:4 * QC].rearrange("p (b q) -> p b q", b=4)
                v.tensor_copy(OT[:, 256 * u:256 * u + 256].rearrange("p (b q) -> p b q", b=4), o[:, :, 0:NPATCH])
                v.tensor_copy(OTc[:, 4 * u:4 * u + 4], o[:, :, NPATCH]).then_inc(S["w1_ev"], 1)

            def repeat(n):
                dve.wait_ge(S["pc_ok"], 4 * n + 4)
                v.tensor_copy(pc_rep[:, 4 * n:4 * n + 4, :, :].rearrange("p r h d -> p (r h) d"),
                              PcA[:, 32 * n:32 * n + 32].unsqueeze(2).to_broadcast([P, 32, HD]))\
                    .then_inc(S["rep_ok"], 1)

            def class_key(n):
                b = slice(n * BLK, (n + 1) * BLK)
                dve.wait_ge(S["pcT_ps"], n + 1)
                if n:
                    dve.wait_ge(S["pc_m"], n)
                dve.wait_ge(S["w1_ev"], 2 * n + 2)
                v.tensor_tensor(tmpx[:, :].rearrange("p (b q) -> p b q", q=NPATCH),
                                bank[n][:, :].rearrange("p (b q) -> p b q", q=NPATCH),
                                vcq[:, :].unsqueeze(1).to_broadcast([P, 8, NPATCH]), ALU.mult)\
                    .then_inc(S["pcx_ok"], 1)
                dve.wait_ge(S["pcx_ok"], n + 1)
                v.tensor_tensor(OT[:, b], OT[:, b], tmpx[:, :], ALU.add).then_inc(S["pc_m"], 1)

            for p in range(PAIRS + 6):
                softmax(p if p < PAIRS else None, p - 2 if 0 <= p - 2 < PAIRS else None,
                        p + 1 if p + 1 < PAIRS else None)
                if p == PAIRS + 1:
                    dve.wait_ge(S["r_ok"], PAIRS)
                    js = PJ // 2
                    ev = SP[(PAIRS - 1) % 4][:, P * js:512].rearrange("p (j k s) -> p j k s", j=js, s=2)
                    rv = rsum[:, 8 * ((PAIRS - 1) % 2) + 2 * js:8 * ((PAIRS - 1) % 2) + 8]\
                        .rearrange("p (j s) -> p j s", j=js).unsqueeze(2).to_broadcast([P, js, NPATCH, 2])
                    v.tensor_tensor(ev, ev, rv, ALU.mult).then_inc(S["half_ok"], 1)
                if 3 <= p < PAIRS + 3:
                    probs(p - 3)
                if p < 2:
                    red(4 + 2 * p)
                    red(5 + 2 * p)
                if p == 2:
                    class_scores()
                if p == 3:
                    class_probs()
                if p == 4:
                    class_turned()
                if p >= 6 and p % 2 == 1:
                    outputs((p - 7) // 2)
                if p == PAIRS:
                    repeat(0)
                    repeat(1)
                if p == PAIRS + 1:
                    repeat(2)
                if p == PAIRS + 2:
                    repeat(3)
                    class_key(0)
                    class_key(1)
                if p == PAIRS + 3:
                    class_key(2)
                if p == PAIRS + 5:
                    class_key(3)
            dve.wait_ge(S["pc_m"], NBLK)

            ov = OT[:, :].rearrange("p (b q) -> p b q", q=NPATCH)
            for n in range(4):
                dve.wait_ge(S["w2_ps"], n + 1)
                o = ov[:, :, 16 * n:16 * n + 16]
                v.scalar_tensor_tensor(o, bank[4 + n][:, :].rearrange("p (q b) -> p b q", q=16),
                                       vecs[:, V_BV:V_BV + 1], o, op0=ALU.add, op1=ALU.add).then_inc(S["o_ok"], 1)
            dve.wait_ge(S["w2_ps"], 5)
            link(v.scalar_tensor_tensor(OTc[:, :], bank[0][:, 0:IMG], vecs[:, V_BV:V_BV + 1], OTc[:, :],
                                        op0=ALU.add, op1=ALU.add))
            v.scalar_tensor_tensor(OTc[:, :], bank[0][:, IMG:2 * IMG], clsv[:, 5:6], OTc[:, :], op0=ALU.mult,
                                   op1=ALU.add).then_inc(S["oc_ok"], 1)
            link(v.tensor_tensor(clsr[0:IMG, :], clsr[0:IMG, :], bob[0:IMG, :], ALU.add))
            link(v.memset(lg[:, PAIRS * E:NT * E], 0.0))

            def residual(n):
                if n < NBLK:
                    if n < 2:
                        dve.wait_ge(S["h0o_ok"], 1)
                        dve.wait_ge(S["op_ps"], n + 1)
                        b = slice(n * BLK, (n + 1) * BLK)
                        v.tensor_tensor(KT[:, b], bank[OP_BANKS[n]][:, :], h0[:, b], ALU.add)\
                            .then_inc(S["h1_ok"], 1)
                        dve.wait_ge(S["h1_ok"], n + 1)
                    else:
                        dve.wait_ge(S["h1a_ok"], n - 1)
                    moments(KT, n, TPB, P, "ve2_ok")
                else:
                    dve.wait_ge(S["h1c_ok"], 1)
                    moments(KT, n, 1, IMG, "ve2_ok")

            def norm2(n):
                full = n < NBLK
                normalise(KT, n, TPB if full else 1, P if full else IMG, "rstd2_ok", "xn2_ok", "x2T_ps", n - 1)

            residual(0)
            dve.wait_ge(S["opc_ps"], 1)
            v.tensor_tensor(KT[0:IMG, TOK:TOK + C], bank[4][0:IMG, 128:256], clsr[0:IMG, :], ALU.add)\
                .then_inc(S["h1c_ok"], 1)
            for n in range(1, 5):
                residual(n)
                norm2(n - 1)
            norm2(4)
            for n in (2, 3, 4):
                b = slice(n * BLK, n * BLK + (BLK if n < NBLK else IMG))
                dve.wait_ge(S["xhi_ok"], n + 1)
                dve.wait_ge(S["x2T_ok"], n + 1)
                v.tensor_tensor(x_lo[:, b], xn2T[:, b], x_hi[:, b].bitcast(F32), ALU.subtract).then_inc(S["xloD_ok"], 1)
            lv = lg[:, :].rearrange("p (t e) -> p t e", e=E)
            full = [P, NT, E]
            ra, rb, rc, rd = (rt[:, i * NT * E:(i + 1) * NT * E].rearrange("p (t e) -> p t e", e=E) for i in range(4))
            cb = comb[:, :].rearrange("p (t e) -> p t e", e=E)
            m1 = rs_[:, 0:NT]
            prio = kc[:, K_PRIO:K_PRIO + E].unsqueeze(1).to_broadcast(full)

            def over(r):
                return r.unsqueeze(2).to_broadcast(full)
            dve.wait_ge(S["lg_ps"], 5)
            lp = bank[4][:, 256:256 + NT * E].rearrange("p (t e) -> p t e", e=E)
            v.tensor_tensor(lv[:, 0:PAIRS, :], lp[:, 0:PAIRS, :],
                            brb[:, :].unsqueeze(1).to_broadcast([P, PAIRS, E]), ALU.add)
            link(v.tensor_tensor(lv[0:IMG, PAIRS, :], lp[0:IMG, PAIRS, :], brb[0:IMG, :], ALU.add))
            link(v.tensor_reduce(m1, lv, axis=AX_X, op=ALU.max))
            v.tensor_tensor(lv, lv, over(m1), ALU.subtract).then_inc(S["lg_ok"], 1)
            dve.wait_ge(S["lexp_ok"], 1)
            link(v.tensor_reduce(m1, lv, axis=AX_X, op=ALU.add))
            link(v.reciprocal(rs_[:, NT:2 * NT], m1))
            link(v.tensor_tensor(ra, lv, over(rs_[:, NT:2 * NT]), ALU.mult))
            link(v.tensor_reduce(m1, ra, axis=AX_X, op=ALU.max))
            link(v.tensor_tensor(rb, ra, over(m1), ALU.is_equal))
            link(v.tensor_tensor(rb, rb, prio, ALU.mult))
            link(v.tensor_reduce(m1, rb, axis=AX_X, op=ALU.max))
            link(v.tensor_tensor(rb, rb, over(m1), ALU.is_equal))
            link(v.scalar_tensor_tensor(rc, rb, -2.0, ra, op0=ALU.mult, op1=ALU.add))
            link(v.tensor_reduce(m1, rc, axis=AX_X, op=ALU.max))
            link(v.tensor_tensor(rc, rc, over(m1), ALU.is_equal))
            link(v.tensor_tensor(rc, rc, prio, ALU.mult))
            link(v.tensor_reduce(m1, rc, axis=AX_X, op=ALU.max))
            link(v.tensor_tensor(rc, rc, over(m1), ALU.is_equal))
            link(v.tensor_tensor(rd, rb, rc, ALU.add))
            v.tensor_tensor(cb, ra, rd, ALU.mult).then_inc(S["comb_ok"], 1)
            def base(g):
                dve.wait_ge(S["base_ps"], g + 1)
                m, w = (P, BLK) if g < NBLK else (IMG, C)
                a_ = KT[0:m, g * BLK:g * BLK + w]
                v.tensor_tensor(a_, bank[out_bank(out_base(g))][0:m, 0:w], a_, ALU.add).then_inc(S["acc_ok"], 1)

            for e in range(E):
                for g in range(5):
                    if e == 0:
                        base(g)
                    u = out_expert(e, g)
                    dve.wait_ge(S["y2_ps"], 5 * e + g + 1)
                    dve.wait_ge(S["acc_ok"], u if e == 0 else u - 4)
                    for i in range(4 if g < 4 else 1):
                        t = 4 * g + i
                        m = P if t < PAIRS else IMG
                        last = v.scalar_tensor_tensor(acc[0:m, t, :], bank[out_bank(u)][0:m, i * C:(i + 1) * C],
                                                      comb[0:m, t * E + e:t * E + e + 1], acc[0:m, t, :],
                                                      op0=ALU.mult, op1=ALU.add)
                    last.then_inc(S["acc_ok"], 1)

        @block.tensor
        def _(pe):
            t_ = nc.tensor

            def mm(o, l, r, start=True, stop=True):
                return t_.matmul(o, l, r, start=start, stop=stop)

            def patches(t):
                s, r, jh = t // 4, (t // 2) % 2, t % 2
                pe.wait_ge(S["xperm_ok"], 2 * s + r + 1)
                if t >= 2:
                    pe.wait_ge(S["xT_evA" if t % 2 == 0 else "xT_evD"], t // 2)
                for j in range(4):
                    src = (2 * s + r) * 1024 + (4 * jh + j) * P
                    last = t_.transpose(bank[t % 2][:, j * P:(j + 1) * P], xperm[:, src:src + P], ident)
                last.then_inc(S["xT_ps"], 1)

            def embed1(w, n):
                b = slice(n * BLK, (n + 1) * BLK)
                if n >= 2 and w == 0:
                    pe.wait_ge(S["gate_ok"], n - 1)
                    pe.wait_ge(S["tmin_ok"], n - 1)
                if w == 0 and n % 2 == 0:
                    pe.wait_ge(S["xT_evA"], n + 2)
                    pe.wait_ge(S["xT_evD"], n + 2)
                o = bank[4 + n % 2] if w == 0 else bank[IN_BANKS[n]]
                mm(o[:, :], WnT[:, w, 0, :], xT[:, 0, b], True, False)
                mm(o[:, :], WnT[:, w, 1, :], xT[:, 1, b], False, True)\
                    .then_inc(S["g_ps" if w == 0 else "in_ps"], 1)

            def keep_warm(times, spare=7):
                for _ in range(times):
                    mm(bank[spare][:, 0:P], ident, ident)

            pe.wait_ge(S["d_const"], 16)
            keep_warm(2)
            for t in range(2):
                patches(t)
            pe.wait_ge(S["d_rows"], 16 * 6)
            pe.wait_ge(S["d_bias"], 16 * 4)
            t_.transpose(bank[2][:, 0:NVEC], rows[0:NVEC, :], ident[0:NVEC, 0:NVEC]).then_inc(S["vec_ps"], 1)
            keep_warm(5)
            for t in range(2, 4):
                patches(t)

            def turn_weights(w):
                pe.wait_ge(S["wn_ok"], w + 1)
                for r in range(2):
                    last = t_.transpose(bank[3][:, (2 * w + r) * P:(2 * w + r + 1) * P],
                                        wn[:, w, r * P:(r + 1) * P], ident)
                last.then_inc(S["wnT_ps"], 1)

            turn_weights(0)
            keep_warm(2)
            pe.wait_ge(S["wnT_okA"], 1)
            embed1(0, 0)
            patches(4)
            patches(5)
            turn_weights(1)
            embed1(0, 1)
            patches(6)
            patches(7)
            pe.wait_ge(S["d_w3"], 16)
            pe.wait_ge(S["d_rel"], 64)
            pe.wait_ge(S["cls_n"], 1)
            o = bank[2][:, 128:128 + M_ALL]
            t_.transpose(o[:, M_W3:M_W3 + C], w3[:, :], ident)
            t_.transpose(o[:, M_WR:M_WR + E], wr[0:E, :], ident[0:E, 0:E])
            t_.transpose(o[:, M_RK:M_RK + P], rel_rows[:, 0:C], ident)
            t_.transpose(o[:, M_RK + P:M_RK + P + 1], rel_rows[0:1, C:2 * C], ident[0:1, 0:1])
            t_.transpose(o[:, M_RV:M_RV + 65], rel_rows[0:65, 2 * C:3 * C], ident[0:65, 0:65])
            t_.transpose(o[:, M_XC:M_XC + 1], clsn[0:1, :], ident[0:1, 0:1]).then_inc(S["misc_ps"], 1)
            embed1(0, 2)
            pe.wait_ge(S["wnT_ok"], 1)
            embed1(1, 0)
            embed1(0, 3)

            def embed3(n):
                pe.wait_ge(S["xi_ok"], n + 1)
                if n:
                    pe.wait_ge(S["gate_ok"], (4, 3, 4)[n - 1])
                if n == 3:
                    pe.wait_ge(S["h0_ok"], 2)
                for i in range(TPB):
                    t = n * TPB + i
                    last = mm(bank[Y_BANKS[n]][:, i * C:(i + 1) * C], xi[:, t * P:(t + 1) * P], W3T)
                last.then_inc(S["y_ps"], 1)

            def turn1(n):
                pe.wait_ge(S["xn_ok"], n + 1)
                if n == 0:
                    pe.wait_ge(S["clsv_ok"], 1)
                if n == 1:
                    pe.wait_ge(S["h0_ok"], 1)
                if n >= 2:
                    pe.wait_ge(S["xnTd_ok"], n - 1)
                for i in range(TPB):
                    last = t_.transpose(bank[2 + n % 2][:, i * P:(i + 1) * P], ST[n % 2][:, i * C:(i + 1) * C], ident)
                last.then_inc(S["xnT_ps"], 1)

            def queries_keys(n):
                b = slice(n * BLK, (n + 1) * BLK)
                pe.wait_ge(S["xnT_ok"], n + 1)
                if n:
                    pe.wait_ge(S["QT_ok"], n)
                mm(bank[6][:, :], wq, xnT[:, b]).then_inc(S["q_ps"], 1)
                if n:
                    pe.wait_ge(S["KT_ok"], n)
                mm(bank[7][:, :], wk, xnT[:, b]).then_inc(S["k_ps"], 1)

            def values_of(n):
                pe.wait_ge(S["xnTd_ok"], n + 1)
                if n == 0:
                    pe.wait_ge(S["xi_ok"], 4)
                for half in range(2):
                    if n:
                        pe.wait_ge(S["VBD_ok"], 2 * n - 1 + half)
                    for i in range(4):
                        im = 8 * n + 4 * half + i
                        last = mm(bank[half][:, i * C:(i + 1) * C],
                                  xnTd[:, im * NPATCH:(im + 1) * NPATCH, :].rearrange("p t s -> p (t s)"), wv)
                    last.then_inc(S["v_ps"], 1)

            pe.wait_ge(S["misc_ok"], 1)
            pe.wait_ge(S["d_attn"], 64)
            mm(bank[2][:, CLS:CLS + 1], wq, xcT)
            mm(bank[2][:, CLS + 1:CLS + 2], wk, xcT)
            mm(bank[2][:, CLS + 2:CLS + 3], wv, xcT).then_inc(S["cls_ps"], 1)
            embed3(0)
            embed1(1, 1)
            embed1(1, 2)
            embed3(1)
            turn1(0)
            embed1(1, 3)
            embed3(2)
            queries_keys(0)
            turn1(1)
            values_of(0)
            embed3(3)
            queries_keys(1)
            turn1(2)
            values_of(1)
            queries_keys(2)
            turn1(3)
            values_of(2)
            queries_keys(3)
            values_of(3)

            def turn_cls(g):
                n = g % 4
                src = tc_ if g < 4 else KT
                pe.wait_ge(S["tc_ok" if g < 4 else "uc_ok"], n + 1)
                if g >= 4:
                    pe.wait_ge(S["tc_red"], g - 3)
                for i in range(TPB):
                    t = n * TPB + i
                    last = t_.transpose(bank[4 + n][:, i * P:(i + 1) * P], src[:, t * P:(t + 1) * P], ident)
                last.then_inc(S["tcT_ps"], 1)

            pe.wait_ge(S["QP_ok"], 4)
            pe.wait_ge(S["QP0_ok"], 4)
            pe.wait_ge(S["xnTd_ok"], 4)
            pe.wait_ge(S["relkb_ok"], 2)
            for a in range(16):
                if a >= 4:
                    pe.wait_ge(S["a2_evA" if a % 2 == 0 else "a2_evD"], (a - 4) // 2 + 1)
                elif a >= 2:
                    pe.wait_ge(S["VBD_ok"], 8)
                for i in range(4):
                    q = 4 * a + i
                    last = mm(bank[(a + 2) % 4][:, i * P:(i + 1) * P], relk_bd[:, 2 * (64 - q):2 * (64 - q) + P],
                              QP[:, :, :, q])
                last.then_inc(S["a2_ps"], 1)
                if a == 7:
                    pe.wait_ge(S["h0_ok"], 4)
                    pe.wait_ge(S["KT_ok"], 4)
                if a >= 8 and a % 2 == 1:
                    turn_cls((a - 8) // 2)

            def scores(p):
                if p < 2:
                    pe.wait_ge(S["a2_evD" if p else "a2_evA"], 8)
                    pe.wait_ge(S["KM_ok"], 4)
                else:
                    pe.wait_ge(S["st_ok"], p - 1)
                o = bank[p % 2][:, :].rearrange("p (j b q) -> p j b q", j=PJ, b=2)
                for b2 in range(2):
                    im = 2 * p + b2
                    last = mm(o[:, :, b2, :], KM[:, im * NPATCH:(im + 1) * NPATCH, :].rearrange("p t s -> p (t s)"),
                              QP[:, :, im, :])
                last.then_inc(S["s1_ps"], 1)

            def turn_scores(p):
                pe.wait_ge(S["st_ok"], p + 1)
                if p >= 2:
                    pe.wait_ge(S["top_ok"], p - 1)
                    pe.wait_ge(S["e_ok"], p - 1)
                for j in range(PJ):
                    last = t_.transpose(bank[2 + p % 2][:, j * P:(j + 1) * P], ST[p % 2][:, j * P:(j + 1) * P], ident)
                last.then_inc(S["s_ps"], 1)

            def turn_probs(p):
                pe.wait_ge(S["pn_ok"], p + 1)
                if p == PAIRS - 1:
                    pe.wait_ge(S["half_ok"], 1)
                if p >= 2:
                    pe.wait_ge(S["pt_ok"], p - 1)
                else:
                    pe.wait_ge(S["tc_red"], 5 + p)
                for j in range(PJ):
                    last = t_.transpose(bank[4 + p % 2][:, j * P:(j + 1) * P], SP[p % 4][:, j * P:(j + 1) * P], ident)
                last.then_inc(S["pt_ps"], 1)

            def values(p):
                u = p // 2
                pe.wait_ge(S["pt_ok"], p + 1)
                if p == 0:
                    pe.wait_ge(S["ptc_ok"], 1)
                if u >= 2:
                    pe.wait_ge(S["w1_ev"], u - 1)
                for b2 in range(2):
                    im = 2 * p + b2
                    c0 = (im % 4) * QC
                    for j in range(PJ):
                        last = mm(bank[6 + u % 2][32 * j:32 * j + 32, c0:c0 + QC], VBD[:, im, 32 * j:32 * j + 32],
                                  PT[:, j, im, :])
                if p % 2 == 1:
                    last.then_inc(S["w1_ps"], 1)

            def turn_pc(n):
                pe.wait_ge(S["rep_ok"], n + 1)
                if n == 0:
                    pe.wait_ge(S["st_ok"], PAIRS)
                if n == 2:
                    pe.wait_ge(S["top_ok"], PAIRS)
                    pe.wait_ge(S["e_ok"], PAIRS)
                for i in range(TPB):
                    last = t_.transpose(bank[n][:, i * P:(i + 1) * P],
                                        pc_rep[:, n * TPB + i, :, :].rearrange("p h d -> p (h d)"), ident)
                last.then_inc(S["pcT_ps"], 1)

            scores(0)
            for p in range(PAIRS + 5):
                if p < PAIRS:
                    turn_scores(p)
                if p + 1 < PAIRS:
                    scores(p + 1)
                if p < 2:
                    turn_cls(4 + 2 * p)
                    turn_cls(5 + 2 * p)
                if p == 2:
                    pe.wait_ge(S["tc_red"], 8)
                    t_.transpose(bank[7][:, 0:P], Sct[:, :], ident)
                    mm(bank[7][:, P:P + 1], kc[:, K_E8:K_E8 + P], clsv[:, 4:5]).then_inc(S["c0_ps"], 1)
                if p == 4:
                    pe.wait_ge(S["p0d_ok"], 1)
                    for b2 in range(2):
                        last = t_.transpose(bank[6][:, b2 * P:(b2 + 1) * P], p0d[:, b2 * P:(b2 + 1) * P], ident)
                    last.then_inc(S["p0T_ps"], 1)
                if PAIRS <= p < PAIRS + 2:
                    keep_warm(5 if p == PAIRS else 3, spare=0)
                if 0 <= p - 3 < PAIRS:
                    turn_probs(p - 3)
                if p >= 5:
                    values(p - 5)
                for n in {PAIRS + 1: (0, 1), PAIRS + 2: (2,), PAIRS + 3: (3,)}.get(p, ()):
                    turn_pc(n)

            pe.wait_ge(S["pt_ok"], PAIRS)
            for n in range(4):
                if n == 2:
                    pe.wait_ge(S["w1_ev"], 8)
                for i in range(16):
                    q = 16 * n + i
                    for j in range(PJ):
                        last = mm(bank[4 + n][32 * j:32 * j + 32, i * IMG:(i + 1) * IMG],
                                  RVBD[:, 32 * (63 - q):32 * (63 - q) + 32], PT[:, j, :, q])
                last.then_inc(S["w2_ps"], 1)
            pe.wait_ge(S["pcx_ok"], 1)
            mm(bank[0][:, IMG:2 * IMG], kc[:, K_E8T:K_E8T + P], p0x[:, :])
            for j in range(PJ):
                last = mm(bank[0][32 * j:32 * j + 32, 0:IMG], RVBD[:, 32 * NPATCH:32 * NPATCH + 32], PT[:, j, :, NPATCH])
            last.then_inc(S["w2_ps"], 1)

            def residual(n):
                mm(bank[OP_BANKS[n]][:, :], ident, h0[:, n * BLK:(n + 1) * BLK], True, False)

            def project(n):
                for i in range(TPB):
                    t = n * TPB + i
                    last = mm(bank[OP_BANKS[n]][:, i * C:(i + 1) * C], OT[:, t * P:(t + 1) * P], wo, n < 2,
                              n < 2 or i == TPB - 1)
                last.then_inc(S["op_ps"], 1)

            pe.wait_ge(S["h0o_ok"], 1)
            pe.wait_ge(S["pcx_ok"], 4)
            residual(2)
            pe.wait_ge(S["o_ok"], 4)
            project(0)
            project(1)
            pe.wait_ge(S["oc_ok"], 1)
            mm(bank[4][0:IMG, 128:256], OTc[:, :], wo).then_inc(S["opc_ps"], 1)
            project(2)
            residual(3)
            project(3)

            def turn2(n):
                pe.wait_ge(S["xn2_ok"], n + 1)
                if n:
                    pe.wait_ge(S["x2T_ok"], n)
                for i in range(TPB if n < 4 else 1):
                    m = P if n < 4 else IMG
                    last = t_.transpose(bank[7][:, i * P:i * P + m], ST[n % 2][0:m, i * C:(i + 1) * C], ident[0:m, 0:m])
                last.then_inc(S["x2T_ps"], 1)

            def up(e, blk):
                for s in range(2):
                    i = 10 * e + 2 * blk + s
                    if h_before(i) > 0:
                        pe.wait_ge(S["gelu_ok"], h_before(i))
                    w = slice(e * FH + s * P, e * FH + (s + 1) * P)
                    t = slice(blk * FB, (blk + 1) * FB)
                    o = bank[h_bank(i)][:, 0:FB]
                    mm(o, w1_hi[:, w], x_hi[:, t], True, False)
                    mm(o, w1_lo[:, w], x_hi[:, t], False, False)
                    mm(o, w1_hi[:, w], x_lo[:, t], False, True).then_inc(S["h_ps"], 1)

            def router(n):
                m = BLK if n < NBLK else IMG
                pe.wait_ge(S["x2T_ok"], n + 1)
                pe.wait_ge(S["h1_ok"], 2)
                if n >= 2:
                    pe.wait_ge(S["lr_ok"], n - 1)
                mm(bank[5 + n % 2][0:E, 0:m], WrT, xn2T[:, n * BLK:n * BLK + m]).then_inc(S["lr_ps"], 1)

            def turn_logits(n):
                pe.wait_ge(S["lr_ok"], n + 1)
                if n == 0:
                    pe.wait_ge(S["h1c_ok"], 1)
                for t in range(4 * n, 4 * n + TPB if n < NBLK else NT):
                    m = P if t < PAIRS else IMG
                    last = t_.transpose(bank[4][0:m, 256 + t * E:256 + (t + 1) * E], LR[:, t * P:t * P + m],
                                        ident[0:E, 0:E])
                last.then_inc(S["lg_ps"], 1)

            keep_warm(9)
            turn2(0)
            keep_warm(6, spare=0)
            pe.wait_ge(S["w1_split"], 1)
            for n in range(1, 5):
                turn2(n)
                router(n - 1)
                if n == 4:
                    router(4)
                pe.wait_ge(S["xlo_ok" if n < 3 else "xloD_ok"], n if n < 3 else n - 2)
                up(0, n - 1)
                turn_logits(n - 1)
            turn_logits(4)
            pe.wait_ge(S["xloD_ok"], 3)
            up(0, 4)
            for blk in range(5):
                up(1, blk)

            def down(e, g):
                need = min(5, ((g + 1) * BLK + FB - 1) // FB)
                pe.wait_ge(S["gelu_ok"], 10 * e + 2 * need)
                u = out_expert(e, g)
                if u >= 4:
                    pe.wait_ge(S["acc_ok"], u - 3)
                else:
                    pe.wait_ge(S["cT_ok"], u + 2)
                for i in range(4 if g < 4 else 1):
                    t = 4 * g + i
                    m = P if t < PAIRS else IMG
                    for s in range(2):
                        last = mm(bank[out_bank(u)][0:m, i * C:(i + 1) * C], HB[:, e % 2, s, t * P:t * P + m],
                                  w2_sb[:, e, s, :], s == 0, s == 1)
                last.then_inc(S["y2_ps"], 1)

            pe.wait_ge(S["d_ffn"], 16)
            pe.wait_ge(S["gelu_ok"], 14)
            pe.wait_ge(S["comb_ok"], 1)
            pe.wait_ge(S["x2T_ok"], 5)
            pe.wait_ge(S["h1a_ok"], 2)
            for g in range(5):
                if g == 4:
                    pe.wait_ge(S["cT_ok"], 1)
                for i in range(4 if g < 4 else 1):
                    t = 4 * g + i
                    m = P if t < PAIRS else IMG
                    last = t_.transpose(bank[4 + g % 4][0:E, i * P:i * P + m], comb[0:m, t * E:(t + 1) * E],
                                        ident[0:m, 0:m])
                last.then_inc(S["cT_ps"], 1)
            pe.wait_ge(S["d_small"], 64)

            def base(g):
                u = out_base(g)
                if u >= 4:
                    pe.wait_ge(S["acc_ok"], u - 3)
                else:
                    pe.wait_ge(S["cT_ok"], u + 2)
                for i in range(4 if g < 4 else 1):
                    t = 4 * g + i
                    m = P if t < PAIRS else IMG
                    last = mm(bank[out_bank(u)][0:m, i * C:(i + 1) * C], combT[0:E, t * P:t * P + m], b2s[0:E, :])
                last.then_inc(S["base_ps"], 1)

            for e in range(E):
                for g in range(5):
                    if e == 0:
                        base(g)
                    down(e, g)
                if e + 2 < E:
                    for blk in range(5):
                        up(e + 2, blk)


_NAMES = ['x', 'cls_tok'] + ['L0_tok_' + n for n in (
    'W1_w', 'W1_b', 'W1_sw', 'W1_sb', 'W2_w', 'W2_b', 'W2_sw', 'W2_sb', 'W3_w', 'W3_b', 'eps_in1', 'eps_out1',
    'eps_in2', 'eps_out2')] + ['L0_attn_' + n for n in (
        'Wq', 'bq', 'Wk', 'bk', 'Wv', 'bv', 'Wo', 'bo', 'rel_k', 'rel_v')] + ['L0_ffn_' + n for n in (
            'Wr', 'br', 'W1', 'b1', 'W2', 'b2')]


def kernel(**inputs):
    import numpy as _np
    import concourse.bacc as _bacc
    from concourse import mybir as _mybir
    from concourse.bass_utils import run_bass_kernel_spmd as _run

    nc = _bacc.Bacc("TRN2", target_bir_lowering=False, num_devices=1)
    arrays, args = {}, []
    for name in ["consts"] + _NAMES:
        a = constants() if name == "consts" else _np.ascontiguousarray(inputs[name])
        arrays[f"in_{name}"] = a
        args.append(nc.dram_tensor(f"in_{name}", a.shape, _mybir.dt.from_np(a.dtype), kind="ExternalInput").ap())
    args.append(nc.dram_tensor("out_0", (IMG, QC, C), _mybir.dt.float32, kind="ExternalOutput").ap())
    vit_kernel(nc, *args)
    r = _run(nc, [arrays], core_ids=[0])
    return r.results[0]["out_0"]
```
